# Optimizing a Trainium2 kernel written in Bass

```python
import numpy as np
import jax
import jax.numpy as jnp

def _softmax(x, axis=-1):
    return jax.nn.softmax(x, axis=axis)

def _gelu(x):
    return jax.nn.gelu(x, approximate=True)

def _silu(x):
    return jax.nn.silu(x)

def _sigmoid(x):
    return jax.nn.sigmoid(x)

def _layernorm(x, axis=-1, eps=1e-05):
    m = jnp.mean(x, axis=axis, keepdims=True)
    v = jnp.var(x, axis=axis, keepdims=True)
    return (x - m) / jnp.sqrt(v + eps)

def _scatter_add(tgt, idx, src, axis=0):
    return tgt.at[idx].add(src)

def _segment_sum(src, seg, n):
    return jax.ops.segment_sum(src, seg, n)
kernel_name = 'mk_recurrent_d2_jaxref_r8_d0f701'

def setup_inputs(seed: int=0):
    np.random.seed(seed)
    _w = jnp.asarray

    def _L0_attn_setup():
        import jax, jax.numpy as jnp
        import numpy as np
        B, S, DIN = (2, 256, 256)
        HQ, HKV, DH = (16, 1, 128)
        key = jax.random.key(seed)
        ks = jax.random.split(key, 9)
        sc_in = 1.0 / np.sqrt(DIN)
        sc_o = 1.0 / np.sqrt(HQ * DH)
        return {'q': jax.random.normal(ks[0], (B, S, DIN), dtype=jnp.float32), 'Wq': jax.random.normal(ks[1], (DIN, HQ * DH), dtype=jnp.float32) * sc_in, 'bq': jnp.zeros((HQ * DH,), dtype=jnp.float32), 'Wk': jax.random.normal(ks[2], (DIN, HKV * DH), dtype=jnp.float32) * sc_in, 'bk': jnp.zeros((HKV * DH,), dtype=jnp.float32), 'Wv': jax.random.normal(ks[3], (DIN, HKV * DH), dtype=jnp.float32) * sc_in, 'bv': jnp.zeros((HKV * DH,), dtype=jnp.float32), 'Wo': jax.random.normal(ks[4], (HQ * DH, DIN), dtype=jnp.float32) * sc_o, 'bo': jnp.zeros((DIN,), dtype=jnp.float32)}
    _L0_attn_in = _L0_attn_setup()

    def _L0_ffn_setup():
        import jax, jax.numpy as jnp
        import numpy as np
        from jax import lax
        E = 64
        H = 256
        I = 88
        G = 8
        TOPK_GROUP = 4
        K = 8
        B, S = (2, 256)
        N = B * S
        CAP = 2 * N * K // E
        SCALE = 2.5

        def _route(x, router_weight, e_bias):
            logits = x.astype(jnp.float32) @ router_weight.astype(jnp.float32).T
            scores = jax.nn.sigmoid(logits)
            sc = scores + e_bias
            n = x.shape[0]
            group_scores = lax.top_k(sc.reshape(n, G, E // G), 2)[0].sum(-1)
            grp_idx = lax.top_k(group_scores, TOPK_GROUP)[1]
            group_mask = jnp.zeros((n, G), jnp.float32).at[jnp.arange(n)[:, None], grp_idx].set(1.0)
            score_mask = jnp.repeat(group_mask, E // G, axis=1)
            masked = jnp.where(score_mask > 0, sc, 0.0)
            topk_idx = lax.top_k(masked, K)[1]
            topk_w = jnp.take_along_axis(scores, topk_idx, axis=1)
            topk_w = topk_w / (topk_w.sum(-1, keepdims=True) + 1e-20)
            return (topk_idx, topk_w * SCALE)

        def _moe_experts(x, topk_idx, topk_w, w_gate, w_up, w_down):
            n = x.shape[0]
            flat_e = topk_idx.reshape(-1)
            rows = jnp.repeat(jnp.arange(n), K)
            oh = jax.nn.one_hot(flat_e, E, dtype=jnp.int32)
            pos = jnp.cumsum(oh, axis=0) - oh
            pos = jnp.take_along_axis(pos, flat_e[:, None], axis=1)[:, 0]
            valid = (pos < CAP).astype(x.dtype)
            p = jnp.minimum(pos, CAP - 1)
            buf = jnp.zeros((E, CAP, H), x.dtype).at[flat_e, p].add(x[rows] * valid[:, None])
            g = jnp.einsum('ech,ehi->eci', buf, w_gate)
            u = jnp.einsum('ech,ehi->eci', buf, w_up)
            y = jnp.einsum('eci,eih->ech', jax.nn.silu(g) * u, w_down)
            y_tok = y[flat_e, p] * (topk_w.reshape(-1) * valid)[:, None]
            return jnp.zeros((n, H), x.dtype).at[rows].add(y_tok)

        def _shared_mlp(x, sh_gate, sh_up, sh_down):
            return jax.nn.silu(x @ sh_gate) * (x @ sh_up) @ sh_down
        key = jax.random.key(seed)
        ks = jax.random.split(key, 9)
        f32 = jnp.float32
        return {'hidden_states': jax.random.normal(ks[0], (B, S, H), f32), 'router_weight': jax.random.normal(ks[1], (E, H), f32) * (2.0 / H) ** 0.5, 'e_bias': jnp.zeros((E,), f32), 'w_gate': jax.random.normal(ks[2], (E, H, I), f32) * (1.0 / H) ** 0.5, 'w_up': jax.random.normal(ks[3], (E, H, I), f32) * (1.0 / H) ** 0.5, 'w_down': jax.random.normal(ks[4], (E, I, H), f32) * (1.0 / I) ** 0.5, 'sh_gate': jax.random.normal(ks[5], (H, I), f32) * (1.0 / H) ** 0.5, 'sh_up': jax.random.normal(ks[6], (H, I), f32) * (1.0 / H) ** 0.5, 'sh_down': jax.random.normal(ks[7], (I, H), f32) * (1.0 / I) ** 0.5}
    _L0_ffn_in = _L0_ffn_setup()

    def _L1_attn_setup():
        import jax, jax.numpy as jnp
        import numpy as np
        HIDDEN = 256
        NUM_HEADS = 16
        NUM_KV_HEADS = 4
        HEAD_DIM = HIDDEN // NUM_HEADS
        Q_PER_KV = NUM_HEADS // NUM_KV_HEADS
        GROUP_SIZE = (Q_PER_KV + 2) * HEAD_DIM
        TOTAL_PROJ = NUM_KV_HEADS * GROUP_SIZE
        SEQ, BATCH = (256, 2)
        key = jax.random.key(seed)
        k1, k2, k3 = jax.random.split(key, 3)
        x = jax.random.normal(k1, (SEQ, BATCH, HIDDEN), dtype=jnp.float32)
        weight_qkv = jax.random.normal(k2, (TOTAL_PROJ, HIDDEN), dtype=jnp.float32) * 0.02
        weight_proj = jax.random.normal(k3, (HIDDEN, NUM_HEADS * HEAD_DIM), dtype=jnp.float32) * 0.02
        return {'x': x, 'weight_qkv': weight_qkv, 'weight_proj': weight_proj}
    _L1_attn_in = _L1_attn_setup()

    def _L1_ffn_setup():
        import jax, jax.numpy as jnp
        import numpy as np
        EPS = 1e-06
        Q_B = 128.0

        def layer_norm(x):
            mean = jnp.mean(x, axis=-1, keepdims=True)
            var = jnp.var(x, axis=-1, keepdims=True)
            return (x - mean) / jnp.sqrt(var + EPS)

        def absmax_quant(x):
            gamma = jnp.max(jnp.abs(x), axis=-1, keepdims=True)
            x_hat = jnp.clip(x * Q_B / gamma, -Q_B + EPS, Q_B - EPS)
            return x_hat * gamma / Q_B

        def ternarize_weights(w):
            gamma = jnp.mean(jnp.abs(w))
            return jnp.sign(jnp.round(w / (gamma + EPS))) * gamma

        def bitlinear(x, w):
            xn = layer_norm(x)
            x_hat = xn + jax.lax.stop_gradient(absmax_quant(xn) - xn)
            w_hat = w + jax.lax.stop_gradient(ternarize_weights(w) - w)
            return jnp.einsum('bsd,od->bso', x_hat, w_hat)
        key = jax.random.key(seed)
        k1, k2, k3 = jax.random.split(key, 3)
        B, S, D = (4, 256, 256)
        x = jax.random.normal(k1, (B, S, D), dtype=jnp.float32)
        w_fc = jax.random.normal(k2, (4 * D, D), dtype=jnp.float32) / np.sqrt(D)
        w_proj = jax.random.normal(k3, (D, 4 * D), dtype=jnp.float32) / np.sqrt(4 * D)
        return {'x': x, 'w_fc': w_fc, 'w_proj': w_proj}
    _L1_ffn_in = _L1_ffn_setup()
    _d = {'L0_attn_q': _L0_attn_in['q'], 'L0_attn_Wq': _L0_attn_in['Wq'], 'L0_attn_bq': _L0_attn_in['bq'], 'L0_attn_Wk': _L0_attn_in['Wk'], 'L0_attn_bk': _L0_attn_in['bk'], 'L0_attn_Wv': _L0_attn_in['Wv'], 'L0_attn_bv': _L0_attn_in['bv'], 'L0_attn_Wo': _L0_attn_in['Wo'], 'L0_attn_bo': _L0_attn_in['bo'], 'L0_ffn_router_weight': _L0_ffn_in['router_weight'], 'L0_ffn_e_bias': _L0_ffn_in['e_bias'], 'L0_ffn_w_gate': _L0_ffn_in['w_gate'], 'L0_ffn_w_up': _L0_ffn_in['w_up'], 'L0_ffn_w_down': _L0_ffn_in['w_down'], 'L0_ffn_sh_gate': _L0_ffn_in['sh_gate'], 'L0_ffn_sh_up': _L0_ffn_in['sh_up'], 'L0_ffn_sh_down': _L0_ffn_in['sh_down'], 'L1_attn_weight_qkv': _L1_attn_in['weight_qkv'], 'L1_attn_weight_proj': _L1_attn_in['weight_proj'], 'L1_ffn_w_fc': _L1_ffn_in['w_fc'], 'L1_ffn_w_proj': _L1_ffn_in['w_proj']}
    _x0 = _d['L0_attn_q']
    _d['L0_attn_q'] = jax.random.normal(jax.random.fold_in(jax.random.key(seed), 1), (2, 1024, 256), dtype=_x0.dtype)
    del _x0
    return _d

def reference(L0_attn_q, L0_attn_Wq, L0_attn_bq, L0_attn_Wk, L0_attn_bk, L0_attn_Wv, L0_attn_bv, L0_attn_Wo, L0_attn_bo, L0_ffn_router_weight, L0_ffn_e_bias, L0_ffn_w_gate, L0_ffn_w_up, L0_ffn_w_down, L0_ffn_sh_gate, L0_ffn_sh_up, L0_ffn_sh_down, L1_attn_weight_qkv, L1_attn_weight_proj, L1_ffn_w_fc, L1_ffn_w_proj):

    def _L0_attn_ref(q, Wq, bq, Wk, bk, Wv, bv, Wo, bo):
        import jax, jax.numpy as jnp
        import numpy as np
        B, S, DIN = (2, 256, 256)
        HQ, HKV, DH = (16, 1, 128)
        r = HQ // HKV
        lead = q.shape[:-1]
        k_lin = (q @ Wk + bk).reshape(*lead, HKV, DH)
        v_lin = (q @ Wv + bv).reshape(*lead, HKV, DH)
        qx = jnp.swapaxes(v_lin, -3, -2)
        kx = jnp.repeat(jnp.swapaxes(k_lin, -3, -2), r, axis=-3)
        vx = jnp.repeat(qx, r, axis=-3)
        scores = jnp.einsum('...jd,...id->...ji', qx, kx) / DH
        attn = jax.nn.softmax(scores, axis=-1)
        out = jnp.einsum('...jk,...kd->...jd', attn, vx)
        out = jnp.swapaxes(out, -3, -2).reshape(*lead, HQ * DH)
        return out @ Wo + bo

    def _L0_ffn_ref(hidden_states, router_weight, e_bias, w_gate, w_up, w_down, sh_gate, sh_up, sh_down):
        import jax, jax.numpy as jnp
        import numpy as np
        from jax import lax
        E = 64
        H = 256
        I = 88
        G = 8
        TOPK_GROUP = 4
        K = 8
        B, S = (2, 256)
        N = B * S
        CAP = 2 * N * K // E
        SCALE = 2.5

        def _route(x, router_weight, e_bias):
            logits = x.astype(jnp.float32) @ router_weight.astype(jnp.float32).T
            scores = jax.nn.sigmoid(logits)
            sc = scores + e_bias
            n = x.shape[0]
            group_scores = lax.top_k(sc.reshape(n, G, E // G), 2)[0].sum(-1)
            grp_idx = lax.top_k(group_scores, TOPK_GROUP)[1]
            group_mask = jnp.zeros((n, G), jnp.float32).at[jnp.arange(n)[:, None], grp_idx].set(1.0)
            score_mask = jnp.repeat(group_mask, E // G, axis=1)
            masked = jnp.where(score_mask > 0, sc, 0.0)
            topk_idx = lax.top_k(masked, K)[1]
            topk_w = jnp.take_along_axis(scores, topk_idx, axis=1)
            topk_w = topk_w / (topk_w.sum(-1, keepdims=True) + 1e-20)
            return (topk_idx, topk_w * SCALE)

        def _moe_experts(x, topk_idx, topk_w, w_gate, w_up, w_down):
            n = x.shape[0]
            flat_e = topk_idx.reshape(-1)
            rows = jnp.repeat(jnp.arange(n), K)
            oh = jax.nn.one_hot(flat_e, E, dtype=jnp.int32)
            pos = jnp.cumsum(oh, axis=0) - oh
            pos = jnp.take_along_axis(pos, flat_e[:, None], axis=1)[:, 0]
            valid = (pos < CAP).astype(x.dtype)
            p = jnp.minimum(pos, CAP - 1)
            buf = jnp.zeros((E, CAP, H), x.dtype).at[flat_e, p].add(x[rows] * valid[:, None])
            g = jnp.einsum('ech,ehi->eci', buf, w_gate)
            u = jnp.einsum('ech,ehi->eci', buf, w_up)
            y = jnp.einsum('eci,eih->ech', jax.nn.silu(g) * u, w_down)
            y_tok = y[flat_e, p] * (topk_w.reshape(-1) * valid)[:, None]
            return jnp.zeros((n, H), x.dtype).at[rows].add(y_tok)

        def _shared_mlp(x, sh_gate, sh_up, sh_down):
            return jax.nn.silu(x @ sh_gate) * (x @ sh_up) @ sh_down
        orig_shape = hidden_states.shape
        x = hidden_states.reshape(-1, H)
        topk_idx, topk_w = _route(x, router_weight, e_bias)
        moe_out = _moe_experts(x, topk_idx, topk_w.astype(x.dtype), w_gate, w_up, w_down)
        out = moe_out + _shared_mlp(x, sh_gate, sh_up, sh_down)
        return out.reshape(orig_shape)

    def _L1_attn_ref(x, weight_qkv, weight_proj):
        import jax, jax.numpy as jnp
        import numpy as np
        HIDDEN = 256
        NUM_HEADS = 16
        NUM_KV_HEADS = 4
        HEAD_DIM = HIDDEN // NUM_HEADS
        Q_PER_KV = NUM_HEADS // NUM_KV_HEADS
        GROUP_SIZE = (Q_PER_KV + 2) * HEAD_DIM
        TOTAL_PROJ = NUM_KV_HEADS * GROUP_SIZE
        SEQ, BATCH = (256, 2)
        seq, batch, hidden = x.shape
        q_size = Q_PER_KV * HEAD_DIM
        qkv = x.reshape(-1, hidden) @ weight_qkv.T
        qkv = qkv.reshape(-1, NUM_KV_HEADS, GROUP_SIZE)
        q = qkv[:, :, :q_size].reshape(seq, batch, NUM_HEADS, HEAD_DIM)
        k = qkv[:, :, q_size:q_size + HEAD_DIM].reshape(seq, batch, NUM_KV_HEADS, HEAD_DIM)
        v = qkv[:, :, q_size + HEAD_DIM:].reshape(seq, batch, NUM_KV_HEADS, HEAD_DIM)
        k = jnp.repeat(k, Q_PER_KV, axis=2)
        v = jnp.repeat(v, Q_PER_KV, axis=2)
        q = q.transpose(1, 2, 0, 3)
        k = k.transpose(1, 2, 0, 3)
        v = v.transpose(1, 2, 0, 3)
        scale = 1.0 / np.sqrt(HEAD_DIM)
        scores = jnp.einsum('bhqd,bhkd->bhqk', q, k) * scale
        causal = jnp.tril(jnp.ones((seq, seq), dtype=bool))
        scores = jnp.where(causal, scores, jnp.float32(-jnp.inf))
        probs = jax.nn.softmax(scores, axis=-1)
        attn = jnp.einsum('bhqk,bhkd->bhqd', probs, v)
        attn = attn.transpose(2, 0, 1, 3).reshape(seq * batch, NUM_HEADS * HEAD_DIM)
        out = attn @ weight_proj.T
        return out.reshape(seq, batch, hidden)

    def _L1_ffn_ref(x, w_fc, w_proj):
        import jax, jax.numpy as jnp
        import numpy as np
        EPS = 1e-06
        Q_B = 128.0

        def layer_norm(x):
            mean = jnp.mean(x, axis=-1, keepdims=True)
            var = jnp.var(x, axis=-1, keepdims=True)
            return (x - mean) / jnp.sqrt(var + EPS)

        def absmax_quant(x):
            gamma = jnp.max(jnp.abs(x), axis=-1, keepdims=True)
            x_hat = jnp.clip(x * Q_B / gamma, -Q_B + EPS, Q_B - EPS)
            return x_hat * gamma / Q_B

        def ternarize_weights(w):
            gamma = jnp.mean(jnp.abs(w))
            return jnp.sign(jnp.round(w / (gamma + EPS))) * gamma

        def bitlinear(x, w):
            xn = layer_norm(x)
            x_hat = xn + jax.lax.stop_gradient(absmax_quant(xn) - xn)
            w_hat = w + jax.lax.stop_gradient(ternarize_weights(w) - w)
            return jnp.einsum('bsd,od->bso', x_hat, w_hat)
        h = bitlinear(x, w_fc)
        h = jax.nn.gelu(h, approximate=False)
        return bitlinear(h, w_proj)
    x = L0_attn_q
    xn = _layernorm(x, axis=-1)
    s = _L0_attn_ref(xn, L0_attn_Wq, L0_attn_bq, L0_attn_Wk, L0_attn_bk, L0_attn_Wv, L0_attn_bv, L0_attn_Wo, L0_attn_bo)
    g = _silu(_L0_ffn_ref(xn, L0_ffn_router_weight, L0_ffn_e_bias, L0_ffn_w_gate, L0_ffn_w_up, L0_ffn_w_down, L0_ffn_sh_gate, L0_ffn_sh_up, L0_ffn_sh_down))
    x = x + s * g
    xn = _layernorm(x, axis=-1)
    s = _L1_attn_ref(xn, L1_attn_weight_qkv, L1_attn_weight_proj)
    g = _silu(_L1_ffn_ref(xn, L1_ffn_w_fc, L1_ffn_w_proj))
    x = x + s * g
    return x

_drawn_inputs = setup_inputs


def setup_inputs(seed=0):
    import zlib

    import numpy as np

    out = dict(_drawn_inputs(seed))
    spreads = {'L0_attn_bq': (0.0, 0.1),
     'L0_attn_bk': (0.0, 0.8),
     'L0_attn_bv': (0.0, 0.1),
     'L0_attn_bo': (0.0, 0.1),
     'L0_ffn_e_bias': (0.0, 0.292)}
    factors = {'L0_attn_Wk': 8.0, 'L0_attn_Wv': 4.295}
    for name, (base, spread) in spreads.items():
        noise = np.random.default_rng([zlib.crc32(name.encode()), seed]).standard_normal(out[name].shape)
        drawn = base * np.exp(spread * noise) if base else spread * noise
        out[name] = jnp.asarray(drawn.astype(out[name].dtype))
    for name, factor in factors.items():
        out[name] = (out[name] * factor).astype(out[name].dtype)
    return out
```

```python
from contextlib import ExitStack

import concourse.bass as bass
from concourse import mybir

F32 = mybir.dt.float32
F16 = mybir.dt.float16
I32 = mybir.dt.int32
ACT = mybir.ActivationFunctionType
ALU = mybir.AluOpType
AX = mybir.AxisListType

P = 128
BATCH, SEQ, D = 2, 1024, 256
NTOK = BATCH * SEQ
NT = NTOK // P
KH = D // P
HQ, DH = 16, 128
NE, FF, TOPK, GROUPS, TOPG = 64, 88, 8, 8, 4
PER_G = NE // GROUPS
CAP = 128
ROUTE_SCALE = 2.5
NH1, NKV1, HD1 = 16, 4, 16
REP1 = NH1 // NKV1
GS1 = (REP1 + 2) * HD1
QKV1 = NKV1 * GS1
FF1 = 4 * D
QB = 128.0
EPS_LN, EPS_Q = 1e-5, 1e-6

SA, SB = 8, 16
GE = 16
NGE = NE // GE
BIG, SENTINEL = 3.0e38, -3.0e38
SKIP = 1.0e6
XR = 4
YR = 16
WG = 2
WR = 3
YS = 3
NU = NE + NT
GT = 4
NG = NT // GT
RSQRT_SEED = 1597463007.0


def group_tiles(g):
    return [2 * g, 2 * g + 1, 2 * g + NT // 2, 2 * g + 1 + NT // 2]


WSCALE = 256.0
COMBINE = [t for g in range(NG) for t in group_tiles(g)]


def build(nc, q, Wk, bk, Wv, bv, Wo, bo, rw, eb, wg, wu, wd, sg, su, sd, wqkv, wpo, wfc, wpj, out):
    x_v = q.rearrange("b (t p) d -> p (b t) d", p=P)
    out_v = out.rearrange("b (t p) d -> p (b t) d", p=P)
    tok_d = nc.dram_tensor("tok_d", (NTOK, D + NE), F32, kind="Internal").ap()
    y_d = nc.dram_tensor("y_d", (NE * CAP, D), F32, kind="Internal").ap()
    slot_d = nc.dram_tensor("slot_d", (NE * CAP,), F32, kind="Internal").ap()
    tok_v = tok_d.rearrange("(t p) d -> p t d", p=P)

    with ExitStack() as ctx:
        def sb(name, shape, dt=F32):
            return ctx.enter_context(nc.sbuf_tensor(name, shape, dt))

        def sem(name):
            return ctx.enter_context(nc.semaphore(name))

        two = [ctx.enter_context(nc.psum_tensor(f"two{i}", [P, 1024], F32)) for i in range(4)]

        def bk_(i):
            return two[i // 2][:, (i % 2) * 512:(i % 2) * 512 + 512]

        x = sb("x", [P, NT, D])
        xn = sb("xn", [P, NT, D])
        kT = sb("kT", [P, NTOK])
        vT = sb("vT", [P, NTOK])
        v = sb("v", [P, NT, DH])
        wfcT = sb("wfcT", [P, KH, FF1], F16)
        wpjT = sb("wpjT", [P, FF1 // P, D], F16)
        wqT_hi = sb("wqT_hi", [P, KH, QKV1], F16)
        wqT_lo = sb("wqT_lo", [P, KH, QKV1], F16)
        wpoT = sb("wpoT", [P, KH, D])
        WoS = sb("WoS", [P, D])
        rwT = sb("rwT", [P, KH, NE])
        Wk_s = sb("Wk_s", [P, KH, DH])
        Wv_s = sb("Wv_s", [P, KH, DH])
        sgu = sb("sgu", [P, 2, KH, FF])
        sdn = sb("sdn", [FF, D])
        bkc = sb("bkc", [P, 1])
        bks = sb("bks", [P, 1])
        bvc = sb("bvc", [P, 1])
        bvr = sb("bvr", [1, DH])
        bo_b = sb("bo_b", [P, D])
        eb_b = sb("eb_b", [P, NE])
        ident = sb("ident", [P, P])
        ones = sb("ones", [P, P])
        ones16 = sb("ones16", [P, P], F16)
        before16 = sb("before16", [P, P], F16)
        tid_i = sb("tid_i", [P, NT], I32)
        tid = sb("tid", [P, NT])
        row_i = sb("row_i", [P, NE], I32)
        row1 = sb("row1", [P, NE])
        diag = sb("diag", [P, GE])
        st = sb("st", [P, NT, 6])
        mv = sb("mv", [P, NT, 2])
        rstd = sb("rstd", [P, NT])
        gsum = sb("gsum", [P, 2])
        gwv = sb("gwv", [P, 2])
        thr = sb("thr", [P, 2])
        nthr = sb("nthr", [P, 2])
        gsp = sb("gsp", [P, NT, 12])
        gr = sb("gr", [P, NT, 12])
        mx8 = sb("mx8", [P, NT, 8])
        rep8 = sb("rep8", [P, NT, 8])
        gmask = sb("gmask", [P, NT, GROUPS])
        den = sb("den", [P, NT])
        rden = sb("rden", [P, NT])
        key8 = sb("key8", [P, NT, TOPK])
        kmask = sb("kmask", [P, NT, TOPK])
        idxY = sb("idxY", [P, NT, TOPK], I32)
        slotR = sb("slotR", [P, NGE * SB])
        slotE = sb("slotE", [NE, CAP])
        idxE = sb("idxE", [P, NE], I32)
        nmax = sb("nmax", [P, NT])
        rsum = sb("rsum", [P, NT])
        rinv = sb("rinv", [P, NT])

        A = sb("A", [P, 8192])
        xT = A[:, 0:4096].rearrange("p (t k n) -> p t k n", t=NT, k=KH)
        Wo_s = A[:, 4096:8192].rearrange("p (h n) -> p h n", h=HQ)
        hot_b = A[:, :].bitcast(F16).rearrange("p (b t e) -> p b t e", b=SB, t=NT)
        probs = [A[:, 1024 * i:1024 * i + 1024] for i in range(2)]
        probT = [A[:, 2048 + 1024 * i:3072 + 1024 * i].rearrange("p (i j) -> p i j", i=8) for i in range(2)]
        yg = A[:, 4096:8192].rearrange("p (s d) -> p s d", s=YR)
        hid = A[:, 0:4096].rearrange("p (q f) -> p q f", q=GT)

        F = sb("F", [P, 15104])
        def f_te(i):
            return F[:, 1024 * i:1024 * i + 1024].rearrange("p (t e) -> p t e", t=NT)
        s_sig, s_sc, s_masked, s_rep, s_sel, s_w = f_te(0), f_te(1), f_te(4), f_te(5), f_te(6), f_te(7)
        t_hi1 = F[:, 2048:2560].rearrange("p (g j) -> p g j", j=4)
        t_lo1 = F[:, 2560:3072].rearrange("p (g j) -> p g j", j=4)
        t_hi2, t_m2, t_l2, t_lo2 = [F[:, 3072 + 256 * i:3328 + 256 * i].rearrange("p (g j) -> p g j", j=2)
                                    for i in range(4)]
        t_hi3, t_m3, t_l3, t_lo3 = [F[:, 4096 + 128 * i:4224 + 128 * i].rearrange("p (g j) -> p g j", j=1)
                                    for i in range(4)]
        s_pos, s_key = f_te(1), f_te(5)
        pos_i, b_i, a_i = f_te(2).bitcast(I32), f_te(3).bitcast(I32), f_te(4).bitcast(I32)
        rw_s = F[0:NE, 5120:5120 + D]
        H = F[:, 8192:10752].bitcast(F16)
        sel16 = H[:, 0:1024].rearrange("p (e t) -> p e t", t=NT)
        cum16 = H[:, 1024:2048].rearrange("p (e t) -> p e t", t=NT)
        keep16 = H[:, 2048:3072].rearrange("p (e t) -> p e t", t=NT)
        a16 = H[:, 3072:4096].rearrange("p (t e) -> p t e", t=NT)
        b16 = H[:, 4096:5120].rearrange("p (t e) -> p t e", t=NT)
        slot_m = F[:, 0:1024].rearrange("p (g e) -> p g e", e=GE)
        hot_a = F[:, 10752:14848].bitcast(F16).rearrange("p (t e a) -> p t e a", t=NT, a=SA)
        wfc_s = F[:, 10752:12800].rearrange("p (c d) -> p c d", c=FF1 // P)
        wpj_s = F[:, 12800:14848].rearrange("p (c d) -> p c d", c=KH)
        s0 = F[:, 10752:14848].rearrange("p (t d) -> p t d", t=NT)

        at = [0]

        def l1(n):
            at[0] += n
            assert at[0] <= 10752, at
            return F[:, at[0] - n:at[0]]
        hT_hi = [l1(512).bitcast(F16).rearrange("p (k n) -> p k n", k=FF1 // P) for _ in range(2)]
        hT_lo = [l1(512).bitcast(F16).rearrange("p (k n) -> p k n", k=FF1 // P) for _ in range(2)]
        xq = l1(GT * D).rearrange("p (q d) -> p q d", q=GT)
        qT_hi = l1(GT * D // 2).bitcast(F16).rearrange("p (q k n) -> p q k n", q=GT, k=KH)
        qT_lo = l1(GT * D // 2).bitcast(F16).rearrange("p (q k n) -> p q k n", q=GT, k=KH)
        s1 = l1(GT * D).rearrange("p (q d) -> p q d", q=GT)
        qkv1 = l1(2 * QKV1).rearrange("p (g c) -> p g c", c=GS1)
        kv0 = l1(2 * NKV1 * 2 * HD1).rearrange("p (g c) -> p g c", c=2 * HD1)
        pr = [l1(2 * D).rearrange("p (g r d) -> p g r d", r=REP1, d=HD1) for _ in range(2)]
        att = l1(GT * D).rearrange("p (s n) -> p s n", s=2)
        tg = l1(GT * D).rearrange("p (s i d) -> p s i d", s=2, i=2)
        sq = [vT[:, FF1 * i:FF1 * i + FF1] for i in range(2)]
        attT = kT[:, 0:GT * D].rearrange("p (u s k n) -> p u s k n", u=2, s=2, k=KH)
        tz = [kT[:, 1024 + 256 * i:1280 + 256 * i] for i in range(2)]
        zu = [kT[:, 1536 + 256 * i:1792 + 256 * i] for i in range(2)]

        W = sb("W", [P, 7232])
        wqkv_s = W[:, 0:768].rearrange("p (c d) -> p c d", c=QKV1 // P)
        wpo_s = W[:, 768:1280].rearrange("p (c d) -> p c d", c=KH)
        tern_tmp = W[:, 1280:3328]
        wgu = [W[:, 704 * r:704 * r + 704].rearrange("p (e m k f) -> p e m k f", e=WG, m=2, k=KH) for r in range(WR)]
        wdn = [W[0:FF, 2112 + 512 * r:2624 + 512 * r].rearrange("p (e n) -> p e n", e=WG) for r in range(WR)]
        xg = [W[:, 3648 + 320 * r:3968 + 320 * r] for r in range(XR)]
        xgT = [W[:, 4928 + 256 * r:5184 + 256 * r].rearrange("p (k n) -> p k n", k=KH) for r in range(2)]
        hT = [W[0:FF, 5440 + 128 * r:5568 + 128 * r] for r in range(2)]
        eth = [W[0:FF, 5696 + 128 * r:5824 + 128 * r] for r in range(2)]
        ea = [W[0:FF, 5952 + 128 * r:6080 + 128 * r] for r in range(2)]
        ysb = [W[:, 6208 + 256 * r:6464 + 256 * r] for r in range(YS)]
        oT = [W[:, 6976 + 128 * r:7104 + 128 * r] for r in range(2)]
        st1 = sb("st1", [P, GT, 6])
        mv1 = sb("mv1", [P, GT, 2])
        amax, qscale, kvscale, fcscale, hsum, nmean, ssq, hscale, zscale, zhalf, tmpc = [
            sb(n, [P, GT]) for n in ("amax", "qscale", "kvscale", "fcscale", "hsum", "nmean", "ssq", "hscale",
                                     "zscale", "zhalf", "tmpc")]
        nv, ny, nt2 = [sb(n, [P, 2 * GT]) for n in ("nv", "ny", "nt2")]
        ni = sb("ni", [P, 2 * GT], I32)
        score1, score0, dif, td, p1, p0 = [sb(n, [P, 2 * NH1]) for n in ("score1", "score0", "dif", "td", "p1", "p0")]

        ld_x = [sem(f"ld_x{c}") for c in range(4)]
        ld_w0 = sem("ld_w0")
        ld_w1 = sem("ld_w1")
        ld_wo = sem("ld_wo")
        ld_w2 = sem("ld_w2")
        ld_sh = sem("ld_sh")
        ld_e = [sem(f"ld_e{r}") for r in range(WR)]
        consts = sem("consts")
        pool_seq = sem("pool_seq")
        wos_done = sem("wos_done")
        dve = sem("dve_seq")
        act = sem("act_seq")
        ln1_var, ln1_std, xn_ready, xn_stored, w_ready, w_stored = [sem(n) for n in (
            "ln1_var", "ln1_std", "xn_ready", "xn_stored", "w_ready", "w_stored")]
        rwT_ps, rwT_ready, xT_ps, xT_ready, logits_ps, tanh_ready, bks_ready = [sem(n) for n in (
            "rwT_ps", "rwT_ready", "xT_ps", "xT_ready", "logits_ps", "tanh_ready", "bks_ready")]
        kv_ps, kv_ready, gsum_ready, gw_ps, gw_ready, tern_ready, prep_ps, prep_ready, prep_lo = [sem(n) for n in (
            "kv_ps", "kv_ready", "gsum_ready", "gw_ps", "gw_ready", "tern_ready", "prep_ps", "prep_ready", "prep_lo")]
        sel_ready, pos_ps, pos_read, hot_ready, slot_ps, slot_masked, slotR_ready, slot_out, slot_in, idx_ps, idxE_ready, idxY_ready = [
            sem(n) for n in ("sel_ready", "pos_ps", "pos_read", "hot_ready", "slot_ps", "slot_masked", "slotR_ready",
                             "slot_out", "slot_in", "idx_ps", "idxE_ready", "idxY_ready")]
        xg_ld = [sem(f"xg_ld{r}") for r in range(XR)]
        xgT_ps, xgT_ready, gu_ps, gtanh_ready, hT_ready, y_ps, y_ready = [sem(n) for n in (
            "xgT_ps", "xgT_ready", "gu_ps", "gtanh_ready", "hT_ready", "y_ps", "y_ready")]
        y_stored = [sem(f"y_stored{r}") for r in range(YS)]
        yg_clear = sem("yg_clear")
        yg_ld = [sem(f"yg_ld{r}") for r in range(YR)]
        combined = sem("combined")
        sc_ps, nmax_ready, probs_ready, pT_ps, pT_act, pT_dve, o_ps, oT_ready, wo_ps, s0_ready = [sem(n) for n in (
            "sc_ps", "nmax_ready", "probs_ready", "pT_ps", "pT_act", "pT_dve", "o_ps", "oT_ready", "wo_ps", "s0_ready")]
        acc_ready, gate_ready, xq_ready, qT_ps, qT_hi_ready, qT_lo_ready = [sem(n) for n in (
            "acc_ready", "gate_ready", "xq_ready", "qT_ps", "qT_hi_ready", "qT_lo_ready")]
        scale1_ready, qkv_ps, qkv_ready, dif_ready, td_ready, att_ready, attT_ps, attT_ready, s1_ps, s1_ready = [
            sem(n) for n in ("scale1_ready", "qkv_ps", "qkv_ready", "dif_ready", "td_ready", "att_ready", "attT_ps",
                             "attT_ready", "s1_ps", "s1_ready")]
        fc_ps, gelu_ready, nmean_ready, sq_ready, sqmax_ready, hq_ready, hT_ps, hThi_ready, hTlo_ready = [
            sem(n) for n in ("fc_ps", "gelu_ready", "nmean_ready", "sq_ready", "sqmax_ready", "hq_ready", "hT_ps",
                             "hThi_ready", "hTlo_ready")]
        scale2_ready, z_ps, ztanh_ready, out_ready, out_stored = [sem(n) for n in (
            "scale2_ready", "z_ps", "ztanh_ready", "out_ready", "out_stored")]

        def group(a, g):
            return a.rearrange("p (s i) d -> p s i d", s=2)[:, :, 2 * g:2 * g + 2, :] if a is s0 else \
                a[:, :, :].rearrange("p (s i) d -> p s i d", s=2)[:, :, 2 * g:2 * g + 2, :]

        block = ctx.enter_context(nc.Block())

        @block.sync
        def _(sp):
            for c in range(4):
                sp.dma_start(x[:, 4 * c:4 * c + 4, :], x_v[:, 4 * c:4 * c + 4, :]).then_inc(ld_x[c], 16)
            sp.dma_start(rw_s, rw).then_inc(ld_w0, 16)
            sp.dma_start(eb_b[:, :], eb.rearrange("(a n) -> a n", a=1).to_broadcast([P, NE])).then_inc(ld_w0, 16)
            for dst, src in ((Wk_s, Wk), (Wv_s, Wv)):
                sp.dma_start(dst[:, :, :], src.rearrange("(p k) n -> p k n", k=KH)).then_inc(ld_w0, 16)
            for dst, src in ((bkc, bk), (bvc, bv)):
                sp.dma_start(dst[:, :], src.rearrange("(p a) -> p a", a=1)).then_inc(ld_w0, 16)
            sp.dma_start(bvr[:, :], bv.rearrange("(a n) -> a n", a=1)).then_inc(ld_w0, 16)
            sp.dma_start(wfc_s, wfc.rearrange("(c p) d -> p c d", p=P)).then_inc(ld_w1, 16)
            sp.dma_start(wpj_s, wpj.rearrange("(c p) d -> p c d", p=P)).then_inc(ld_w1, 16)
            sp.dma_start(Wo_s, Wo.rearrange("(h p) n -> p h n", p=P)).then_inc(ld_wo, 16)
            sp.dma_start(wqkv_s, wqkv.rearrange("(c p) d -> p c d", p=P)).then_inc(ld_w2, 16)
            sp.dma_start(wpo_s, wpo.rearrange("(c p) d -> p c d", p=P)).then_inc(ld_w2, 16)
            for m, src in enumerate((sg, su)):
                sp.dma_start(sgu[:, m, :, :], src.rearrange("(p k) f -> p k f", k=KH)).then_inc(ld_sh, 16)
            sp.dma_start(sdn[:, :], sd).then_inc(ld_sh, 16)
            sp.dma_start(bo_b[:, :], bo.rearrange("(a n) -> a n", a=1).to_broadcast([P, D])).then_inc(ld_sh, 16)
            for c in range(4):
                sp.wait_ge(xn_ready, 4 * c + 4)
                sp.dma_start(tok_v[:, 4 * c:4 * c + 4, 0:D], xn[:, 4 * c:4 * c + 4, :]).then_inc(xn_stored, 16)
            sp.wait_ge(prep_ready, 11)
            sp.wait_ge(prep_lo, 2)

            def load_experts(g):
                r, e = g % WR, g * WG
                for m, src in enumerate((wg, wu)):
                    sp.dma_start(wgu[r][:, :, m, :, :].rearrange("p e k f -> p e (k f)"),
                                 src[e:e + WG].rearrange("e (p k) f -> p e (k f)", k=KH)).then_inc(ld_e[r], 16)
                sp.dma_start(wdn[r], wd[e:e + WG].rearrange("e f n -> f e n")).then_inc(ld_e[r], 16)

            for g in range(WR):
                load_experts(g)
            sp.wait_ge(w_ready, 1)
            sp.dma_start(tok_v[:, :, D:D + NE], s_w).then_inc(w_stored, 16)
            sp.wait_ge(slotR_ready, 1)
            sp.dma_start(slot_d.rearrange("(g p b) -> p g b", p=P, b=SB),
                         slotR[:, :].rearrange("p (g b) -> p g b", b=SB)).then_inc(slot_out, 16)
            sp.wait_ge(slot_out, 16)
            sp.dma_start(slotE[:, :], slot_d.rearrange("(e s) -> e s", s=CAP)).then_inc(slot_in, 16)
            for n in range(NE):
                sp.wait_ge(y_ready, n + 1)
                sp.dma_start(y_d[n * CAP:n * CAP + CAP, :], ysb[n % YS]).then_inc(y_stored[n % YS], 16)
                g = n // WG + WR
                if n % WG == WG - 1 and g < NE // WG:
                    sp.wait_ge(y_ps, n + 1)
                    load_experts(g)
            for n, t in enumerate(COMBINE):
                sp.wait_ge(out_ready, n + 1)
                sp.dma_start(out_v[:, t, :], x[:, t, :]).then_inc(out_stored, 16)
            sp.wait_ge(out_stored, 16 * NT)

        @block.gpsimd
        def _(pool):
            step = [0]

            def then(ins):
                step[0] += 1
                ins.then_inc(pool_seq, 1)
                pool.wait_ge(pool_seq, step[0])

            then(pool.memset(ident[:, :], 0.0))
            then(pool.affine_select(out=ident[:, :], in_=ident[:, :], compare_op=ALU.not_equal, fill=1.0,
                                    base=0, pattern=[[-1, P]], channel_multiplier=1))
            then(pool.memset(ones[:, :], 1.0))
            then(pool.memset(ones16[:, :], 1.0))
            then(pool.memset(before16[:, :], 0.0))
            then(pool.affine_select(out=before16[:, :], in_=before16[:, :], compare_op=ALU.is_gt, fill=-1.0,
                                    base=0, pattern=[[1, P]], channel_multiplier=-1))
            then(pool.iota(tid_i[:, :], [[P, NT]], base=0, channel_multiplier=1))
            then(pool.tensor_copy(tid[:, :], tid_i[:, :]))
            then(pool.iota(row_i[:, :], [[CAP, NE]], base=1, channel_multiplier=0))
            then(pool.tensor_copy(row1[:, :], row_i[:, :]))
            then(pool.affine_select(out=diag[:, :], in_=ones[:, 0:GE], compare_op=ALU.is_ge, fill=0.0,
                                    base=0, pattern=[[-SA, GE]], channel_multiplier=1))
            then(pool.affine_select(out=diag[:, :], in_=diag[:, :], compare_op=ALU.is_ge, fill=0.0,
                                    base=SA - 1, pattern=[[SA, GE]], channel_multiplier=-1))
            then(pool.memset(keep16, 1.0))
            then(pool.memset(keep16[:, :, 0:1], 0.0))
            then(pool.memset(rep8[:, :, :], SENTINEL))
            then(pool.memset(gsp[:, :, :], SENTINEL))
            pool.memset(gsum[:, :], 0.0).then_inc(consts, 1)
            pool.wait_ge(ld_wo, 16)
            then(pool.tensor_tensor(WoS[:, :], Wo_s[:, 0, :], Wo_s[:, 1, :], ALU.add))
            for h in range(2, HQ):
                ins = pool.tensor_tensor(WoS[:, :], WoS[:, :], Wo_s[:, h, :], ALU.add)
                if h < HQ - 1:
                    then(ins)
            ins.then_inc(wos_done, 1)
            pool.wait_ge(idxE_ready, 1)
            pool.wait_ge(xn_stored, 64)
            pool.wait_ge(w_stored, 16)
            for n in range(NE):
                if n >= XR:
                    pool.wait_ge(y_ready, n - XR + 1)
                pool.indirect_dma_start(out=xg[n % XR], out_offset=None, in_=tok_d[:, :],
                                        in_offset=bass.IndirectOffsetOnAxis(ap=idxE[:, n:n + 1], axis=0))\
                    .then_inc(xg_ld[n % XR], 16)
            pool.wait_ge(slot_ps, 1)
            pool.memset(A[:, 4096:8192], 0.0).then_inc(yg_clear, 1)
            pool.wait_ge(yg_clear, 1)
            pool.wait_ge(idxY_ready, 1)
            for r in range(YS):
                pool.wait_ge(y_stored[r], 16 * len(range(r, NE, YS)))
            for n, t in enumerate(COMBINE):
                for k in range(TOPK):
                    m = n * TOPK + k
                    if m >= YR:
                        pool.wait_ge(combined, m - YR + 1)
                    pool.indirect_dma_start(out=yg[:, m % YR, :], out_offset=None, in_=y_d[:, :],
                                            in_offset=bass.IndirectOffsetOnAxis(ap=idxY[:, t, k:k + 1], axis=0),
                                            bounds_check=NE * CAP - 1, oob_is_err=False)\
                        .then_inc(yg_ld[m % YR], 16)

        @block.scalar
        def _(sc):
            step = [0]

            def then(ins):
                step[0] += 1
                ins.then_inc(act, 1)
                sc.wait_ge(act, step[0])

            sc.wait_ge(ln1_var, 1)
            sc.activation(rstd[:, :], rstd[:, :], ACT.Sqrt).then_inc(ln1_std, 1)
            sc.wait_ge(rwT_ps, 1)
            sc.activation(rwT[:, :, :], bk_(4)[:, 0:KH * NE].rearrange("p (k e) -> p k e", k=KH), ACT.Copy).then_inc(rwT_ready, 1)
            for t in range(NT):
                sc.wait_ge(xT_ps, t + 1)
                sc.activation(xT[:, t, :, :], bk_(t % 2)[:, 0:D].rearrange("p (k n) -> p k n", k=KH), ACT.Copy)\
                    .then_inc(xT_ready, 1)
            for c in range(2):
                sc.wait_ge(logits_ps, c + 1)
                sc.activation(s_sig[:, 8 * c:8 * c + 8, :], bk_(2 + c).rearrange("p (t e) -> p t e", t=8), ACT.Tanh,
                              scale=0.5).then_inc(tanh_ready, 1)
            sc.wait_ge(ld_w1, 32)
            sc.wait_ge(consts, 1)
            for m, w in enumerate((wfc_s, wpj_s)):
                sc.activation(tern_tmp, w.rearrange("p c d -> p (c d)"), ACT.Abs,
                              accum_out=gsum[:, m:m + 1]).then_inc(gsum_ready, 1)
                sc.wait_ge(gsum_ready, m + 1)
            sc.wait_ge(gw_ps, 1)
            sc.activation(gwv[:, :], bk_(7)[:, 0:2], ACT.Copy, scale=1.0 / (FF1 * D)).then_inc(gw_ready, 1)
            sc.wait_ge(bks_ready, 1)
            for c in range(4):
                cols = slice(512 * c, 512 * c + 512)
                sc.wait_ge(kv_ps, 3 * c + 1)
                sc.activation(kT[:, cols], bk_(4), ACT.Identity, bias=bks[:, 0:1], scale=1.0 / DH).then_inc(kv_ready, 1)
                sc.wait_ge(kv_ps, 3 * c + 2)
                sc.activation(vT[:, cols], bk_(5), ACT.Identity, bias=bvc[:, 0:1], scale=1.0).then_inc(kv_ready, 1)
                sc.wait_ge(kv_ps, 3 * c + 3)
                sc.activation(v[:, 4 * c:4 * c + 4, :], bk_(6).rearrange("p (t d) -> p t d", t=4), ACT.Copy)\
                    .then_inc(kv_ready, 1)
            for j in range(11):
                sc.wait_ge(prep_ps, j + 1)
                b = bk_(4 + j % 2)
                if j < 4:
                    ins = sc.activation(wfcT[:, j // 2, 512 * (j % 2):512 * (j % 2) + 512], b, ACT.Copy)
                elif j < 8:
                    ins = sc.activation(wpjT[:, 2 * (j - 4):2 * (j - 4) + 2, :],
                                        b.rearrange("p (k n) -> p k n", k=2), ACT.Copy)
                elif j == 8:
                    ins = sc.activation(wpoT[:, :, :], b.rearrange("p (k n) -> p k n", k=KH), ACT.Copy)
                else:
                    ins = sc.activation(wqT_hi[:, j - 9, :], b[:, 0:QKV1], ACT.Copy, scale=WSCALE)
                ins.then_inc(prep_ready, 1)
            def turn(n):
                sc.wait_ge(xgT_ps, n + 1)
                if n >= 2:
                    sc.wait_ge(gu_ps, n - 1)
                sc.activation(xgT[n % 2], bk_(n % 2)[:, 0:D].rearrange("p (k n) -> p k n", k=KH), ACT.Copy)\
                    .then_inc(xgT_ready, 1)

            turn(0)
            for n in range(NU):
                if n + 1 < NU:
                    turn(n + 1)
                sc.wait_ge(gu_ps, n + 1)
                if n >= 2:
                    sc.wait_ge(hT_ready, n - 1)
                sc.activation(eth[n % 2], bk_(2 + n % 2)[0:FF, 0:CAP], ACT.Tanh, scale=0.5).then_inc(gtanh_ready, 1)

            def exps(t):
                sc.wait_ge(nmax_ready, t + 1)
                if t >= 2:
                    sc.wait_ge(pT_ps, 2 * (t - 1))
                sc.activation(probs[t % 2], two[t % 2][:, :], ACT.Exp, bias=nmax[:, t:t + 1], scale=1.0,
                              accum_out=rsum[:, t:t + 1]).then_inc(probs_ready, 1)

            def turn_out(t):
                sc.wait_ge(o_ps, t + 1)
                if t >= 2:
                    sc.wait_ge(wo_ps, t - 1)
                sc.activation(oT[t % 2], bk_(6)[:, 0:P], ACT.Copy).then_inc(oT_ready, 1)

            exps(0)
            for t in range(NT):
                sc.wait_ge(pT_ps, 2 * t + 1)
                if t >= 2:
                    sc.wait_ge(o_ps, t - 1)
                sc.activation(probT[t % 2][:, 0:4, :], bk_(4).rearrange("p (i j) -> p i j", i=4), ACT.Copy)\
                    .then_inc(pT_act, 1)
                if t + 1 < NT:
                    exps(t + 1)
                if t >= 1:
                    turn_out(t - 1)
            turn_out(NT - 1)

            def square(n):
                q_ = n % GT
                sc.wait_ge(nmean_ready, n + 1)
                if n >= 2:
                    sc.wait_ge(sqmax_ready, n - 1)
                sc.activation(sq[n % 2], hid[:, q_, :], ACT.Square, bias=nmean[:, q_:q_ + 1], scale=1.0,
                              accum_out=ssq[:, q_:q_ + 1]).then_inc(sq_ready, 1)

            def ztanh(n):
                q_ = n % GT
                sc.wait_ge(z_ps, n + 1)
                if n >= 2:
                    sc.wait_ge(out_ready, n - 1)
                sc.activation(tz[n % 2], bk_(n % 2)[:, 0:D], ACT.Tanh, scale=zhalf[:, q_:q_ + 1])\
                    .then_inc(ztanh_ready, 1)

            def gate(g):
                sc.wait_ge(acc_ready, g + 1)
                sc.activation(tg, group(xn, g), ACT.Tanh, scale=0.5).then_inc(gate_ready, 1)

            gate(0)
            for g in range(NG):
                for j in range(2):
                    sc.wait_ge(qT_ps, 2 * g + j + 1)
                    sc.activation(qT_hi[:, 2 * j:2 * j + 2, :, :], bk_(j).rearrange("p (q k n) -> p q k n", q=2, k=KH),
                                  ACT.Copy).then_inc(qT_hi_ready, 1)
                sc.wait_ge(scale1_ready, g + 1)
                for j in range(2):
                    sc.wait_ge(qkv_ps, 2 * g + j + 1)
                    sc.activation(qkv1[:, NKV1 * j:NKV1 * j + NKV1, :],
                                  bk_(6 + j)[:, 0:QKV1].rearrange("p (g c) -> p g c", g=NKV1), ACT.Copy,
                                  scale=kvscale[:, 2 + j:3 + j]).then_inc(qkv_ready, 1)
                    sc.activation(kv0[:, NKV1 * j:NKV1 * j + NKV1, :],
                                  bk_(6 + j)[:, QKV1:512].rearrange("p (g c) -> p g c", g=NKV1), ACT.Copy,
                                  scale=kvscale[:, j:j + 1]).then_inc(qkv_ready, 1)
                for q_ in range(GT):
                    n = GT * g + q_
                    sc.wait_ge(fc_ps, n + 1)
                    sc.activation(hid[:, q_, :], two[1][:, :], ACT.Gelu, scale=fcscale[:, q_:q_ + 1],
                                  accum_out=hsum[:, q_:q_ + 1]).then_inc(gelu_ready, 1)
                    if q_ == 1:
                        sc.wait_ge(dif_ready, g + 1)
                        sc.activation(td[:, :], dif[:, :], ACT.Tanh, scale=0.5 / HD1 ** 0.5).then_inc(td_ready, 1)
                    if q_ >= 1:
                        square(n - 1)
                square(GT * g + GT - 1)
                for j in range(2):
                    sc.wait_ge(attT_ps, 2 * g + j + 1)
                    sc.activation(attT[:, j, :, :, :], bk_(j).rearrange("p (s k n) -> p s k n", s=2, k=KH), ACT.Copy)\
                        .then_inc(attT_ready, 1)
                for j in range(2):
                    sc.wait_ge(s1_ps, 2 * g + j + 1)
                    sc.activation(s1[:, j:j + 3:2, :], bk_(6 + j).rearrange("p (s d) -> p s d", s=2), ACT.Copy)\
                        .then_inc(s1_ready, 1)
                sc.wait_ge(scale2_ready, g + 1)
                for q_ in range(GT):
                    n = GT * g + q_
                    if n >= 2:
                        sc.wait_ge(z_ps, n - 1)
                    for hf in range(2):
                        sc.wait_ge(hT_ps, 2 * n + hf + 1)
                        sc.activation(hT_hi[n % 2][:, 4 * hf:4 * hf + 4, :],
                                      bk_(4 + hf).rearrange("p (k n) -> p k n", k=4), ACT.Copy).then_inc(hThi_ready, 1)
                    if q_ >= 1:
                        ztanh(n - 1)
                ztanh(GT * g + GT - 1)
                if g + 1 < NG:
                    gate(g + 1)


        @block.vector
        def _(ve):
            step = [0]

            def mark(ins):
                step[0] += 1
                ins.then_inc(dve, 1)
                return step[0]

            def then(ins):
                ve.wait_ge(dve, mark(ins))

            for t in range(NT):
                ve.wait_ge(ld_x[t // 4], 16)
                last = mark(ve.bn_stats(st[:, t, :], x[:, t, :]))
            ve.wait_ge(dve, last)
            for t in range(NT):
                last = mark(ve.bn_aggr(mv[:, t, :], st[:, t, :]))
            ve.wait_ge(dve, last)
            ve.tensor_scalar(rstd[:, :], mv[:, :, 1], EPS_LN, None, ALU.add).then_inc(ln1_var, 1)
            ve.wait_ge(ln1_std, 1)
            then(ve.reciprocal(rstd[:, :], rstd[:, :]))
            for t in range(NT):
                ve.tensor_scalar(xn[:, t, :], x[:, t, :], mv[:, t, 0:1], rstd[:, t:t + 1], ALU.subtract, ALU.mult)\
                    .then_inc(xn_ready, 1)
            ve.wait_ge(ld_w0, 7 * 16)
            ve.tensor_scalar(bks[:, :], bkc[:, :], 1.0 / DH, None, ALU.mult).then_inc(bks_ready, 1)
            ve.wait_ge(gw_ready, 1)
            then(ve.tensor_scalar(thr[:, :], gwv[:, :], EPS_Q, 0.5, ALU.add, ALU.mult))
            then(ve.tensor_scalar(nthr[:, :], thr[:, :], -1.0, None, ALU.mult))
            for m, w in enumerate((wfc_s, wpj_s)):
                w = w.rearrange("p c d -> p (c d)")
                then(ve.tensor_scalar(tern_tmp, w, nthr[:, m:m + 1], None, ALU.is_lt))
                ins = ve.scalar_tensor_tensor(out=w, in0=w, scalar=thr[:, m:m + 1], in1=tern_tmp, op0=ALU.is_gt,
                                              op1=ALU.subtract)
                ins.then_inc(tern_ready, 1)
                ve.wait_ge(tern_ready, m + 1)

            def flat(a):
                return a.rearrange("p t e -> p (t e)")

            ve.wait_ge(tanh_ready, 2)
            then(ve.tensor_scalar(flat(s_sig), flat(s_sig), 0.5, 0.5, ALU.mult, ALU.add))
            then(ve.tensor_tensor(s_sc, s_sig, eb_b[:, :].unsqueeze(1).to_broadcast([P, NT, NE]), ALU.add))
            sc_g = flat(s_sc).rearrange("p (g j) -> p g j", j=PER_G)
            mark(ve.tensor_tensor(t_hi1, sc_g[:, :, 0:4], sc_g[:, :, 4:8], ALU.max))
            then(ve.tensor_tensor(t_lo1, sc_g[:, :, 0:4], sc_g[:, :, 4:8], ALU.min))
            mark(ve.tensor_tensor(t_hi2, t_hi1[:, :, 0:2], t_hi1[:, :, 2:4], ALU.max))
            mark(ve.tensor_tensor(t_m2, t_hi1[:, :, 0:2], t_hi1[:, :, 2:4], ALU.min))
            then(ve.tensor_tensor(t_l2, t_lo1[:, :, 0:2], t_lo1[:, :, 2:4], ALU.max))
            then(ve.tensor_tensor(t_lo2, t_m2, t_l2, ALU.max))
            mark(ve.tensor_tensor(t_hi3, t_hi2[:, :, 0:1], t_hi2[:, :, 1:2], ALU.max))
            mark(ve.tensor_tensor(t_m3, t_hi2[:, :, 0:1], t_hi2[:, :, 1:2], ALU.min))
            then(ve.tensor_tensor(t_l3, t_lo2[:, :, 0:1], t_lo2[:, :, 1:2], ALU.max))
            then(ve.tensor_tensor(t_lo3, t_m3, t_l3, ALU.max))
            ve.wait_ge(consts, 1)
            then(ve.tensor_tensor(gsp[:, :, 0:GROUPS], t_hi3.rearrange("p (t g) j -> p t (g j)", t=NT),
                                  t_lo3.rearrange("p (t g) j -> p t (g j)", t=NT), ALU.add))
            for t in range(NT):
                last = mark(ve.max(mx8[:, t, :], gsp[:, t, 0:GROUPS]))
            ve.wait_ge(dve, last)
            then(ve.tensor_copy(rep8[:, :, 0:TOPG], mx8[:, :, 0:TOPG]))
            for t in range(NT):
                last = mark(ve.match_replace(gr[:, t, :], rep8[:, t, :], gsp[:, t, :], BIG))
            ve.wait_ge(dve, last)
            then(ve.tensor_scalar(gmask[:, :, :], gr[:, :, 0:GROUPS], BIG / 2, None, ALU.is_ge))
            then(ve.tensor_tensor(flat(s_masked).rearrange("p (g j) -> p g j", j=PER_G), sc_g,
                                  gmask[:, :, :].rearrange("p t g -> p (t g)").unsqueeze(2)
                                  .to_broadcast([P, NT * GROUPS, PER_G]), ALU.mult))
            then(ve.tensor_scalar(flat(s_masked), flat(s_masked), 0.0, None, ALU.add))
            for t in range(NT):
                last = mark(ve.max(mx8[:, t, :], s_masked[:, t, :]))
            ve.wait_ge(dve, last)
            for t in range(NT):
                last = mark(ve.match_replace(s_rep[:, t, :], mx8[:, t, :], s_masked[:, t, :], BIG))
            ve.wait_ge(dve, last)
            then(ve.tensor_scalar(sel16, s_rep.rearrange("p t e -> p e t"), BIG / 2, None, ALU.is_ge))
            ve.tensor_tensor_scan(cum16.rearrange("p e t -> p (e t)"), keep16.rearrange("p e t -> p (e t)"),
                                  sel16.rearrange("p e t -> p (e t)"), 0.0, ALU.mult, ALU.add).then_inc(sel_ready, 1)
            mark(ve.tensor_scalar(flat(s_sel), flat(s_rep), BIG / 2, None, ALU.is_ge))
            then(ve.scalar_tensor_tensor(out=s_w, in0=s_rep, scalar=BIG / 2, in1=s_sig, op0=ALU.is_ge, op1=ALU.mult))
            then(ve.tensor_reduce(den[:, :], s_w, AX.X, ALU.add))
            then(ve.tensor_scalar(den[:, :], den[:, :], 1e-20, None, ALU.add))
            then(ve.reciprocal(rden[:, :], den[:, :]))
            then(ve.tensor_scalar(rden[:, :], rden[:, :], ROUTE_SCALE, None, ALU.mult))
            ve.tensor_tensor(s_w, s_w, rden[:, :].unsqueeze(2).to_broadcast([P, NT, NE]), ALU.mult).then_inc(w_ready, 1)
            for j in range(2):
                ve.wait_ge(prep_ready, 10 + j)
                ve.scalar_tensor_tensor(out=wqT_lo[:, j, :], in0=bk_(4 + (9 + j) % 2)[:, 0:QKV1], scalar=WSCALE,
                                        in1=wqT_hi[:, j, :], op0=ALU.mult, op1=ALU.subtract).then_inc(prep_lo, 1)
            ve.wait_ge(pos_ps, 1)
            then(ve.tensor_copy(s_pos, two[3][:, :].rearrange("p (e t) -> p t e", t=NT)))
            mark(ve.tensor_copy(flat(pos_i), flat(s_pos)))
            then(ve.scalar_tensor_tensor(out=s_sel, in0=s_pos, scalar=float(CAP), in1=s_sel, op0=ALU.is_lt,
                                         op1=ALU.mult))
            mark(ve.tensor_scalar(flat(a_i), flat(pos_i), 4, None, ALU.logical_shift_right))
            then(ve.tensor_scalar(flat(b_i), flat(pos_i), SB - 1, None, ALU.bitwise_and))
            mark(ve.scalar_tensor_tensor(out=a16, in0=s_sel, scalar=-128.0, in1=a_i, op0=ALU.mult, op1=ALU.add))
            then(ve.tensor_copy(b16, b_i))
            tid_b = tid[:, :].unsqueeze(2).to_broadcast([P, NT, NE])
            ve.wait_ge(prep_ready, 8)
            ve.wait_ge(kv_ready, 12)
            ve.wait_ge(wos_done, 1)
            for a in range(SA):
                mark(ve.scalar_tensor_tensor(out=hot_a[:, :, :, a], in0=a16, scalar=float(a - 128), in1=tid_b,
                                             op0=ALU.is_equal, op1=ALU.mult))
            for b in range(SB):
                ins = ve.tensor_scalar(flat(hot_b[:, b, :, :]), flat(b16), float(b), None, ALU.is_equal)
            ins.then_inc(hot_ready, 1)
            then(ve.tensor_tensor(s_key, s_pos, row1[:, :].unsqueeze(1).to_broadcast([P, NT, NE]), ALU.add))
            then(ve.tensor_tensor(s_key, s_key, s_sel, ALU.mult))
            for t in range(NT):
                last = mark(ve.max(key8[:, t, :], s_key[:, t, :]))
            ve.wait_ge(dve, last)
            then(ve.tensor_scalar(kmask[:, :, :], key8[:, :, :], 0.5, None, ALU.is_ge))
            then(ve.scalar_tensor_tensor(out=key8[:, :, :], in0=kmask[:, :, :], scalar=-SKIP, in1=key8[:, :, :],
                                         op0=ALU.mult, op1=ALU.add))
            ve.tensor_scalar(idxY[:, :, :], key8[:, :, :], SKIP - 1.0, None, ALU.add).then_inc(idxY_ready, 1)
            ve.wait_ge(slot_ps, 1)
            then(ve.tensor_tensor(slot_m, two[3][:, :].rearrange("p (g e) -> p g e", e=GE),
                                  diag[:, :].unsqueeze(1).to_broadcast([P, NGE * SB, GE]), ALU.mult))
            ve.tensor_reduce(slotR[:, :], slot_m, AX.X, ALU.add).then_inc(slotR_ready, 1)
            ve.wait_ge(idx_ps, 1)
            ve.tensor_copy(idxE[:, :], bk_(6)[:, 0:NE]).then_inc(idxE_ready, 1)

            def put(n):
                ve.wait_ge(y_ps, n + 1)
                y = bk_(4 + n % 2)[:, 0:D]
                if n < NE:
                    if n >= YS:
                        ve.wait_ge(y_stored[n % YS], 16 * (n // YS))
                    ve.tensor_scalar(ysb[n % YS], y, xg[n % XR][:, D + n:D + n + 1], 0.5, ALU.mult, ALU.mult)\
                        .then_inc(y_ready, 1)
                else:
                    ve.tensor_scalar(xn[:, n - NE, :], y, 0.5, None, ALU.mult).then_inc(y_ready, 1)

            ve.wait_ge(xn_stored, 64)
            for n in range(NU):
                gu = bk_(2 + n % 2)
                ve.wait_ge(gtanh_ready, n + 1)
                got = mark(ve.scalar_tensor_tensor(out=ea[n % 2], in0=eth[n % 2], scalar=1.0, in1=gu[0:FF, 0:CAP],
                                                   op0=ALU.add, op1=ALU.mult))
                if n >= 1:
                    put(n - 1)
                ve.wait_ge(dve, got)
                if n >= 2:
                    ve.wait_ge(y_ps, n - 1)
                ve.tensor_tensor(hT[n % 2], ea[n % 2], gu[0:FF, CAP:2 * CAP], ALU.mult).then_inc(hT_ready, 1)
            put(NU - 1)

            def combine(n):
                t = COMBINE[n]
                for k in range(TOPK):
                    m = n * TOPK + k
                    ve.wait_ge(yg_ld[m % YR], 16 * (m // YR + 1))
                    if m:
                        ve.wait_ge(combined, m)
                    ve.scalar_tensor_tensor(out=xn[:, t, :], in0=yg[:, m % YR, :], scalar=kmask[:, t, k:k + 1],
                                            in1=xn[:, t, :], op0=ALU.mult, op1=ALU.add).then_inc(combined, 1)

            def top(t):
                ve.wait_ge(sc_ps, t + 1)
                ve.tensor_reduce(nmax[:, t:t + 1], two[t % 2][:, :], AX.X, ALU.max, negate=True).then_inc(nmax_ready, 1)

            def project(t):
                ve.wait_ge(wo_ps, t + 1)
                ve.scalar_tensor_tensor(out=s0[:, t, :], in0=bk_(7)[:, 0:D], scalar=rinv[:, t:t + 1], in1=bo_b[:, :],
                                        op0=ALU.mult, op1=ALU.add).then_inc(s0_ready, 1)

            combined_n = 0
            ve.wait_ge(y_ready, NU)
            top(0)
            for t in range(NT):
                if t + 1 < NT:
                    top(t + 1)
                ve.wait_ge(pT_ps, 2 * t + 2)
                if t >= 2:
                    ve.wait_ge(o_ps, t - 1)
                ve.tensor_copy(probT[t % 2][:, 4:8, :], bk_(5).rearrange("p (i j) -> p i j", i=4)).then_inc(pT_dve, 1)
                then(ve.reciprocal(rinv[:, t:t + 1], rsum[:, t:t + 1]))
                if t >= 2:
                    project(t - 2)
                if t >= 3 and t % 2:
                    combine(combined_n)
                    combined_n += 1
            project(NT - 2)
            project(NT - 1)

            def rsqrt(v, y, t_, i_):
                then(ve.tensor_scalar(i_, v.bitcast(I32), 1, None, ALU.logical_shift_right))
                then(ve.tensor_scalar(y.bitcast(I32), i_, -1.0, RSQRT_SEED, ALU.mult, ALU.add))
                for _ in range(3):
                    then(ve.tensor_tensor(t_, y, y, ALU.mult))
                    then(ve.tensor_tensor(t_, t_, v, ALU.mult))
                    then(ve.tensor_scalar(t_, t_, -0.5, 1.5, ALU.mult, ALU.add))
                    then(ve.tensor_tensor(y, y, t_, ALU.mult))

            def enter(g):
                nonlocal combined_n
                while combined_n < GT * (g + 1):
                    combine(combined_n)
                    combined_n += 1
                ve.wait_ge(combined, TOPK * combined_n)
                ve.nop().then_inc(acc_ready, 1)
                ve.wait_ge(gate_ready, g + 1)
                then(ve.scalar_tensor_tensor(out=tg, in0=tg, scalar=1.0, in1=group(xn, g), op0=ALU.add, op1=ALU.mult))
                ve.wait_ge(s0_ready, NT)
                then(ve.scalar_tensor_tensor(out=tg, in0=tg, scalar=0.5, in1=group(s0, g), op0=ALU.mult, op1=ALU.mult))
                then(ve.tensor_tensor(group(x, g), group(x, g), tg, ALU.add))
                for q_, t in enumerate(group_tiles(g)):
                    last = mark(ve.bn_stats(st1[:, q_, :], x[:, t, :]))
                ve.wait_ge(dve, last)
                for q_ in range(GT):
                    last = mark(ve.bn_aggr(mv1[:, q_, :], st1[:, q_, :]))
                ve.wait_ge(dve, last)
                for q_, t in enumerate(group_tiles(g)):
                    last = mark(ve.tensor_scalar(xq[:, q_, :], x[:, t, :], mv1[:, q_, 0:1], None, ALU.subtract))
                ve.wait_ge(dve, last)
                then(ve.tensor_reduce(amax[:, :], xq, AX.X, ALU.max, apply_absolute_value=True))
                then(ve.reciprocal(qscale[:, :], amax[:, :]))
                then(ve.tensor_scalar(qscale[:, :], qscale[:, :], QB, None, ALU.mult))
                for q_ in range(GT):
                    last = mark(ve.tensor_scalar(xq[:, q_, :], xq[:, q_, :], qscale[:, q_:q_ + 1], QB, ALU.mult, ALU.min))
                ve.wait_ge(dve, last)
                ve.tensor_scalar(xq, xq, -QB, None, ALU.max).then_inc(xq_ready, 1)
                var = mv1[:, :, 1]
                mark(ve.tensor_scalar(nv[:, 0:GT], var, EPS_LN, None, ALU.add))
                then(ve.tensor_scalar(nv[:, GT:], var, 1.0 + EPS_Q, EPS_Q * EPS_LN, ALU.mult, ALU.add))
                rsqrt(nv[:, :], ny[:, :], nt2[:, :], ni[:, :])
                then(ve.tensor_scalar(tmpc[:, :], amax[:, :], 1.0 / QB, None, ALU.mult))
                if g:
                    ve.wait_ge(qkv_ready, 4 * g)
                    ve.wait_ge(gelu_ready, GT * g)
                then(ve.tensor_tensor(fcscale[:, :], tmpc[:, :], ny[:, 0:GT], ALU.mult))
                mark(ve.tensor_scalar(kvscale[:, :], fcscale[:, :], 1.0 / WSCALE, None, ALU.mult))
                then(ve.tensor_tensor(nt2[:, 0:GT], nv[:, 0:GT], ny[:, 0:GT], ALU.mult))
                then(ve.tensor_tensor(nt2[:, 0:GT], nt2[:, 0:GT], ny[:, GT:], ALU.mult))
                then(ve.tensor_tensor(fcscale[:, :], fcscale[:, :], nt2[:, 0:GT], ALU.mult))
                ve.tensor_scalar(fcscale[:, :], fcscale[:, :], gwv[:, 0:1], None, ALU.mult).then_inc(scale1_ready, 1)

            enter(0)
            for g in range(NG):
                for j in range(2):
                    ve.wait_ge(qT_hi_ready, 2 * g + j + 1)
                    ve.tensor_tensor(qT_lo[:, 2 * j:2 * j + 2, :, :], bk_(j).rearrange("p (q k n) -> p q k n", q=2, k=KH),
                                     qT_hi[:, 2 * j:2 * j + 2, :, :], ALU.subtract).then_inc(qT_lo_ready, 1)
                ve.wait_ge(qkv_ready, 4 * g + 4)
                qh = qkv1[:, :, 0:REP1 * HD1].rearrange("p g (r d) -> p g r d", r=REP1)

                def heads(a):
                    return a.unsqueeze(2).to_broadcast([P, 2 * NKV1, REP1, HD1])

                def per_head(a):
                    return a.rearrange("p (g r) -> p g r", r=REP1).unsqueeze(3).to_broadcast([P, 2 * NKV1, REP1, HD1])

                k1, v1 = qkv1[:, :, 64:80], qkv1[:, :, 80:96]
                k0, v0 = kv0[:, :, 0:16], kv0[:, :, 16:32]
                mark(ve.tensor_tensor(pr[0], qh, heads(k1), ALU.mult))
                then(ve.tensor_tensor(pr[1], qh, heads(k0), ALU.mult))
                mark(ve.tensor_reduce(score1[:, :].rearrange("p (g r) -> p g r", r=REP1), pr[0], AX.X, ALU.add))
                then(ve.tensor_reduce(score0[:, :].rearrange("p (g r) -> p g r", r=REP1), pr[1], AX.X, ALU.add))
                ve.tensor_tensor(dif[:, :], score1[:, :], score0[:, :], ALU.subtract).then_inc(dif_ready, 1)
                att_h = [att[:, s_, :].rearrange("p (g r d) -> p g r d", r=REP1, d=HD1) for s_ in range(2)]
                if g:
                    ve.wait_ge(attT_ps, 2 * g)
                mark(ve.tensor_copy(att_h[0], heads(v0)))
                ve.wait_ge(td_ready, g + 1)
                mark(ve.tensor_scalar(p1[:, :], td[:, :], 0.5, 0.5, ALU.mult, ALU.add))
                then(ve.tensor_scalar(p0[:, :], td[:, :], -0.5, 0.5, ALU.mult, ALU.add))
                mark(ve.tensor_tensor(pr[0], heads(v1), per_head(p1[:, :]), ALU.mult))
                then(ve.tensor_tensor(pr[1], heads(v0), per_head(p0[:, :]), ALU.mult))
                ve.tensor_tensor(att_h[1], pr[0], pr[1], ALU.add).then_inc(att_ready, 1)
                for q_ in range(GT):
                    n = GT * g + q_
                    ve.wait_ge(gelu_ready, n + 1)
                    ve.tensor_scalar(nmean[:, q_:q_ + 1], hsum[:, q_:q_ + 1], -1.0 / FF1, None, ALU.mult)\
                        .then_inc(nmean_ready, 1)
                    if q_ >= 1:
                        ve.wait_ge(sq_ready, n)
                        ve.tensor_reduce(nv[:, GT + q_ - 1:GT + q_], sq[(n - 1) % 2], AX.X, ALU.max).then_inc(sqmax_ready, 1)
                n = GT * g + GT - 1
                ve.wait_ge(sq_ready, n + 1)
                ve.tensor_reduce(nv[:, 2 * GT - 1:], sq[n % 2], AX.X, ALU.max).then_inc(sqmax_ready, 1)
                ve.wait_ge(sqmax_ready, n + 1)
                then(ve.tensor_scalar(nv[:, 0:GT], ssq[:, :], 1.0 / FF1, EPS_Q, ALU.mult, ALU.add))
                rsqrt(nv[:, :], ny[:, :], nt2[:, :], ni[:, :])
                then(ve.tensor_scalar(hscale[:, :], ny[:, GT:], QB, None, ALU.mult))
                for q_ in range(GT):
                    then(ve.tensor_scalar(hid[:, q_, :], hid[:, q_, :], nmean[:, q_:q_ + 1], hscale[:, q_:q_ + 1],
                                          ALU.add, ALU.mult))
                    ve.tensor_scalar(hid[:, q_, :], hid[:, q_, :], QB, -QB, ALU.min, ALU.max).then_inc(hq_ready, 1)
                then(ve.tensor_tensor(tmpc[:, :], nv[:, GT:], ny[:, GT:], ALU.mult))
                then(ve.tensor_tensor(tmpc[:, :], tmpc[:, :], ny[:, 0:GT], ALU.mult))
                then(ve.tensor_scalar(zhalf[:, :], tmpc[:, :], gwv[:, 1:2], 0.5 / QB, ALU.mult, ALU.mult))
                ve.nop().then_inc(scale2_ready, 1)

                def finish(n):
                    q_ = n % GT
                    t = group_tiles(n // GT)[q_]
                    ve.wait_ge(ztanh_ready, n + 1)
                    then(ve.scalar_tensor_tensor(out=zu[n % 2], in0=tz[n % 2], scalar=1.0, in1=bk_(n % 2)[:, 0:D],
                                                 op0=ALU.add, op1=ALU.mult))
                    ve.wait_ge(s1_ready, 2 * (n // GT) + 2)
                    then(ve.scalar_tensor_tensor(out=zu[n % 2], in0=zu[n % 2], scalar=zhalf[:, q_:q_ + 1],
                                                 in1=s1[:, q_, :], op0=ALU.mult, op1=ALU.mult))
                    ve.tensor_tensor(x[:, t, :], x[:, t, :], zu[n % 2], ALU.add).then_inc(out_ready, 1)

                for q_ in range(GT):
                    n = GT * g + q_
                    for hf in range(2):
                        ve.wait_ge(hThi_ready, 2 * n + hf + 1)
                        ve.tensor_tensor(hT_lo[n % 2][:, 4 * hf:4 * hf + 4, :],
                                         bk_(4 + hf).rearrange("p (k n) -> p k n", k=4),
                                         hT_hi[n % 2][:, 4 * hf:4 * hf + 4, :], ALU.subtract).then_inc(hTlo_ready, 1)
                    if q_ >= 1:
                        finish(n - 1)
                finish(GT * g + GT - 1)
                if g + 1 < NG:
                    enter(g + 1)

        @block.tensor
        def _(pe):
            pe.wait_ge(consts, 1)
            pe.wait_ge(ld_w0, 7 * 16)
            for k in range(KH):
                ins = pe.transpose(bk_(4)[:, NE * k:NE * k + NE], rw_s.rearrange("e (n k) -> e k n", k=KH)[:, k, :],
                                   ident[0:NE, 0:NE])
            ins.then_inc(rwT_ps, 1)

            def logits(t):
                pe.wait_ge(xT_ready, t + 1)
                for k in range(KH):
                    ins = pe.matmul(bk_(2 + t // 8)[:, NE * (t % 8):NE * (t % 8) + NE], xT[:, t, k, :], rwT[:, k, :],
                                    start=(k == 0), stop=(k == KH - 1))
                if t % 8 == 7:
                    ins.then_inc(logits_ps, 1)

            for t in range(NT):
                pe.wait_ge(xn_ready, t + 1)
                if t >= 2:
                    pe.wait_ge(xT_ready, t - 1)
                for k in range(KH):
                    ins = pe.transpose(bk_(t % 2)[:, P * k:P * k + P],
                                       xn[:, t, :].rearrange("p (n k) -> p k n", k=KH)[:, k, :], ident[:, :])
                ins.then_inc(xT_ps, 1)
                if t == 0:
                    pe.wait_ge(rwT_ready, 1)
                if t >= 1:
                    logits(t - 1)
            logits(NT - 1)
            pe.wait_ge(gsum_ready, 2)
            pe.matmul(bk_(7)[:, 0:2], ones[:, :], gsum[:, :], start=True, stop=True).then_inc(gw_ps, 1)
            for c in range(4):
                if c:
                    pe.wait_ge(kv_ready, 3 * c)
                for b, w in ((4, Wk_s), (5, Wv_s)):
                    for k in range(KH):
                        ins = pe.matmul(bk_(b), w[:, k, :], xT[:, 4 * c:4 * c + 4, k, :], start=(k == 0),
                                        stop=(k == KH - 1))
                    ins.then_inc(kv_ps, 1)
                for t in range(4):
                    for k in range(KH):
                        pe.matmul(bk_(6)[:, DH * t:DH * t + DH], xT[:, 4 * c + t, k, :], Wv_s[:, k, :], start=(k == 0),
                                  stop=False)
                    ins = pe.matmul(bk_(6)[:, DH * t:DH * t + DH], ones[0:1, :], bvr[0:1, :], start=False, stop=True)
                ins.then_inc(kv_ps, 1)
            pe.wait_ge(kv_ready, 12)
            for j in range(11):
                if j >= 2:
                    pe.wait_ge(prep_ready, j - 1)
                if j < 4:
                    pe.wait_ge(tern_ready, 1)
                    k, c0 = j // 2, 4 * (j % 2)
                    parts = [wfc_s[:, c0 + c, P * k:P * k + P] for c in range(4)]
                elif j < 8:
                    pe.wait_ge(tern_ready, 2)
                    parts = [wpj_s[:, c, P * k:P * k + P] for k in (2 * (j - 4), 2 * (j - 4) + 1) for c in range(2)]
                elif j == 8:
                    pe.wait_ge(ld_w2, 32)
                    parts = [wpo_s[:, c, P * k:P * k + P] for k in range(2) for c in range(2)]
                else:
                    parts = [wqkv_s[:, c, P * (j - 9):P * (j - 9) + P] for c in range(3)]
                for i, part in enumerate(parts):
                    ins = pe.transpose(bk_(4 + j % 2)[:, P * i:P * i + P], part, ident[:, :])
                ins.then_inc(prep_ps, 1)
            pe.wait_ge(sel_ready, 1)
            for h in range(2):
                es = slice(32 * h, 32 * h + 32)
                pe.matmul(bk_(6 + h), before16[:, :], sel16[:, es, :].rearrange("p e t -> p (e t)"), start=True, stop=False)
                ins = pe.matmul(bk_(6 + h), ones16[:, :], cum16[:, es, :].rearrange("p e t -> p (e t)"), start=False,
                                stop=True)
            ins.then_inc(pos_ps, 1)
            pe.wait_ge(hot_ready, 1)
            for g in range(NGE):
                es = slice(GE * g, GE * g + GE)
                for t in range(NT):
                    ins = pe.matmul(two[3][:, 256 * g:256 * g + 256],
                                    hot_a[:, t, es, :].rearrange("p e a -> p (e a)"), hot_b[:, :, t, es],
                                    start=(t == 0), stop=(t == NT - 1))
            ins.then_inc(slot_ps, 1)
            pe.wait_ge(slot_in, 16)
            pe.wait_ge(slotR_ready, 1)
            pe.transpose(bk_(6)[:, 0:NE], slotE[:, :], ident[0:NE, 0:NE]).then_inc(idx_ps, 1)

            pe.wait_ge(prep_lo, 2)
            pe.wait_ge(ld_sh, 4 * 16)

            def turn(n):
                if n < NE:
                    pe.wait_ge(xg_ld[n % XR], 16 * (n // XR + 1))
                    src = xg[n % XR][:, 0:D]
                else:
                    src = xn[:, n - NE, :]
                if n >= 2:
                    pe.wait_ge(xgT_ready, n - 1)
                for k in range(KH):
                    ins = pe.transpose(bk_(n % 2)[:, P * k:P * k + P],
                                       src.rearrange("p (n k) -> p k n", k=KH)[:, k, :], ident[:, :])
                ins.then_inc(xgT_ps, 1)

            def up(n):
                pe.wait_ge(xgT_ready, n + 1)
                if n < NE:
                    r = (n // WG) % WR
                    pe.wait_ge(ld_e[r], 48 * (n // WG // WR + 1))
                if n >= 2:
                    pe.wait_ge(hT_ready, n - 1)
                for m in range(2):
                    for k in range(KH):
                        w = wgu[r][:, n % WG, m, k, :] if n < NE else sgu[:, m, k, :]
                        ins = pe.matmul(bk_(2 + n % 2)[0:FF, CAP * m:CAP * m + CAP], w, xgT[n % 2][:, k, :],
                                        start=(k == 0), stop=(k == KH - 1))
                ins.then_inc(gu_ps, 1)

            def down(n):
                pe.wait_ge(hT_ready, n + 1)
                if n >= 2:
                    pe.wait_ge(y_ready, n - 1)
                w = wdn[(n // WG) % WR][:, n % WG, :] if n < NE else sdn[:, :]
                pe.matmul(bk_(4 + n % 2)[:, 0:D], hT[n % 2], w, start=True, stop=True).then_inc(y_ps, 1)

            turn(0)
            for n in range(NU):
                if n + 1 < NU:
                    turn(n + 1)
                up(n)
                if n >= 1:
                    down(n - 1)
            down(NU - 1)

            def score(t):
                if t >= 2:
                    pe.wait_ge(probs_ready, t - 1)
                for h in range(2):
                    at = (t // 8) * SEQ + 512 * h
                    ins = pe.matmul(two[t % 2][:, 512 * h:512 * h + 512], vT[:, P * t:P * t + P], kT[:, at:at + 512],
                                    start=True, stop=True)
                ins.then_inc(sc_ps, 1)

            def attend(t):
                pe.wait_ge(pT_act, t + 1)
                pe.wait_ge(pT_dve, t + 1)
                if t >= 1:
                    pe.wait_ge(oT_ready, t)
                for i in range(8):
                    ins = pe.matmul(bk_(6)[:, 0:P], v[:, (t // 8) * 8 + i, :], probT[t % 2][:, i, :], start=(i == 0),
                                    stop=(i == 7))
                ins.then_inc(o_ps, 1)

            def out_project(t):
                pe.wait_ge(oT_ready, t + 1)
                if t >= 1:
                    pe.wait_ge(s0_ready, t)
                pe.matmul(bk_(7)[:, 0:D], oT[t % 2], WoS[:, :], start=True, stop=True).then_inc(wo_ps, 1)

            pe.wait_ge(y_ready, NU)
            pe.wait_ge(wos_done, 1)
            score(0)
            for t in range(NT):
                if t + 1 < NT:
                    score(t + 1)
                pe.wait_ge(probs_ready, t + 1)
                if t >= 1:
                    pe.wait_ge(pT_act, t)
                    pe.wait_ge(pT_dve, t)
                for h in range(2):
                    for i in range(4):
                        ins = pe.transpose(bk_(4 + h)[:, P * i:P * i + P],
                                           probs[t % 2][:, 512 * h + P * i:512 * h + P * i + P], ident[:, :])
                    ins.then_inc(pT_ps, 1)
                if t >= 1:
                    attend(t - 1)
                if t >= 2:
                    out_project(t - 2)
            attend(NT - 1)
            out_project(NT - 2)
            out_project(NT - 1)

            def fc(n):
                q_ = n % GT
                if n >= 1:
                    pe.wait_ge(gelu_ready, n)
                for h in range(2):
                    for i, (k, part) in enumerate((k, part) for k in range(KH) for part in (qT_hi, qT_lo)):
                        ins = pe.matmul(bk_(2 + h), part[:, q_, k, :], wfcT[:, k, 512 * h:512 * h + 512], start=(i == 0),
                                        stop=(i == 3))
                ins.then_inc(fc_ps, 1)

            def turn_hidden(n):
                q_ = n % GT
                pe.wait_ge(hq_ready, n + 1)
                if n >= 1:
                    pe.wait_ge(hTlo_ready, 2 * n)
                for h in range(2):
                    for i in range(4):
                        k = 4 * h + i
                        ins = pe.transpose(bk_(4 + h)[:, P * i:P * i + P], hid[:, q_, P * k:P * k + P], ident[:, :])
                    ins.then_inc(hT_ps, 1)

            def down1(n):
                pe.wait_ge(hTlo_ready, 2 * n + 2)
                if n >= 2:
                    pe.wait_ge(out_ready, n - 1)
                i = 0
                for k in range(FF1 // P):
                    for part in (hT_hi, hT_lo):
                        ins = pe.matmul(bk_(n % 2)[:, 0:D], part[n % 2][:, k, :], wpjT[:, k, :], start=(i == 0),
                                        stop=(i == 2 * FF1 // P - 1))
                        i += 1
                ins.then_inc(z_ps, 1)

            pe.wait_ge(s0_ready, NT)
            for g in range(NG):
                pe.wait_ge(xq_ready, g + 1)
                if g:
                    pe.wait_ge(out_ready, GT * g)
                for j in range(2):
                    for i in range(2):
                        for k in range(KH):
                            ins = pe.transpose(bk_(j)[:, D * i + P * k:D * i + P * k + P],
                                               xq[:, 2 * j + i, P * k:P * k + P], ident[:, :])
                    ins.then_inc(qT_ps, 1)
                pe.wait_ge(qT_lo_ready, 2 * g + 2)
                if g:
                    pe.wait_ge(s1_ready, 2 * g)
                for j in range(2):
                    for q_, cols, width in ((2 + j, slice(0, QKV1), GS1), (j, slice(QKV1, 512), 2 * HD1)):
                        i = 0
                        for k in range(KH):
                            for part, w in ((qT_hi, wqT_hi), (qT_lo, wqT_hi), (qT_hi, wqT_lo)):
                                rhs = w[:, k, :].rearrange("p (g c) -> p g c", c=GS1)[:, :, GS1 - width:GS1]
                                ins = pe.matmul(bk_(6 + j)[:, cols], part[:, q_, k, :], rhs, start=(i == 0), stop=(i == 5))
                                i += 1
                    ins.then_inc(qkv_ps, 1)
                for q_ in range(GT):
                    fc(GT * g + q_)
                pe.wait_ge(att_ready, g + 1)
                for j in range(2):
                    for s_ in range(2):
                        for k in range(KH):
                            ins = pe.transpose(bk_(j)[:, D * s_ + P * k:D * s_ + P * k + P],
                                               att[:, s_, D * j + P * k:D * j + P * k + P], ident[:, :])
                    ins.then_inc(attT_ps, 1)
                for j in range(2):
                    pe.wait_ge(attT_ready, 2 * g + j + 1)
                    pe.wait_ge(qkv_ready, 4 * g + 4)
                    for s_ in range(2):
                        for k in range(KH):
                            ins = pe.matmul(bk_(6 + j)[:, D * s_:D * s_ + D], attT[:, j, s_, k, :], wpoT[:, k, :],
                                            start=(k == 0), stop=(k == KH - 1))
                    ins.then_inc(s1_ps, 1)
                for q_ in range(GT):
                    turn_hidden(GT * g + q_)
                    if q_ >= 1:
                        down1(GT * g + q_ - 1)
                down1(GT * g + GT - 1)


_INS = ["L0_attn_q", "L0_attn_Wk", "L0_attn_bk", "L0_attn_Wv", "L0_attn_bv", "L0_attn_Wo", "L0_attn_bo",
        "L0_ffn_router_weight", "L0_ffn_e_bias", "L0_ffn_w_gate", "L0_ffn_w_up", "L0_ffn_w_down", "L0_ffn_sh_gate",
        "L0_ffn_sh_up", "L0_ffn_sh_down", "L1_attn_weight_qkv", "L1_attn_weight_proj", "L1_ffn_w_fc", "L1_ffn_w_proj"]


def kernel(**inputs):
    import numpy as _np
    import concourse.bacc as _bacc
    from concourse import mybir as _mybir
    from concourse.bass_utils import run_bass_kernel_spmd as _run

    nc = _bacc.Bacc("TRN2", target_bir_lowering=False, num_devices=1)
    arrays, args = {}, []
    for name in _INS:
        a = _np.ascontiguousarray(inputs[name])
        arrays[f"in_{name}"] = a
        args.append(nc.dram_tensor(f"in_{name}", a.shape, _mybir.dt.from_np(a.dtype), kind="ExternalInput").ap())
    out = nc.dram_tensor("out_0", (BATCH, SEQ, D), F32, kind="ExternalOutput").ap()
    build(nc, *args, out)
    r = _run(nc, [arrays], core_ids=[0])
    return r.results[0]["out_0"]
```

```python
from contextlib import ExitStack

import concourse.bass as bass
from concourse import mybir

F32 = mybir.dt.float32
F16 = mybir.dt.float16
I32 = mybir.dt.int32
ACT = mybir.ActivationFunctionType
ALU = mybir.AluOpType
AX = mybir.AxisListType

P = 128
BATCH, SEQ, D = 2, 1024, 256
NTOK = BATCH * SEQ
NT = NTOK // P
KH = D // P
HQ, DH = 16, 128
NE, FF, TOPK, GROUPS, TOPG = 64, 88, 8, 8, 4
PER_G = NE // GROUPS
CAP = 128
ROUTE_SCALE = 2.5
NH1, NKV1, HD1 = 16, 4, 16
REP1 = NH1 // NKV1
GS1 = (REP1 + 2) * HD1
QKV1 = NKV1 * GS1
FF1 = 4 * D
QB = 128.0
EPS_LN, EPS_Q = 1e-5, 1e-6

SA, SB = 8, 16
GE = 16
NGE = NE // GE
BIG, SENTINEL = 3.0e38, -3.0e38
SKIP = 1.0e6
XR = 7
WG = 2
WR = 3
YS = 4
EARLY = 4
STEPS = 5
SC = 4
NP = NT // 2
GT = 2
NEWTON, ROW_STEPS = 11, 8
RSQRT_SEED = 1597463007.0


WSCALE = 256.0


def build(nc, q, Wk, bk, Wv, bv, Wo, bo, rw, eb, wg, wu, wd, sg, su, sd, wqkv, wpo, wfc, wpj, out):
    x_v = q.rearrange("b (t p) d -> p (b t) d", p=P)
    out_v = out.rearrange("b (t p) d -> p (b t) d", p=P)
    tok_d = nc.dram_tensor("tok_d", (NTOK + P, D + NE), F32, kind="Internal").ap()
    acc_d = [nc.dram_tensor(f"acc_d{i}", (NTOK + P, D), F32, kind="Internal").ap() for i in range(2)]
    slot_d = nc.dram_tensor("slot_d", (NE * CAP,), F32, kind="Internal").ap()
    tok_v = tok_d.rearrange("(t p) d -> p t d", p=P)
    acc_v = [a.rearrange("(t p) d -> p t d", p=P) for a in acc_d]

    with ExitStack() as ctx:
        def sb(name, shape, dt=F32):
            return ctx.enter_context(nc.sbuf_tensor(name, shape, dt))

        def sem(name):
            return ctx.enter_context(nc.semaphore(name))

        two = [ctx.enter_context(nc.psum_tensor(f"two{i}", [P, 1024], F32)) for i in range(4)]

        def bk_(i):
            return two[i // 2][:, (i % 2) * 512:(i % 2) * 512 + 512]

        x = sb("x", [P, NT, D])
        xn = sb("xn", [P, NT, D])
        kT = sb("kT", [P, NTOK])
        vT = sb("vT", [P, NTOK])
        v = sb("v", [P, NT, DH])
        wfcT = sb("wfcT", [P, KH, FF1], F16)
        wpjT = sb("wpjT", [P, FF1 // P, D], F16)
        wqT_hi = sb("wqT_hi", [P, KH, QKV1], F16)
        wqT_lo = sb("wqT_lo", [P, KH, QKV1], F16)
        wpoT = sb("wpoT", [P, KH, D])
        WoS = sb("WoS", [P, D])
        rwT = sb("rwT", [P, KH, NE])
        sgu = sb("sgu", [P, 2, KH, FF])
        sdn = sb("sdn", [FF, D])
        bkc = sb("bkc", [P, 1])
        bks = sb("bks", [P, 1])
        bvc = sb("bvc", [P, 1])
        bvr = sb("bvr", [1, DH])
        bo_b = sb("bo_b", [P, D])
        eb_b = sb("eb_b", [P, NE])
        ident = sb("ident", [P, P])
        ident16 = sb("ident16", [P, P], F16)
        ones = sb("ones", [P, P])
        ones16 = sb("ones16", [P, P], F16)
        before16 = sb("before16", [P, P], F16)
        tid_i = sb("tid_i", [P, NT], I32)
        tid = sb("tid", [P, NT])
        trash_i = sb("trash_i", [P, 1], I32)
        trash = sb("trash", [P, 1])
        diag = sb("diag", [P, GE])
        st = sb("st", [P, NT, 6])
        mv = sb("mv", [P, NT, 2])
        rstd = sb("rstd", [P, NT])
        gsum = sb("gsum", [P, 2])
        gwv = sb("gwv", [P, 2])
        thr = sb("thr", [P, 2])
        nthr = sb("nthr", [P, 2])
        gsp = sb("gsp", [P, NT, 12])
        gr = sb("gr", [P, NT, 12])
        mx8 = sb("mx8", [P, NT, 8])
        rep8 = sb("rep8", [P, NT, 8])
        gmask = sb("gmask", [P, NT, GROUPS])
        den = sb("den", [P, NT])
        rden = sb("rden", [P, NT])
        empty = sb("empty", [P, NE])
        slotR = sb("slotR", [P, NGE * SB])
        slotE = sb("slotE", [NE, CAP])
        idxE = sb("idxE", [P, NE], I32)
        nmax = sb("nmax", [P, NT])
        rsum = sb("rsum", [P, NT])
        rinv = sb("rinv", [P, NT])

        A = sb("A", [P, 8192])
        xT = A[:, 0:4096].rearrange("p (t k n) -> p t k n", t=NT, k=KH)
        Wo_s = A[:, 4096:8192].rearrange("p (h n) -> p h n", h=HQ)
        sh_t, sh_a = A[0:FF, 6144:6656], A[0:FF, 6656:7168]
        sh_h = [A[0:FF, 7168 + 512 * i:7680 + 512 * i] for i in range(2)]
        probs = [A[:, 1024 * i:1024 * i + 1024] for i in range(2)]
        probT = [A[:, 2048 + 1024 * i:3072 + 1024 * i].rearrange("p (i j) -> p i j", i=8) for i in range(2)]
        s0 = A[:, 4096:8192].rearrange("p (t d) -> p t d", t=NT)
        hid = [A[:, 2048 * i:2048 * i + 2048].rearrange("p (q f) -> p q f", q=GT) for i in range(2)]

        F = sb("F", [P, 15104])
        def f_te(i):
            return F[:, 1024 * i:1024 * i + 1024].rearrange("p (t e) -> p t e", t=NT)
        s_sig, s_sc, s_masked, s_rep, s_sel, s_w = f_te(0), f_te(1), f_te(4), f_te(5), f_te(6), f_te(7)
        t_hi1 = F[:, 2048:2560].rearrange("p (g j) -> p g j", j=4)
        t_lo1 = F[:, 2560:3072].rearrange("p (g j) -> p g j", j=4)
        t_hi2, t_m2, t_l2, t_lo2 = [F[:, 3072 + 256 * i:3328 + 256 * i].rearrange("p (g j) -> p g j", j=2)
                                    for i in range(4)]
        t_hi3, t_m3, t_l3, t_lo3 = [F[:, 4096 + 128 * i:4224 + 128 * i].rearrange("p (g j) -> p g j", j=1)
                                    for i in range(4)]
        s_pos = f_te(1)
        pos_i, b_i, a_i = f_te(2).bitcast(I32), f_te(3).bitcast(I32), f_te(4).bitcast(I32)
        rw_s = F[0:NE, 5120:5120 + D]
        Wk_s, Wv_s = [F[:, 6144 + 256 * i:6400 + 256 * i].rearrange("p (k n) -> p k n", k=KH) for i in range(2)]
        H = F[:, 8192:10752].bitcast(F16)
        sel16 = H[:, 0:1024].rearrange("p (e t) -> p e t", t=NT)
        cum16 = H[:, 1024:2048].rearrange("p (e t) -> p e t", t=NT)
        keep16 = H[:, 2048:3072].rearrange("p (e t) -> p e t", t=NT)
        a16 = H[:, 3072:4096].rearrange("p (t e) -> p t e", t=NT)
        b16 = H[:, 4096:5120].rearrange("p (t e) -> p t e", t=NT)
        slot_m = F[:, 0:1024].rearrange("p (g e) -> p g e", e=GE)
        hot_a = F[:, 10752:14848].bitcast(F16).rearrange("p (t e a) -> p t e a", t=NT, a=SA)
        wfc_s = F[:, 10752:12800].rearrange("p (c d) -> p c d", c=FF1 // P)
        wpj_s = F[:, 12800:14848].rearrange("p (c d) -> p c d", c=KH)
        acc1 = F[:, 10752:14848].rearrange("p (t d) -> p t d", t=NT)
        oT = [F[:, 14848 + 128 * i:14976 + 128 * i] for i in range(2)]

        at = [0]

        def l1(n):
            at[0] += n
            assert at[0] <= 10752, at
            return F[:, at[0] - n:at[0]]
        hiT = [l1(512).bitcast(F16) for _ in range(2)]
        loT = [l1(512).bitcast(F16) for _ in range(2)]
        hi16 = [l1(512).bitcast(F16) for _ in range(GT)]
        lo16 = [l1(512).bitcast(F16) for _ in range(GT)]
        xq = [l1(GT * D).rearrange("p (q d) -> p q d", q=GT) for _ in range(2)]
        qT_hi = l1(GT * D // 2).bitcast(F16).rearrange("p (q k n) -> p q k n", q=GT, k=KH)
        qT_lo = l1(GT * D // 2).bitcast(F16).rearrange("p (q k n) -> p q k n", q=GT, k=KH)
        s1 = [l1(GT * D).rearrange("p (q d) -> p q d", q=GT) for _ in range(2)]
        qkv1 = [l1(QKV1).rearrange("p (g c) -> p g c", c=GS1) for _ in range(2)]
        kv0 = [l1(NKV1 * 2 * HD1).rearrange("p (g c) -> p g c", c=2 * HD1) for _ in range(2)]
        pr = l1(D).rearrange("p (g r d) -> p g r d", r=REP1, d=HD1)
        dk, dv, hv, mid = [l1(NKV1 * HD1).rearrange("p (g d) -> p g d", d=HD1) for _ in range(4)]
        att = l1(GT * D).rearrange("p (s n) -> p s n", s=2)
        tg = [l1(GT * D).rearrange("p (s d) -> p s d", s=2) for _ in range(2)]
        tz = l1(GT * D).rearrange("p (q d) -> p q d", q=GT)
        zu = l1(GT * D).rearrange("p (q d) -> p q d", q=GT)
        sq = [vT[:, FF1 * i:FF1 * i + FF1] for i in range(GT)]
        attT = kT[:, 0:GT * D].rearrange("p (s k n) -> p s k n", s=2, k=KH)

        W = sb("W", [P, 8192])
        wqkv_s = W[:, 0:768].rearrange("p (c d) -> p c d", c=QKV1 // P)
        wpo_s = W[:, 768:1280].rearrange("p (c d) -> p c d", c=KH)
        tern_tmp = W[:, 1280:3328]
        hot_b = W[:, :].bitcast(F16).rearrange("p (b t e) -> p b t e", b=SB, t=NT)
        wgu = [W[:, 704 * r:704 * r + 704].rearrange("p (e m k f) -> p e m k f", e=WG, m=2, k=KH) for r in range(WR)]
        wdn = [W[0:FF, 2112 + 512 * r:2624 + 512 * r].rearrange("p (e n) -> p e n", e=WG) for r in range(WR)]
        xg = [W[:, 3648 + 320 * r:3968 + 320 * r] for r in range(XR)]
        xgT = [W[:, 5888 + 256 * r:6144 + 256 * r].rearrange("p (k n) -> p k n", k=KH) for r in range(2)]
        hT = [W[0:FF, 6400 + 128 * r:6528 + 128 * r] for r in range(2)]
        eth = [W[0:FF, 6656 + 128 * r:6784 + 128 * r] for r in range(2)]
        ea = [W[0:FF, 6912 + 128 * r:7040 + 128 * r] for r in range(2)]
        ysb = [W[:, 7168 + 256 * r:7424 + 256 * r] for r in range(YS)]
        st1 = sb("st1", [P, GT, 6])
        mv1 = sb("mv1", [P, GT, 2])
        amax, qscale, hsum, nmean, ssq, hscale, hbias, tmpc = [
            sb(n, [P, GT]) for n in ("amax", "qscale", "hsum", "nmean", "ssq", "hscale", "hbias", "tmpc")]
        kvscale, fcscale, zhalf = [[sb(f"{n}{i}", [P, GT]) for i in range(2)] for n in ("kvscale", "fcscale", "zhalf")]
        gwc = sb("gwc", [P, 2])
        nv, ny, nt2 = [sb(n, [P, 4 * GT]) for n in ("nv", "ny", "nt2")]
        ni = sb("ni", [P, 4 * GT], I32)
        dif, td = [sb(n, [P, NH1]) for n in ("dif", "td")]

        ld_x = [sem(f"ld_x{c}") for c in range(4)]
        ld_w0 = sem("ld_w0")
        ld_w1 = sem("ld_w1")
        ld_wo = sem("ld_wo")
        ld_w2 = sem("ld_w2")
        ld_sh = sem("ld_sh")
        ld_e = [sem(f"ld_e{r}") for r in range(WR)]
        consts = sem("consts")
        pool_seq = sem("pool_seq")
        wos_done = sem("wos_done")
        dve = sem("dve_seq")
        act = sem("act_seq")
        ln1_var, ln1_std, xn_ready, xn_stored, w_ready, w_stored = [sem(n) for n in (
            "ln1_var", "ln1_std", "xn_ready", "xn_stored", "w_ready", "w_stored")]
        rwT_ps, rwT_ready, xT_ps, xT_ready, logits_ps, tanh_ready, bks_ready = [sem(n) for n in (
            "rwT_ps", "rwT_ready", "xT_ps", "xT_ready", "logits_ps", "tanh_ready", "bks_ready")]
        kv_ps, kv_ready, gsum_ready, gw_ps, gw_ready, tern_ready, prep_ps, prep_ready, prep_lo = [sem(n) for n in (
            "kv_ps", "kv_ready", "gsum_ready", "gw_ps", "gw_ready", "tern_ready", "prep_ps", "prep_ready", "prep_lo")]
        sel_ready, pos_ps, hot_ready, slot_ps, slotR_ready, slot_out, slot_in, idx_ps, idxE_ready = [
            sem(n) for n in ("sel_ready", "pos_ps", "hot_ready", "slot_ps", "slotR_ready", "slot_out", "slot_in",
                             "idx_ps", "idxE_ready")]
        sgu_ps, stanh_ready, shT_ready, sdn_ps, sy_ready, acc_init = [sem(n) for n in (
            "sgu_ps", "stanh_ready", "shT_ready", "sdn_ps", "sy_ready", "acc_init")]
        xg_ld = [sem(f"xg_ld{r}") for r in range(XR)]
        xgT_ps, xgT_ready, gu_ps, gtanh_ready, hT_ready, y_ps, y_ready = [sem(n) for n in (
            "xgT_ps", "xgT_ready", "gu_ps", "gtanh_ready", "hT_ready", "y_ps", "y_ready")]
        y_added = [sem(f"y_added{i}") for i in range(2)]
        acc_ld = [sem(f"acc_ld{i}") for i in range(NP)]
        sc_ps, nmax_ready, probs_ready, pT_ps, pT_act, pT_dve, o_ps, oT_ready, wo_ps, s0_ready = [sem(n) for n in (
            "sc_ps", "nmax_ready", "probs_ready", "pT_ps", "pT_act", "pT_dve", "o_ps", "oT_ready", "wo_ps", "s0_ready")]
        acc_ready, gate_ready, silu_ready, x1_ready, xq_ready, qT_ps, qT_hi_ready, qT_lo_ready = [sem(n) for n in (
            "acc_ready", "gate_ready", "silu_ready", "x1_ready", "xq_ready", "qT_ps", "qT_hi_ready", "qT_lo_ready")]
        scale_ready, qkv_ps, qkv_ready, prod_ready, dif_ready, td_ready, att0_ready, att_ready, attT_ps, attT_ready, s1_ps, s1_ready = [
            sem(n) for n in ("scale_ready", "qkv_ps", "qkv_ready", "prod_ready", "dif_ready", "td_ready", "att0_ready",
                             "att_ready", "attT_ps",
                             "attT_ready", "s1_ps", "s1_ready")]
        fc_ps, gelu_ready, nmean_ready, sq_ready, zhalf_ready, hi_ready, lo_ready, hT1_ps, hT1_ready = [
            sem(n) for n in ("fc_ps", "gelu_ready", "nmean_ready", "sq_ready", "zhalf_ready",
                             "hi_ready", "lo_ready", "hT1_ps", "hT1_ready")]
        z_ps, ztanh_ready, zu_ready, out_ready, out_stored = [sem(n) for n in (
            "z_ps", "ztanh_ready", "zu_ready", "out_ready", "out_stored")]

        def pair(a, p):
            return a.rearrange("p (s i) d -> p s i d", s=2)[:, :, p, :]

        def heads(a):
            return a.unsqueeze(2).to_broadcast([P, NKV1, REP1, HD1])

        att_h = [att[:, s_, :].rearrange("p (g r d) -> p g r d", r=REP1, d=HD1) for s_ in range(2)]

        block = ctx.enter_context(nc.Block())

        @block.sync
        def _(sp):
            for c in range(4):
                sp.dma_start(x[:, 4 * c:4 * c + 4, :], x_v[:, 4 * c:4 * c + 4, :]).then_inc(ld_x[c], 16)
            sp.dma_start(rw_s, rw).then_inc(ld_w0, 16)
            sp.dma_start(eb_b[:, :], eb.rearrange("(a n) -> a n", a=1).to_broadcast([P, NE])).then_inc(ld_w0, 16)
            for dst, src in ((Wk_s, Wk), (Wv_s, Wv)):
                sp.dma_start(dst[:, :, :], src.rearrange("(p k) n -> p k n", k=KH)).then_inc(ld_w0, 16)
            for dst, src in ((bkc, bk), (bvc, bv)):
                sp.dma_start(dst[:, :], src.rearrange("(p a) -> p a", a=1)).then_inc(ld_w0, 16)
            sp.dma_start(bvr[:, :], bv.rearrange("(a n) -> a n", a=1)).then_inc(ld_w0, 16)
            sp.dma_start(wfc_s, wfc.rearrange("(c p) d -> p c d", p=P)).then_inc(ld_w1, 16)
            sp.dma_start(wpj_s, wpj.rearrange("(c p) d -> p c d", p=P)).then_inc(ld_w1, 16)
            sp.dma_start(Wo_s, Wo.rearrange("(h p) n -> p h n", p=P)).then_inc(ld_wo, 16)
            sp.dma_start(wqkv_s, wqkv.rearrange("(c p) d -> p c d", p=P)).then_inc(ld_w2, 16)
            sp.dma_start(wpo_s, wpo.rearrange("(c p) d -> p c d", p=P)).then_inc(ld_w2, 16)
            for m, src in enumerate((sg, su)):
                sp.dma_start(sgu[:, m, :, :], src.rearrange("(p k) f -> p k f", k=KH)).then_inc(ld_sh, 16)
            sp.dma_start(sdn[:, :], sd).then_inc(ld_sh, 16)
            sp.dma_start(bo_b[:, :], bo.rearrange("(a n) -> a n", a=1).to_broadcast([P, D])).then_inc(ld_sh, 16)
            for c in range(4):
                sp.wait_ge(xn_ready, 4 * c + 4)
                sp.dma_start(tok_v[:, 4 * c:4 * c + 4, 0:D], xn[:, 4 * c:4 * c + 4, :]).then_inc(xn_stored, 16)
            sp.wait_ge(xn_ready, NT)
            sp.dma_start(tok_d[NTOK:NTOK + P, 0:D], xn[:, 0, :]).then_inc(xn_stored, 16)
            sp.wait_ge(w_ready, 1)
            sp.dma_start(tok_v[:, 0:NT, D:D + NE], s_w).then_inc(w_stored, 16)
            sp.dma_start(tok_d[NTOK:NTOK + P, D:D + NE], s_w[:, 0, :]).then_inc(w_stored, 16)
            for c in range(NT // SC):
                sp.wait_ge(sy_ready, 2 * c + 2)
                for a in acc_v:
                    sp.dma_start(a[:, SC * c:SC * c + SC, :], xn[:, SC * c:SC * c + SC, :]).then_inc(acc_init, 16)
            for a in acc_d:
                sp.dma_start(a[NTOK:NTOK + P, :], xn[:, 0, :]).then_inc(acc_init, 16)

            def load_experts(g):
                r, e = g % WR, g * WG
                for m, src in enumerate((wg, wu)):
                    sp.dma_start(wgu[r][:, :, m, :, :].rearrange("p e k f -> p e (k f)"),
                                 src[e:e + WG].rearrange("e (p k) f -> p e (k f)", k=KH)).then_inc(ld_e[r], 16)
                sp.dma_start(wdn[r], wd[e:e + WG].rearrange("e f n -> f e n")).then_inc(ld_e[r], 16)

            sp.wait_ge(slot_ps, 1)
            for g in range(WR):
                load_experts(g)
            sp.wait_ge(slotR_ready, 1)
            sp.dma_start(slot_d.rearrange("(g p b) -> p g b", p=P, b=SB),
                         slotR[:, :].rearrange("p (g b) -> p g b", b=SB)).then_inc(slot_out, 16)
            sp.wait_ge(slot_out, 16)
            sp.dma_start(slotE[:, :], slot_d.rearrange("(e s) -> e s", s=CAP)).then_inc(slot_in, 16)
            for g in range(WR, NE // WG):
                sp.wait_ge(y_ps, WG * (g - WR + 1))
                load_experts(g)
            for i in range(2):
                sp.wait_ge(y_added[i], 16 * (NE // 2))
            for p in range(NP):
                for a, dst in zip(acc_v, (xn, acc1)):
                    sp.dma_start(pair(dst, p), a[:, 0:NT, :].rearrange("p (s i) d -> p s i d", s=2)[:, :, p, :])\
                        .then_inc(acc_ld[p], 16)
            for p in range(NP):
                for q_ in range(GT):
                    t = p + NP * q_
                    sp.wait_ge(out_ready, GT * p + q_ + 1)
                    sp.dma_start(out_v[:, t, :], x[:, t, :]).then_inc(out_stored, 16)
            sp.wait_ge(out_stored, 16 * NT)

        @block.gpsimd
        def _(pool):
            step = [0]

            def then(ins):
                step[0] += 1
                ins.then_inc(pool_seq, 1)
                pool.wait_ge(pool_seq, step[0])

            then(pool.memset(ident[:, :], 0.0))
            then(pool.affine_select(out=ident[:, :], in_=ident[:, :], compare_op=ALU.not_equal, fill=1.0,
                                    base=0, pattern=[[-1, P]], channel_multiplier=1))
            then(pool.tensor_copy(ident16[:, :], ident[:, :]))
            then(pool.memset(ones[:, :], 1.0))
            then(pool.memset(ones16[:, :], 1.0))
            then(pool.memset(before16[:, :], 0.0))
            then(pool.affine_select(out=before16[:, :], in_=before16[:, :], compare_op=ALU.is_gt, fill=-1.0,
                                    base=0, pattern=[[1, P]], channel_multiplier=-1))
            then(pool.iota(tid_i[:, :], [[P, NT]], base=1, channel_multiplier=1))
            then(pool.tensor_copy(tid[:, :], tid_i[:, :]))
            then(pool.iota(trash_i[:, :], [[0, 1]], base=NTOK + 1, channel_multiplier=1))
            then(pool.tensor_copy(trash[:, :], trash_i[:, :]))
            then(pool.affine_select(out=diag[:, :], in_=ones[:, 0:GE], compare_op=ALU.is_ge, fill=0.0,
                                    base=0, pattern=[[-SA, GE]], channel_multiplier=1))
            then(pool.affine_select(out=diag[:, :], in_=diag[:, :], compare_op=ALU.is_ge, fill=0.0,
                                    base=SA - 1, pattern=[[SA, GE]], channel_multiplier=-1))
            then(pool.memset(keep16, 1.0))
            then(pool.memset(keep16[:, :, 0:1], 0.0))
            then(pool.memset(rep8[:, :, :], SENTINEL))
            then(pool.memset(gsp[:, :, :], SENTINEL))
            then(pool.memset(nv[:, :], 1.0))
            pool.memset(gsum[:, :], 0.0).then_inc(consts, 1)
            pool.wait_ge(ld_wo, 16)
            then(pool.tensor_tensor(WoS[:, :], Wo_s[:, 0, :], Wo_s[:, 1, :], ALU.add))
            for h in range(2, HQ):
                ins = pool.tensor_tensor(WoS[:, :], WoS[:, :], Wo_s[:, h, :], ALU.add)
                if h < HQ - 1:
                    then(ins)
            ins.then_inc(wos_done, 1)
            def gather(n):
                if n >= XR:
                    pool.wait_ge(y_ready, n - XR + 1)
                pool.indirect_dma_start(out=xg[n % XR], out_offset=None, in_=tok_d[:, :],
                                        in_offset=bass.IndirectOffsetOnAxis(ap=idxE[:, n:n + 1], axis=0))\
                    .then_inc(xg_ld[n % XR], 16)

            pool.wait_ge(idxE_ready, 1)
            pool.wait_ge(xn_stored, 5 * 16)
            pool.wait_ge(w_stored, 2 * 16)
            for n in range(XR - 1):
                gather(n)
            pool.wait_ge(acc_init, 10 * 16)
            for n in range(NE):
                if n + XR - 1 < NE:
                    gather(n + XR - 1)
                pool.wait_ge(y_ready, n + 1)
                if n >= 2:
                    pool.wait_ge(y_added[n % 2], 16 * (n // 2))
                pool.indirect_dma_start(out=acc_d[n % 2][:, :],
                                        out_offset=bass.IndirectOffsetOnAxis(ap=idxE[:, n:n + 1], axis=0),
                                        in_=ysb[n % YS], in_offset=None, compute_op=ALU.add)\
                    .then_inc(y_added[n % 2], 16)

            def total(p):
                pool.wait_ge(acc_ld[p], 32)
                pool.tensor_tensor(pair(xn, p), pair(xn, p), pair(acc1, p), ALU.add).then_inc(acc_ready, 1)

            def add_gated(p):
                pool.wait_ge(silu_ready, p + 1)
                pool.wait_ge(s0_ready, NT)
                then(pool.tensor_tensor(tg[p % 2], tg[p % 2], pair(s0, p), ALU.mult))
                pool.tensor_tensor(pair(x, p), pair(x, p), tg[p % 2], ALU.add).then_inc(x1_ready, 1)

            def score_products(p):
                pool.wait_ge(qkv_ready, 2 * p + 2)
                new, old = qkv1[p % 2], kv0[p % 2]
                if p:
                    pool.wait_ge(dif_ready, p)
                then(pool.tensor_tensor(dk, new[:, :, REP1 * HD1:GS1 - HD1], old[:, :, 0:HD1], ALU.subtract))
                pool.tensor_tensor(pr, new[:, :, 0:REP1 * HD1].rearrange("p g (r d) -> p g r d", r=REP1), heads(dk),
                                   ALU.mult).then_inc(prod_ready, 1)
                then(pool.tensor_tensor(dv, new[:, :, GS1 - HD1:GS1], old[:, :, HD1:2 * HD1], ALU.subtract))
                then(pool.tensor_scalar(hv, dv, 0.5, None, ALU.mult))
                then(pool.tensor_tensor(mid, hv, old[:, :, HD1:2 * HD1], ALU.add))

            def attend(p):
                pool.wait_ge(td_ready, p + 1)
                if p:
                    pool.wait_ge(attT_ps, p)
                then(pool.tensor_tensor(att_h[1], heads(hv), td[:, :].rearrange("p (g r) -> p g r", r=REP1).unsqueeze(3)
                                        .to_broadcast([P, NKV1, REP1, HD1]), ALU.mult))
                pool.tensor_tensor(att_h[1], att_h[1], heads(mid), ALU.add).then_inc(att_ready, 1)

            def low(n):
                pool.wait_ge(hi_ready, n + 1)
                pool.tensor_tensor(lo16[n % GT], hid[n // GT % 2][:, n % GT, :], hi16[n % GT], ALU.subtract)\
                    .then_inc(lo_ready, 1)

            def finish(n):
                q_, t = n % GT, n // GT + NP * (n % GT)
                pool.wait_ge(zu_ready, n + 1)
                pool.wait_ge(s1_ready, n // GT + 1)
                then(pool.tensor_tensor(zu[:, q_, :], zu[:, q_, :], s1[n // GT % 2][:, q_, :], ALU.mult))
                pool.tensor_tensor(x[:, t, :], x[:, t, :], zu[:, q_, :], ALU.add).then_inc(out_ready, 1)

            for p in range(4):
                total(p)
            for p in range(3):
                add_gated(p)
            score_products(0)
            for p in range(NP + 2):
                if p + 4 < NP:
                    total(p + 4)
                if p < NP:
                    attend(p)
                if p >= 2:
                    for q_ in range(GT):
                        finish(GT * (p - 2) + q_)
                if p + 3 < NP:
                    add_gated(p + 3)
                if p + 1 < NP:
                    score_products(p + 1)
                if p < NP:
                    for q_ in range(GT):
                        low(GT * p + q_)

        @block.scalar
        def _(sc):
            step = [0]

            def then(ins):
                step[0] += 1
                ins.then_inc(act, 1)
                sc.wait_ge(act, step[0])

            sc.wait_ge(ln1_var, 1)
            sc.activation(rstd[:, :], rstd[:, :], ACT.Sqrt).then_inc(ln1_std, 1)
            sc.wait_ge(rwT_ps, 1)
            sc.activation(rwT[:, :, :], bk_(4)[:, 0:KH * NE].rearrange("p (k e) -> p k e", k=KH), ACT.Copy).then_inc(rwT_ready, 1)
            for t in range(NT):
                sc.wait_ge(xT_ps, t + 1)
                sc.activation(xT[:, t, :, :], bk_(t % 2)[:, 0:D].rearrange("p (k n) -> p k n", k=KH), ACT.Copy)\
                    .then_inc(xT_ready, 1)
            for c in range(2):
                sc.wait_ge(logits_ps, c + 1)
                sc.activation(s_sig[:, 8 * c:8 * c + 8, :], bk_(2 + c).rearrange("p (t e) -> p t e", t=8), ACT.Tanh,
                              scale=0.5).then_inc(tanh_ready, 1)
            sc.wait_ge(ld_w1, 32)
            sc.wait_ge(consts, 1)
            for m, w in enumerate((wfc_s, wpj_s)):
                sc.activation(tern_tmp, w.rearrange("p c d -> p (c d)"), ACT.Abs,
                              accum_out=gsum[:, m:m + 1]).then_inc(gsum_ready, 1)
                sc.wait_ge(gsum_ready, m + 1)
            sc.wait_ge(gw_ps, 1)
            sc.activation(gwv[:, :], bk_(7)[:, 0:2], ACT.Copy, scale=1.0 / (FF1 * D)).then_inc(gw_ready, 1)
            sc.wait_ge(bks_ready, 1)
            for c in range(4):
                cols = slice(512 * c, 512 * c + 512)
                sc.wait_ge(kv_ps, 3 * c + 1)
                sc.activation(kT[:, cols], bk_(4), ACT.Identity, bias=bks[:, 0:1], scale=1.0 / DH).then_inc(kv_ready, 1)
                sc.wait_ge(kv_ps, 3 * c + 2)
                sc.activation(vT[:, cols], bk_(5), ACT.Identity, bias=bvc[:, 0:1], scale=1.0).then_inc(kv_ready, 1)
                sc.wait_ge(kv_ps, 3 * c + 3)
                sc.activation(v[:, 4 * c:4 * c + 4, :], bk_(6).rearrange("p (t d) -> p t d", t=4), ACT.Copy)\
                    .then_inc(kv_ready, 1)
            for j in range(11):
                sc.wait_ge(prep_ps, j + 1)
                b = bk_(4 + j % 2)
                if j < 4:
                    ins = sc.activation(wfcT[:, j // 2, 512 * (j % 2):512 * (j % 2) + 512], b, ACT.Copy)
                elif j < 8:
                    ins = sc.activation(wpjT[:, 2 * (j - 4):2 * (j - 4) + 2, :],
                                        b.rearrange("p (k n) -> p k n", k=2), ACT.Copy)
                elif j == 8:
                    ins = sc.activation(wpoT[:, :, :], b.rearrange("p (k n) -> p k n", k=KH), ACT.Copy)
                else:
                    ins = sc.activation(wqT_hi[:, j - 9, :], b[:, 0:QKV1], ACT.Copy, scale=WSCALE)
                ins.then_inc(prep_ready, 1)
            def shared_gate(c):
                sc.wait_ge(sgu_ps, c + 1)
                if c >= 1:
                    sc.wait_ge(shT_ready, c)
                sc.activation(sh_t, bk_(0)[0:FF, :], ACT.Tanh, scale=0.5).then_inc(stanh_ready, 1)

            def shared_out(c):
                for j in range(2):
                    sc.wait_ge(sdn_ps, 2 * c + j + 1)
                    t = SC * c + 2 * j
                    sc.activation(xn[:, t:t + 2, :], bk_(2 + j).rearrange("p (t d) -> p t d", t=2), ACT.Copy, scale=0.25)\
                        .then_inc(sy_ready, 1)

            sc.wait_ge(wos_done, 1)
            sc.wait_ge(xn_stored, 5 * 16)
            for c in range(NT // SC):
                shared_gate(c)
                if c:
                    shared_out(c - 1)
            shared_out(NT // SC - 1)

            def exps(t):
                sc.wait_ge(nmax_ready, t + 1)
                if t >= 2:
                    sc.wait_ge(pT_ps, 2 * (t - 1))
                sc.activation(probs[t % 2], two[2][:, :], ACT.Exp, bias=nmax[:, t:t + 1], scale=1.0,
                              accum_out=rsum[:, t:t + 1]).then_inc(probs_ready, 1)

            def attention_step(t, step):
                if step == 0:
                    sc.wait_ge(pT_ps, 2 * t + 1)
                    if t >= 2:
                        sc.wait_ge(o_ps, t - 1)
                    sc.activation(probT[t % 2][:, 0:4, :], bk_(0).rearrange("p (i j) -> p i j", i=4), ACT.Copy)\
                        .then_inc(pT_act, 1)
                elif step == 2 and t + 1 < NT:
                    exps(t + 1)
                elif step == 3:
                    sc.wait_ge(o_ps, t + 1)
                    if t >= 2:
                        sc.wait_ge(wo_ps, t - 1)
                    sc.activation(oT[t % 2], bk_(1)[:, 0:P], ACT.Copy).then_inc(oT_ready, 1)

            exps(0)
            for t in range(EARLY):
                for step_ in range(STEPS):
                    attention_step(t, step_)

            def turn(n):
                sc.wait_ge(xgT_ps, n + 1)
                if n >= 2:
                    sc.wait_ge(gu_ps, n - 1)
                sc.activation(xgT[n % 2], bk_(2)[:, 0:D].rearrange("p (k n) -> p k n", k=KH), ACT.Copy)\
                    .then_inc(xgT_ready, 1)

            turn(0)
            for n in range(NE):
                if n + 1 < NE:
                    turn(n + 1)
                sc.wait_ge(gu_ps, n + 1)
                if n >= 2:
                    sc.wait_ge(hT_ready, n - 1)
                sc.activation(eth[n % 2], bk_(6 + n % 2)[0:FF, 0:CAP], ACT.Tanh, scale=0.5).then_inc(gtanh_ready, 1)
                if EARLY + n // STEPS < NT:
                    attention_step(EARLY + n // STEPS, n % STEPS)

            def gate(p):
                sc.wait_ge(acc_ready, p + 1)
                if p >= 2:
                    sc.wait_ge(x1_ready, p - 1)
                sc.activation(tg[p % 2], pair(xn, p), ACT.Tanh, scale=0.5).then_inc(gate_ready, 1)

            def high_q(p):
                sc.wait_ge(qT_ps, p + 1)
                if p:
                    sc.wait_ge(fc_ps, GT * p)
                sc.activation(qT_hi, bk_(0).rearrange("p (q k n) -> p q k n", q=GT, k=KH), ACT.Copy).then_inc(qT_hi_ready, 1)

            def take_qkv(p):
                sc.wait_ge(scale_ready, p + 1)
                sc.wait_ge(qkv_ps, p + 1)
                if p >= 2:
                    sc.wait_ge(att_ready, p - 1)
                sc.activation(qkv1[p % 2], bk_(1)[:, 0:QKV1].rearrange("p (g c) -> p g c", g=NKV1), ACT.Copy,
                              scale=kvscale[p % 2][:, 1:2]).then_inc(qkv_ready, 1)
                sc.activation(kv0[p % 2], bk_(1)[:, QKV1:512].rearrange("p (g c) -> p g c", g=NKV1), ACT.Copy,
                              scale=kvscale[p % 2][:, 0:1]).then_inc(qkv_ready, 1)

            def gelu(n):
                q_ = n % GT
                sc.wait_ge(scale_ready, n // GT + 1)
                sc.wait_ge(fc_ps, n + 1)
                if n >= 2 * GT:
                    sc.wait_ge(lo_ready, n - 2 * GT + 1)
                sc.activation(hid[n // GT % 2][:, q_, :], two[1][:, :], ACT.Gelu, scale=fcscale[n // GT % 2][:, q_:q_ + 1],
                              accum_out=hsum[:, q_:q_ + 1]).then_inc(gelu_ready, 1)

            def square(n):
                q_ = n % GT
                sc.wait_ge(nmean_ready, n // GT + 1)
                sc.activation(sq[q_], hid[n // GT % 2][:, q_, :], ACT.Square, bias=nmean[:, q_:q_ + 1], scale=1.0,
                              accum_out=ssq[:, q_:q_ + 1]).then_inc(sq_ready, 1)

            def take_hT(n):
                sc.wait_ge(hT1_ps, n + 1)
                if n >= 2:
                    sc.wait_ge(z_ps, n - 1)
                sc.activation(hiT[n % 2], bk_(4).bitcast(F16), ACT.Copy).then_inc(hT1_ready, 1)
                sc.activation(loT[n % 2], bk_(5).bitcast(F16), ACT.Copy).then_inc(hT1_ready, 1)

            def own_value(p):
                if p:
                    sc.wait_ge(attT_ps, p)
                sc.activation(att_h[0], heads(kv0[p % 2][:, :, HD1:2 * HD1]), ACT.Copy).then_inc(att0_ready, 1)

            def half_tanh(p):
                sc.wait_ge(dif_ready, p + 1)
                sc.activation(td[:, :], dif[:, :], ACT.Tanh, scale=0.5 / HD1 ** 0.5).then_inc(td_ready, 1)

            def take_attT(p):
                sc.wait_ge(attT_ps, p + 1)
                sc.activation(attT, bk_(6).rearrange("p (s k n) -> p s k n", s=2, k=KH), ACT.Copy).then_inc(attT_ready, 1)

            def take_s1(p):
                sc.wait_ge(s1_ps, p + 1)
                if p >= 2:
                    sc.wait_ge(out_ready, GT * (p - 1))
                sc.wait_ge(zhalf_ready, p + 1)
                for q_ in range(GT):
                    ins = sc.activation(s1[p % 2][:, q_, :], bk_(6)[:, D * q_:D * q_ + D], ACT.Copy,
                                        scale=zhalf[p % 2][:, q_:q_ + 1])
                ins.then_inc(s1_ready, 1)

            def gate2(p):
                sc.wait_ge(z_ps, GT * p + GT)
                for q_ in range(GT):
                    sc.activation(tz[:, q_, :], bk_(7)[:, D * q_:D * q_ + D], ACT.Tanh, scale=zhalf[p % 2][:, q_:q_ + 1])\
                        .then_inc(ztanh_ready, 1)

            for p in range(3):
                gate(p)
            high_q(0)
            take_qkv(0)
            for q_ in range(GT):
                gelu(q_)
            high_q(1)
            for p in range(NP + 2):
                if p < NP:
                    for q_ in range(GT):
                        square(GT * p + q_)
                    own_value(p)
                    half_tanh(p)
                if 1 <= p <= NP:
                    take_s1(p - 1)
                if p >= 2:
                    gate2(p - 2)
                if p + 1 < NP:
                    take_qkv(p + 1)
                    for q_ in range(GT):
                        gelu(GT * (p + 1) + q_)
                if p + 2 < NP:
                    high_q(p + 2)
                if p + 3 < NP:
                    gate(p + 3)
                if 1 <= p <= NP:
                    take_hT(GT * (p - 1))
                if p < NP:
                    take_attT(p)
                if 1 <= p <= NP:
                    take_hT(GT * (p - 1) + 1)

        @block.vector
        def _(ve):
            step = [0]

            def mark(ins):
                step[0] += 1
                ins.then_inc(dve, 1)
                return step[0]

            def then(ins):
                ve.wait_ge(dve, mark(ins))

            for t in range(NT):
                ve.wait_ge(ld_x[t // 4], 16)
                last = mark(ve.bn_stats(st[:, t, :], x[:, t, :]))
            ve.wait_ge(dve, last)
            for t in range(NT):
                last = mark(ve.bn_aggr(mv[:, t, :], st[:, t, :]))
            ve.wait_ge(dve, last)
            ve.tensor_scalar(rstd[:, :], mv[:, :, 1], EPS_LN, None, ALU.add).then_inc(ln1_var, 1)
            ve.wait_ge(ln1_std, 1)
            then(ve.reciprocal(rstd[:, :], rstd[:, :]))
            for t in range(NT):
                ve.tensor_scalar(xn[:, t, :], x[:, t, :], mv[:, t, 0:1], rstd[:, t:t + 1], ALU.subtract, ALU.mult)\
                    .then_inc(xn_ready, 1)
            ve.wait_ge(ld_w0, 7 * 16)
            ve.tensor_scalar(bks[:, :], bkc[:, :], 1.0 / DH, None, ALU.mult).then_inc(bks_ready, 1)
            ve.wait_ge(gw_ready, 1)
            mark(ve.tensor_scalar(gwc[:, 0:1], gwv[:, 0:1], 1.0 / QB, None, ALU.mult))
            mark(ve.tensor_scalar(gwc[:, 1:2], gwv[:, 1:2], 0.5 / QB, None, ALU.mult))
            then(ve.tensor_scalar(thr[:, :], gwv[:, :], EPS_Q, 0.5, ALU.add, ALU.mult))
            then(ve.tensor_scalar(nthr[:, :], thr[:, :], -1.0, None, ALU.mult))
            for m, w in enumerate((wfc_s, wpj_s)):
                w = w.rearrange("p c d -> p (c d)")
                then(ve.tensor_scalar(tern_tmp, w, nthr[:, m:m + 1], None, ALU.is_lt))
                ins = ve.scalar_tensor_tensor(out=w, in0=w, scalar=thr[:, m:m + 1], in1=tern_tmp, op0=ALU.is_gt,
                                              op1=ALU.subtract)
                ins.then_inc(tern_ready, 1)
                ve.wait_ge(tern_ready, m + 1)

            def flat(a):
                return a.rearrange("p t e -> p (t e)")

            ve.wait_ge(tanh_ready, 2)
            then(ve.tensor_scalar(flat(s_sig), flat(s_sig), 0.5, 0.5, ALU.mult, ALU.add))
            then(ve.tensor_tensor(s_sc, s_sig, eb_b[:, :].unsqueeze(1).to_broadcast([P, NT, NE]), ALU.add))
            sc_g = flat(s_sc).rearrange("p (g j) -> p g j", j=PER_G)
            mark(ve.tensor_tensor(t_hi1, sc_g[:, :, 0:4], sc_g[:, :, 4:8], ALU.max))
            then(ve.tensor_tensor(t_lo1, sc_g[:, :, 0:4], sc_g[:, :, 4:8], ALU.min))
            mark(ve.tensor_tensor(t_hi2, t_hi1[:, :, 0:2], t_hi1[:, :, 2:4], ALU.max))
            mark(ve.tensor_tensor(t_m2, t_hi1[:, :, 0:2], t_hi1[:, :, 2:4], ALU.min))
            then(ve.tensor_tensor(t_l2, t_lo1[:, :, 0:2], t_lo1[:, :, 2:4], ALU.max))
            then(ve.tensor_tensor(t_lo2, t_m2, t_l2, ALU.max))
            mark(ve.tensor_tensor(t_hi3, t_hi2[:, :, 0:1], t_hi2[:, :, 1:2], ALU.max))
            mark(ve.tensor_tensor(t_m3, t_hi2[:, :, 0:1], t_hi2[:, :, 1:2], ALU.min))
            then(ve.tensor_tensor(t_l3, t_lo2[:, :, 0:1], t_lo2[:, :, 1:2], ALU.max))
            then(ve.tensor_tensor(t_lo3, t_m3, t_l3, ALU.max))
            ve.wait_ge(consts, 1)
            then(ve.tensor_tensor(gsp[:, :, 0:GROUPS], t_hi3.rearrange("p (t g) j -> p t (g j)", t=NT),
                                  t_lo3.rearrange("p (t g) j -> p t (g j)", t=NT), ALU.add))
            for t in range(NT):
                last = mark(ve.max(mx8[:, t, :], gsp[:, t, 0:GROUPS]))
            ve.wait_ge(dve, last)
            then(ve.tensor_copy(rep8[:, :, 0:TOPG], mx8[:, :, 0:TOPG]))
            for t in range(NT):
                last = mark(ve.match_replace(gr[:, t, :], rep8[:, t, :], gsp[:, t, :], BIG))
            ve.wait_ge(dve, last)
            then(ve.tensor_scalar(gmask[:, :, :], gr[:, :, 0:GROUPS], BIG / 2, None, ALU.is_ge))
            then(ve.tensor_tensor(flat(s_masked).rearrange("p (g j) -> p g j", j=PER_G), sc_g,
                                  gmask[:, :, :].rearrange("p t g -> p (t g)").unsqueeze(2)
                                  .to_broadcast([P, NT * GROUPS, PER_G]), ALU.mult))
            then(ve.tensor_scalar(flat(s_masked), flat(s_masked), 0.0, None, ALU.add))
            for t in range(NT):
                last = mark(ve.max(mx8[:, t, :], s_masked[:, t, :]))
            ve.wait_ge(dve, last)
            for t in range(NT):
                last = mark(ve.match_replace(s_rep[:, t, :], mx8[:, t, :], s_masked[:, t, :], BIG))
            ve.wait_ge(dve, last)
            then(ve.tensor_scalar(sel16, s_rep.rearrange("p t e -> p e t"), BIG / 2, None, ALU.is_ge))
            ve.tensor_tensor_scan(cum16.rearrange("p e t -> p (e t)"), keep16.rearrange("p e t -> p (e t)"),
                                  sel16.rearrange("p e t -> p (e t)"), 0.0, ALU.mult, ALU.add).then_inc(sel_ready, 1)
            ve.wait_ge(kv_ready, 12)
            mark(ve.tensor_scalar(flat(s_sel), flat(s_rep), BIG / 2, None, ALU.is_ge))
            then(ve.scalar_tensor_tensor(out=s_w, in0=s_rep, scalar=BIG / 2, in1=s_sig, op0=ALU.is_ge, op1=ALU.mult))
            then(ve.tensor_reduce(den[:, :], s_w, AX.X, ALU.add))
            then(ve.tensor_scalar(den[:, :], den[:, :], 1e-20, None, ALU.add))
            then(ve.reciprocal(rden[:, :], den[:, :]))
            then(ve.tensor_scalar(rden[:, :], rden[:, :], ROUTE_SCALE, None, ALU.mult))
            ve.tensor_tensor(s_w, s_w, rden[:, :].unsqueeze(2).to_broadcast([P, NT, NE]), ALU.mult).then_inc(w_ready, 1)
            for j in range(2):
                ve.wait_ge(prep_ready, 10 + j)
                ve.scalar_tensor_tensor(out=wqT_lo[:, j, :], in0=bk_(4 + (9 + j) % 2)[:, 0:QKV1], scalar=WSCALE,
                                        in1=wqT_hi[:, j, :], op0=ALU.mult, op1=ALU.subtract).then_inc(prep_lo, 1)
            ve.wait_ge(pos_ps, 1)
            then(ve.tensor_copy(s_pos, two[3][:, :].rearrange("p (e t) -> p t e", t=NT)))
            mark(ve.tensor_copy(flat(pos_i), flat(s_pos)))
            then(ve.scalar_tensor_tensor(out=s_sel, in0=s_pos, scalar=float(CAP), in1=s_sel, op0=ALU.is_lt,
                                         op1=ALU.mult))
            mark(ve.tensor_scalar(flat(a_i), flat(pos_i), 4, None, ALU.logical_shift_right))
            then(ve.tensor_scalar(flat(b_i), flat(pos_i), SB - 1, None, ALU.bitwise_and))
            mark(ve.scalar_tensor_tensor(out=a16, in0=s_sel, scalar=-128.0, in1=a_i, op0=ALU.mult, op1=ALU.add))
            then(ve.tensor_copy(b16, b_i))
            tid_b = tid[:, :].unsqueeze(2).to_broadcast([P, NT, NE])
            def shared_product(c):
                ve.wait_ge(stanh_ready, c + 1)
                then(ve.scalar_tensor_tensor(out=sh_a, in0=sh_t, scalar=1.0, in1=bk_(0)[0:FF, :], op0=ALU.add, op1=ALU.mult))
                if c >= 2:
                    ve.wait_ge(sdn_ps, 2 * (c - 1))
                ve.tensor_tensor(sh_h[c % 2], sh_a, bk_(1)[0:FF, :], ALU.mult).then_inc(shT_ready, 1)

            def top(t):
                ve.wait_ge(sc_ps, t + 1)
                ve.tensor_reduce(nmax[:, t:t + 1], two[2][:, :], AX.X, ALU.max, negate=True).then_inc(nmax_ready, 1)

            def attention_step(t, step):
                if step == 1 and t + 1 < NT:
                    top(t + 1)
                elif step == 2:
                    ve.wait_ge(pT_ps, 2 * t + 2)
                    if t >= 2:
                        ve.wait_ge(o_ps, t - 1)
                    ve.tensor_copy(probT[t % 2][:, 4:8, :], bk_(0).rearrange("p (i j) -> p i j", i=4)).then_inc(pT_dve, 1)
                elif step == 3:
                    ve.wait_ge(probs_ready, t + 1)
                    then(ve.tensor_scalar(rsum[:, t:t + 1], rsum[:, t:t + 1], 2.0, None, ALU.mult))
                    then(ve.reciprocal(rinv[:, t:t + 1], rsum[:, t:t + 1]))
                elif step == 4:
                    ve.wait_ge(wo_ps, t + 1)
                    ve.scalar_tensor_tensor(out=s0[:, t, :], in0=bk_(1)[:, 0:D], scalar=rinv[:, t:t + 1], in1=bo_b[:, :],
                                            op0=ALU.mult, op1=ALU.add).then_inc(s0_ready, 1)

            ve.wait_ge(prep_ready, 11)
            ve.wait_ge(ld_sh, 4 * 16)
            then(ve.tensor_scalar(bo_b[:, :], bo_b[:, :], 0.5, None, ALU.mult))
            for a in range(SA):
                mark(ve.scalar_tensor_tensor(out=hot_a[:, :, :, a], in0=a16, scalar=float(a - 128), in1=tid_b,
                                             op0=ALU.is_equal, op1=ALU.mult))
                if a % 2:
                    shared_product(a // 2)
            early = [(t, step_) for t in range(EARLY) for step_ in range(STEPS)]
            for b in range(SB):
                ins = ve.tensor_scalar(flat(hot_b[:, b, :, :]), flat(b16), float(b), None, ALU.is_equal)
                if b == 4:
                    top(0)
                if b >= 5:
                    for t, step_ in early[2 * (b - 5):2 * (b - 5) + 2]:
                        attention_step(t, step_)
            ins.then_inc(hot_ready, 1)
            ve.wait_ge(slot_ps, 1)
            then(ve.tensor_tensor(slot_m, two[3][:, :].rearrange("p (g e) -> p g e", e=GE),
                                  diag[:, :].unsqueeze(1).to_broadcast([P, NGE * SB, GE]), ALU.mult))
            ve.tensor_reduce(slotR[:, :], slot_m, AX.X, ALU.add).then_inc(slotR_ready, 1)
            ve.wait_ge(idx_ps, 1)
            then(ve.tensor_scalar(empty[:, :], bk_(6)[:, 0:NE], 0.5, trash[:, 0:1], ALU.is_lt, ALU.mult))
            then(ve.tensor_tensor(empty[:, :], empty[:, :], bk_(6)[:, 0:NE], ALU.add))
            ve.tensor_scalar(idxE[:, :], empty[:, :], -1.0, None, ALU.add).then_inc(idxE_ready, 1)

            def put(n):
                ve.wait_ge(y_ps, n + 1)
                if n >= YS:
                    ve.wait_ge(y_added[n % 2], 16 * (n // 2 - 1))
                ve.tensor_scalar(ysb[n % YS], bk_(3)[:, 0:D], xg[n % XR][:, D + n:D + n + 1], 0.5, ALU.mult, ALU.mult)\
                    .then_inc(y_ready, 1)

            for n in range(NE):
                gu = bk_(6 + n % 2)
                ve.wait_ge(gtanh_ready, n + 1)
                then(ve.scalar_tensor_tensor(out=ea[n % 2], in0=eth[n % 2], scalar=1.0, in1=gu[0:FF, 0:CAP],
                                             op0=ALU.add, op1=ALU.mult))
                if n >= 2:
                    ve.wait_ge(y_ps, n - 1)
                ve.tensor_tensor(hT[n % 2], ea[n % 2], gu[0:FF, CAP:2 * CAP], ALU.mult).then_inc(hT_ready, 1)
                if n >= 1:
                    put(n - 1)
                if EARLY + n // STEPS < NT:
                    attention_step(EARLY + n // STEPS, n % STEPS)
            put(NE - 1)

            newton_at = [0]

            def newton(k, cols):
                v, y, t_, i_ = nv[:, cols], ny[:, cols], nt2[:, cols], ni[:, cols]
                if k:
                    ve.wait_ge(dve, newton_at[0])
                if k == 0:
                    ins = ve.tensor_scalar(i_, v.bitcast(I32), 1, None, ALU.logical_shift_right)
                elif k == 1:
                    ins = ve.tensor_scalar(y.bitcast(I32), i_, -1.0, RSQRT_SEED, ALU.mult, ALU.add)
                elif k % 3 == 2:
                    ins = ve.tensor_tensor(t_, y, y, ALU.mult)
                elif k % 3 == 0:
                    ins = ve.scalar_tensor_tensor(out=t_, in0=t_, scalar=-0.5, in1=v, op0=ALU.mult, op1=ALU.mult)
                else:
                    ins = ve.scalar_tensor_tensor(out=y, in0=t_, scalar=1.5, in1=y, op0=ALU.add, op1=ALU.mult)
                newton_at[0] = mark(ins)

            def silu(p):
                ve.wait_ge(gate_ready, p + 1)
                ve.scalar_tensor_tensor(out=tg[p % 2], in0=tg[p % 2], scalar=1.0, in1=pair(xn, p), op0=ALU.add, op1=ALU.mult)\
                    .then_inc(silu_ready, 1)

            def moments(p):
                ve.wait_ge(x1_ready, p + 1)
                for q_ in range(GT):
                    last = mark(ve.bn_stats(st1[:, q_, :], x[:, p + NP * q_, :]))
                ve.wait_ge(dve, last)
                for q_ in range(GT):
                    last = mark(ve.bn_aggr(mv1[:, q_, :], st1[:, q_, :]))
                ve.wait_ge(dve, last)
                var = mv1[:, :, 1]
                mark(ve.tensor_scalar(nv[:, 0:GT], var, EPS_LN, None, ALU.add))
                then(ve.tensor_scalar(nv[:, GT:2 * GT], var, 1.0 + EPS_Q, EPS_Q * EPS_LN, ALU.mult, ALU.add))

            row_at = [0]

            def quantise(k, p):
                xp = xq[p % 2]
                if k == 0:
                    if p >= 2:
                        ve.wait_ge(qT_ps, p - 1)
                elif k not in (1, 6):
                    ve.wait_ge(dve, row_at[0])
                if k < 2:
                    ins = ve.tensor_scalar(xp[:, k, :], x[:, p + NP * k, :], mv1[:, k, 0:1], None, ALU.subtract)
                elif k == 2:
                    ins = ve.tensor_reduce(amax[:, :], xp, AX.X, ALU.max, apply_absolute_value=True)
                elif k == 3:
                    ins = ve.reciprocal(qscale[:, :], amax[:, :])
                elif k == 4:
                    ins = ve.tensor_scalar(qscale[:, :], qscale[:, :], QB, None, ALU.mult)
                elif k < 7:
                    q_ = k - 5
                    ins = ve.tensor_scalar(xp[:, q_, :], xp[:, q_, :], qscale[:, q_:q_ + 1], QB, ALU.mult, ALU.min)
                else:
                    ve.tensor_scalar(xp, xp, -QB, None, ALU.max).then_inc(xq_ready, 1)
                    return
                row_at[0] = mark(ins)

            def scales_and_rows(p, cols):
                for k in range(NEWTON):
                    newton(k, cols)
                    if k < ROW_STEPS and p < NP:
                        quantise(k, p)
                ve.wait_ge(dve, newton_at[0])

            def product_scales(p):
                if p >= 2:
                    ve.wait_ge(qkv_ready, 2 * (p - 1))
                    ve.wait_ge(gelu_ready, GT * (p - 1))
                mark(ve.scalar_tensor_tensor(out=kvscale[p % 2][:, :], in0=amax[:, :], scalar=1.0 / (QB * WSCALE),
                                             in1=ny[:, 0:GT], op0=ALU.mult, op1=ALU.mult))
                ve.wait_ge(dve, step[0])
                ve.scalar_tensor_tensor(out=fcscale[p % 2][:, :], in0=amax[:, :], scalar=gwc[:, 0:1], in1=ny[:, GT:2 * GT],
                                        op0=ALU.mult, op1=ALU.mult).then_inc(scale_ready, 1)

            def low_q(p):
                ve.wait_ge(qT_hi_ready, p + 1)
                ve.tensor_tensor(qT_lo, bk_(0).rearrange("p (q k n) -> p q k n", q=GT, k=KH), qT_hi, ALU.subtract)\
                    .then_inc(qT_lo_ready, 1)

            def score_difference(p):
                ve.wait_ge(prod_ready, p + 1)
                ve.tensor_reduce(dif[:, :].rearrange("p (g r) -> p g r", r=REP1), pr, AX.X, ALU.add).then_inc(dif_ready, 1)

            def means(p):
                ve.wait_ge(gelu_ready, GT * p + GT)
                ve.tensor_scalar(nmean[:, :], hsum[:, :], -1.0 / FF1, None, ALU.mult).then_inc(nmean_ready, 1)

            def spreads(p):
                for q_ in range(GT):
                    ve.wait_ge(sq_ready, GT * p + q_ + 1)
                    mark(ve.tensor_reduce(nv[:, 3 * GT + q_:3 * GT + q_ + 1], sq[q_], AX.X, ALU.max))
                then(ve.tensor_scalar(nv[:, 2 * GT:3 * GT], ssq[:, :], 1.0 / FF1, EPS_Q, ALU.mult, ALU.add))

            def hidden_scales(p):
                then(ve.tensor_scalar(hscale[:, :], ny[:, 3 * GT:], QB, None, ALU.mult))
                then(ve.tensor_tensor(hbias[:, :], hscale[:, :], nmean[:, :], ALU.mult))
                then(ve.tensor_tensor(tmpc[:, :], nv[:, 3 * GT:], ny[:, 3 * GT:], ALU.mult))
                if p >= 2:
                    ve.wait_ge(ztanh_ready, GT * (p - 1))
                    ve.wait_ge(s1_ready, p - 1)
                ve.scalar_tensor_tensor(out=zhalf[p % 2][:, :], in0=tmpc[:, :], scalar=gwc[:, 1:2], in1=ny[:, 2 * GT:3 * GT],
                                        op0=ALU.mult, op1=ALU.mult).then_inc(zhalf_ready, 1)

            def quantise_hidden(p):
                rows = [hid[p % 2][:, q_, :] for q_ in range(GT)]
                for q_, h in enumerate(rows):
                    last = mark(ve.tensor_scalar(h, h, hscale[:, q_:q_ + 1], hbias[:, q_:q_ + 1], ALU.mult, ALU.add))
                ve.wait_ge(dve, last)
                for h in rows:
                    last = mark(ve.tensor_scalar(h, h, QB, -QB, ALU.min, ALU.max))
                if p:
                    ve.wait_ge(hT1_ps, GT * p)
                for q_, h in enumerate(rows):
                    ve.wait_ge(dve, last - GT + 1 + q_)
                    ve.tensor_copy(hi16[q_], h).then_inc(hi_ready, 1)

            def silu2(p):
                ve.wait_ge(ztanh_ready, GT * p + GT)
                for q_ in range(GT):
                    if p:
                        ve.wait_ge(out_ready, GT * (p - 1) + q_ + 1)
                    ve.scalar_tensor_tensor(out=zu[:, q_, :], in0=tz[:, q_, :], scalar=1.0, in1=bk_(7)[:, D * q_:D * q_ + D],
                                            op0=ALU.add, op1=ALU.mult).then_inc(zu_ready, 1)

            for p in range(3):
                silu(p)
            for p in range(2):
                moments(p)
                scales_and_rows(p, slice(0, 2 * GT))
                product_scales(p)
                low_q(p)
            for p in range(NP + 2):
                if p < NP:
                    means(p)
                if p + 2 < NP:
                    moments(p + 2)
                if p < NP:
                    score_difference(p)
                    spreads(p)
                if p >= 2:
                    silu2(p - 2)
                if p < NP:
                    scales_and_rows(p + 2, slice(0, 4 * GT))
                    hidden_scales(p)
                if p + 2 < NP:
                    product_scales(p + 2)
                    low_q(p + 2)
                if p + 3 < NP:
                    silu(p + 3)
                if p < NP:
                    quantise_hidden(p)

        @block.tensor
        def _(pe):
            pe.wait_ge(consts, 1)
            pe.wait_ge(ld_w0, 7 * 16)
            for k in range(KH):
                ins = pe.transpose(bk_(4)[:, NE * k:NE * k + NE], rw_s.rearrange("e (n k) -> e k n", k=KH)[:, k, :],
                                   ident[0:NE, 0:NE])
            ins.then_inc(rwT_ps, 1)

            def logits(t):
                pe.wait_ge(xT_ready, t + 1)
                for k in range(KH):
                    ins = pe.matmul(bk_(2 + t // 8)[:, NE * (t % 8):NE * (t % 8) + NE], xT[:, t, k, :], rwT[:, k, :],
                                    start=(k == 0), stop=(k == KH - 1))
                if t % 8 == 7:
                    ins.then_inc(logits_ps, 1)

            for t in range(NT):
                pe.wait_ge(xn_ready, t + 1)
                if t >= 2:
                    pe.wait_ge(xT_ready, t - 1)
                for k in range(KH):
                    ins = pe.transpose(bk_(t % 2)[:, P * k:P * k + P],
                                       xn[:, t, :].rearrange("p (n k) -> p k n", k=KH)[:, k, :], ident[:, :])
                ins.then_inc(xT_ps, 1)
                if t == 0:
                    pe.wait_ge(rwT_ready, 1)
                if t >= 1:
                    logits(t - 1)
            logits(NT - 1)
            pe.wait_ge(gsum_ready, 2)
            pe.matmul(bk_(7)[:, 0:2], ones[:, :], gsum[:, :], start=True, stop=True).then_inc(gw_ps, 1)
            for c in range(4):
                if c:
                    pe.wait_ge(kv_ready, 3 * c)
                for b, w in ((4, Wk_s), (5, Wv_s)):
                    for k in range(KH):
                        ins = pe.matmul(bk_(b), w[:, k, :], xT[:, 4 * c:4 * c + 4, k, :], start=(k == 0),
                                        stop=(k == KH - 1))
                    ins.then_inc(kv_ps, 1)
                for t in range(4):
                    for k in range(KH):
                        pe.matmul(bk_(6)[:, DH * t:DH * t + DH], xT[:, 4 * c + t, k, :], Wv_s[:, k, :], start=(k == 0),
                                  stop=False)
                    ins = pe.matmul(bk_(6)[:, DH * t:DH * t + DH], ones[0:1, :], bvr[0:1, :], start=False, stop=True)
                ins.then_inc(kv_ps, 1)
            pe.wait_ge(kv_ready, 12)
            for j in range(11):
                if j >= 2:
                    pe.wait_ge(prep_ready, j - 1)
                if j < 4:
                    pe.wait_ge(tern_ready, 1)
                    k, c0 = j // 2, 4 * (j % 2)
                    parts = [wfc_s[:, c0 + c, P * k:P * k + P] for c in range(4)]
                elif j < 8:
                    pe.wait_ge(tern_ready, 2)
                    parts = [wpj_s[:, c, P * k:P * k + P] for k in (2 * (j - 4), 2 * (j - 4) + 1) for c in range(2)]
                elif j == 8:
                    pe.wait_ge(ld_w2, 32)
                    parts = [wpo_s[:, c, P * k:P * k + P] for k in range(2) for c in range(2)]
                else:
                    parts = [wqkv_s[:, c, P * (j - 9):P * (j - 9) + P] for c in range(3)]
                for i, part in enumerate(parts):
                    ins = pe.transpose(bk_(4 + j % 2)[:, P * i:P * i + P], part, ident[:, :])
                ins.then_inc(prep_ps, 1)
            pe.wait_ge(sel_ready, 1)
            for h in range(2):
                es = slice(32 * h, 32 * h + 32)
                pe.matmul(bk_(6 + h), before16[:, :], sel16[:, es, :].rearrange("p e t -> p (e t)"), start=True, stop=False)
                ins = pe.matmul(bk_(6 + h), ones16[:, :], cum16[:, es, :].rearrange("p e t -> p (e t)"), start=False,
                                stop=True)
            ins.then_inc(pos_ps, 1)
            pe.wait_ge(ld_sh, 4 * 16)

            def shared_up(c):
                if c:
                    pe.wait_ge(shT_ready, c)
                for m in range(2):
                    for k in range(KH):
                        ins = pe.matmul(bk_(m)[0:FF, :], sgu[:, m, k, :], xT[:, SC * c:SC * c + SC, k, :], start=(k == 0),
                                        stop=(k == KH - 1))
                ins.then_inc(sgu_ps, 1)

            def shared_down(c):
                pe.wait_ge(shT_ready, c + 1)
                for j in range(2):
                    if c:
                        pe.wait_ge(sy_ready, 2 * (c - 1) + j + 1)
                    for i in range(2):
                        at = P * (2 * j + i)
                        ins = pe.matmul(bk_(2 + j)[:, D * i:D * i + D], sh_h[c % 2][:, at:at + P], sdn[:, :], start=True,
                                        stop=True)
                    ins.then_inc(sdn_ps, 1)

            for c in range(NT // SC):
                shared_up(c)
                if c:
                    shared_down(c - 1)
            shared_down(NT // SC - 1)

            def score(t):
                if t:
                    pe.wait_ge(probs_ready, t)
                for h in range(2):
                    at = (t // 8) * SEQ + 512 * h
                    ins = pe.matmul(two[2][:, 512 * h:512 * h + 512], vT[:, P * t:P * t + P], kT[:, at:at + 512],
                                    start=True, stop=True)
                ins.then_inc(sc_ps, 1)

            def turn_probs(t, h):
                pe.wait_ge(probs_ready, t + 1)
                if h:
                    pe.wait_ge(pT_act, t + 1)
                elif t:
                    pe.wait_ge(pT_dve, t)
                for i in range(4):
                    ins = pe.transpose(bk_(0)[:, P * i:P * i + P], probs[t % 2][:, 512 * h + P * i:512 * h + P * i + P],
                                       ident[:, :])
                ins.then_inc(pT_ps, 1)

            def attention_step(t, step):
                if step == 0:
                    turn_probs(t, 0)
                elif step == 1 and t + 1 < NT:
                    score(t + 1)
                elif step == 2:
                    turn_probs(t, 1)
                elif step == 3:
                    pe.wait_ge(pT_act, t + 1)
                    pe.wait_ge(pT_dve, t + 1)
                    if t:
                        pe.wait_ge(s0_ready, t)
                    for i in range(8):
                        ins = pe.matmul(bk_(1)[:, 0:P], v[:, (t // 8) * 8 + i, :], probT[t % 2][:, i, :], start=(i == 0),
                                        stop=(i == 7))
                    ins.then_inc(o_ps, 1)
                elif step == 4:
                    pe.wait_ge(oT_ready, t + 1)
                    pe.matmul(bk_(1)[:, 0:D], oT[t % 2], WoS[:, :], start=True, stop=True).then_inc(wo_ps, 1)

            score(0)
            for t in range(EARLY):
                for step_ in range(STEPS):
                    attention_step(t, step_)

            pe.wait_ge(hot_ready, 1)
            for g in range(NGE):
                es = slice(GE * g, GE * g + GE)
                for t in range(NT):
                    ins = pe.matmul(two[3][:, 256 * g:256 * g + 256],
                                    hot_a[:, t, es, :].rearrange("p e a -> p (e a)"), hot_b[:, :, t, es],
                                    start=(t == 0), stop=(t == NT - 1))
            ins.then_inc(slot_ps, 1)
            pe.wait_ge(slot_in, 16)
            pe.wait_ge(slotR_ready, 1)
            pe.transpose(bk_(6)[:, 0:NE], slotE[:, :], ident[0:NE, 0:NE]).then_inc(idx_ps, 1)

            def turn(n):
                pe.wait_ge(xg_ld[n % XR], 16 * (n // XR + 1))
                if n:
                    pe.wait_ge(xgT_ready, n)
                for k in range(KH):
                    ins = pe.transpose(bk_(2)[:, P * k:P * k + P],
                                       xg[n % XR][:, 0:D].rearrange("p (n k) -> p k n", k=KH)[:, k, :], ident[:, :])
                ins.then_inc(xgT_ps, 1)

            def up(n):
                pe.wait_ge(xgT_ready, n + 1)
                r = (n // WG) % WR
                pe.wait_ge(ld_e[r], 48 * (n // WG // WR + 1))
                if n >= 2:
                    pe.wait_ge(hT_ready, n - 1)
                for m in range(2):
                    for k in range(KH):
                        ins = pe.matmul(bk_(6 + n % 2)[0:FF, CAP * m:CAP * m + CAP], wgu[r][:, n % WG, m, k, :],
                                        xgT[n % 2][:, k, :], start=(k == 0), stop=(k == KH - 1))
                ins.then_inc(gu_ps, 1)

            def down(n):
                pe.wait_ge(hT_ready, n + 1)
                if n:
                    pe.wait_ge(y_ready, n)
                pe.matmul(bk_(3)[:, 0:D], hT[n % 2], wdn[(n // WG) % WR][:, n % WG, :], start=True, stop=True)\
                    .then_inc(y_ps, 1)

            pe.wait_ge(sy_ready, NT // 2)
            pe.wait_ge(idxE_ready, 1)
            turn(0)
            for n in range(NE):
                if n + 1 < NE:
                    turn(n + 1)
                up(n)
                if EARLY + n // STEPS < NT:
                    attention_step(EARLY + n // STEPS, n % STEPS)
                if n >= 1:
                    down(n - 1)
            down(NE - 1)

            def turn_q(p):
                pe.wait_ge(xq_ready, p + 1)
                if p:
                    pe.wait_ge(qT_lo_ready, p)
                for q_ in range(GT):
                    for k in range(KH):
                        ins = pe.transpose(bk_(0)[:, D * q_ + P * k:D * q_ + P * k + P], xq[p % 2][:, q_, P * k:P * k + P],
                                           ident[:, :])
                ins.then_inc(qT_ps, 1)

            def qkv(p):
                pe.wait_ge(qT_lo_ready, p + 1)
                if p:
                    pe.wait_ge(qkv_ready, 2 * p)
                for q_, cols, width in ((1, slice(0, QKV1), GS1), (0, slice(QKV1, 512), 2 * HD1)):
                    i = 0
                    for k in range(KH):
                        for part, w in ((qT_hi, wqT_hi), (qT_lo, wqT_hi), (qT_hi, wqT_lo)):
                            rhs = w[:, k, :].rearrange("p (g c) -> p g c", c=GS1)[:, :, GS1 - width:GS1]
                            ins = pe.matmul(bk_(1)[:, cols], part[:, q_, k, :], rhs, start=(i == 0), stop=(i == 5))
                            i += 1
                ins.then_inc(qkv_ps, 1)

            def fc(n):
                if n:
                    pe.wait_ge(gelu_ready, n)
                for h in range(2):
                    for i, (k, part) in enumerate((k, part) for k in range(KH) for part in (qT_hi, qT_lo)):
                        ins = pe.matmul(bk_(2 + h), part[:, n % GT, k, :], wfcT[:, k, 512 * h:512 * h + 512],
                                        start=(i == 0), stop=(i == 3))
                ins.then_inc(fc_ps, 1)

            def turn_att(p):
                pe.wait_ge(att0_ready, p + 1)
                pe.wait_ge(att_ready, p + 1)
                if p:
                    pe.wait_ge(s1_ready, p)
                for s_ in range(2):
                    for k in range(KH):
                        ins = pe.transpose(bk_(6)[:, D * s_ + P * k:D * s_ + P * k + P], att[:, s_, P * k:P * k + P],
                                           ident[:, :])
                ins.then_inc(attT_ps, 1)

            def project(p):
                pe.wait_ge(attT_ready, p + 1)
                for s_ in range(2):
                    for k in range(KH):
                        ins = pe.matmul(bk_(6)[:, D * s_:D * s_ + D], attT[:, s_, k, :], wpoT[:, k, :],
                                        start=(k == 0), stop=(k == KH - 1))
                ins.then_inc(s1_ps, 1)

            def turn_hidden(n):
                pe.wait_ge(lo_ready, n + 1)
                if n:
                    pe.wait_ge(hT1_ready, 2 * n)
                for b, part in ((4, hi16), (5, lo16)):
                    for k in range(FF1 // P):
                        ins = pe.transpose(bk_(b).bitcast(F16)[:, P * k:P * k + P], part[n % GT][:, P * k:P * k + P],
                                           ident16[:, :])
                ins.then_inc(hT1_ps, 1)

            def down1(n):
                pe.wait_ge(hT1_ready, 2 * n + 2)
                if n >= GT:
                    pe.wait_ge(zu_ready, n // GT * GT)
                i = 0
                for k in range(FF1 // P):
                    for part in (hiT, loT):
                        ins = pe.matmul(bk_(7)[:, D * (n % GT):D * (n % GT) + D], part[n % 2][:, P * k:P * k + P],
                                        wpjT[:, k, :], start=(i == 0), stop=(i == 2 * FF1 // P - 1))
                        i += 1
                ins.then_inc(z_ps, 1)

            pe.wait_ge(y_ready, NE)
            pe.wait_ge(s0_ready, NT)
            turn_q(0)
            qkv(0)
            for q_ in range(GT):
                fc(q_)
            turn_q(1)
            for p in range(NP + 2):
                if p + 1 < NP:
                    qkv(p + 1)
                    for q_ in range(GT):
                        fc(GT * (p + 1) + q_)
                if p + 2 < NP:
                    turn_q(p + 2)
                if 1 <= p <= NP:
                    turn_hidden(GT * (p - 1))
                if p < NP:
                    turn_att(p)
                if 1 <= p <= NP:
                    turn_hidden(GT * (p - 1) + 1)
                if p < NP:
                    project(p)
                if 1 <= p <= NP:
                    for q_ in range(GT):
                        down1(GT * (p - 1) + q_)


_INS = ["L0_attn_q", "L0_attn_Wk", "L0_attn_bk", "L0_attn_Wv", "L0_attn_bv", "L0_attn_Wo", "L0_attn_bo",
        "L0_ffn_router_weight", "L0_ffn_e_bias", "L0_ffn_w_gate", "L0_ffn_w_up", "L0_ffn_w_down", "L0_ffn_sh_gate",
        "L0_ffn_sh_up", "L0_ffn_sh_down", "L1_attn_weight_qkv", "L1_attn_weight_proj", "L1_ffn_w_fc", "L1_ffn_w_proj"]


def kernel(**inputs):
    import numpy as _np
    import concourse.bacc as _bacc
    from concourse import mybir as _mybir
    from concourse.bass_utils import run_bass_kernel_spmd as _run

    nc = _bacc.Bacc("TRN2", target_bir_lowering=False, num_devices=1)
    arrays, args = {}, []
    for name in _INS:
        a = _np.ascontiguousarray(inputs[name])
        arrays[f"in_{name}"] = a
        args.append(nc.dram_tensor(f"in_{name}", a.shape, _mybir.dt.from_np(a.dtype), kind="ExternalInput").ap())
    out = nc.dram_tensor("out_0", (BATCH, SEQ, D), F32, kind="ExternalOutput").ap()
    build(nc, *args, out)
    r = _run(nc, [arrays], core_ids=[0])
    return r.results[0]["out_0"]
```

```python
from contextlib import ExitStack

import concourse.bass as bass
from concourse import mybir

F32 = mybir.dt.float32
F16 = mybir.dt.float16
I32 = mybir.dt.int32
ACT = mybir.ActivationFunctionType
ALU = mybir.AluOpType
AX = mybir.AxisListType

P = 128
BATCH, SEQ, D = 2, 1024, 256
NTOK = BATCH * SEQ
NT = NTOK // P
KH = D // P
HQ, DH = 16, 128
NE, FF, TOPK, GROUPS, TOPG = 64, 88, 8, 8, 4
PER_G = NE // GROUPS
CAP = 128
ROUTE_SCALE = 2.5
NH1, NKV1, HD1 = 16, 4, 16
REP1 = NH1 // NKV1
GS1 = (REP1 + 2) * HD1
QKV1 = NKV1 * GS1
FF1 = 4 * D
QB = 128.0
EPS_LN, EPS_Q = 1e-5, 1e-6

SA, SB = 8, 16
GE = 16
NGE = NE // GE
BIG, SENTINEL = 3.0e38, -3.0e38
XR = 8
WG = 2
WR = 5
YS = 4
EARLY = 1
LATE = 4
STEPS = 4
BESIDE = (NT - EARLY - LATE) * STEPS
POOL_T0 = 10
SUM_AT, TERN_AT = 18, (22, 30, 38, 46)
SC = 4
NP = NT // 2
GT = 2
PREP = 11
ORDER = [p + NP * i for p in range(NP) for i in range(2)]


def beside(n):
    done, now = n * BESIDE // NE, (n + 1) * BESIDE // NE
    return (EARLY + done // STEPS, done % STEPS) if now > done else None


GATE_AT = (4, 6, 8)
MOMENTS_AT = (13, 15)
LATE_STEPS = [(i, step) for i in range(NT - LATE, NT) for step in range(STEPS)]
NEWTON, ROW_STEPS = 11, 8
RSQRT_SEED = 1597463007.0
WSCALE = 256.0


def build(nc, q, Wk, bk, Wv, bv, Wo, bo, rw, eb, wg, wu, wd, sg, su, sd, wqkv, wpo, wfc, wpj, out):
    x_v = q.rearrange("b (t p) d -> p (b t) d", p=P)
    out_v = out.rearrange("b (t p) d -> p (b t) d", p=P)
    tok_d = nc.dram_tensor("tok_d", (NTOK + P, D + NE), F32, kind="Internal").ap()
    acc_d = [nc.dram_tensor(f"acc_d{i}", (NTOK + P, D), F32, kind="Internal").ap() for i in range(2)]
    slot_d = nc.dram_tensor("slot_d", (NE * CAP,), F32, kind="Internal").ap()
    tok_v = tok_d.rearrange("(t p) d -> p t d", p=P)
    acc_v = [a.rearrange("(t p) d -> p t d", p=P) for a in acc_d]

    with ExitStack() as ctx:
        def sb(name, shape, dt=F32):
            return ctx.enter_context(nc.sbuf_tensor(name, shape, dt))

        def sem(name):
            return ctx.enter_context(nc.semaphore(name))

        two = [ctx.enter_context(nc.psum_tensor(f"two{i}", [P, 1024], F32)) for i in range(4)]

        def bk_(i):
            return two[i // 2][:, (i % 2) * 512:(i % 2) * 512 + 512]

        x = sb("x", [P, NT, D])
        xn = sb("xn", [P, NT, D])
        kT = sb("kT", [P, NTOK])
        vT = sb("vT", [P, NTOK])
        v = sb("v", [P, NT, DH])
        wfcT = sb("wfcT", [P, KH, FF1], F16)
        wpjT = sb("wpjT", [P, FF1 // P, D], F16)
        wqT_hi = sb("wqT_hi", [P, KH, QKV1], F16)
        wqT_lo = sb("wqT_lo", [P, KH, QKV1], F16)
        wpoT = sb("wpoT", [P, KH, D])
        WoS = sb("WoS", [P, D])
        rwT = sb("rwT", [P, KH, NE])
        sgu = sb("sgu", [P, 2, KH, FF])
        sdn = sb("sdn", [FF, D])
        bkc = sb("bkc", [P, 1])
        bks = sb("bks", [P, 1])
        bvc = sb("bvc", [P, 1])
        bo_b = sb("bo_b", [P, D])
        eb_b = sb("eb_b", [P, NE])
        ident = sb("ident", [P, P])
        ident16 = sb("ident16", [P, P], F16)
        ones = sb("ones", [P, P])
        ones16 = sb("ones16", [P, P], F16)
        before16 = sb("before16", [P, P], F16)
        tid_i = sb("tid_i", [P, NT], I32)
        tid = sb("tid", [P, NT])
        trash_i = sb("trash_i", [P, 1], I32)
        trash = sb("trash", [P, 1])
        diag = sb("diag", [P, GE])
        st = sb("st", [P, NT, 6])
        mv = sb("mv", [P, NT, 2])
        rstd = sb("rstd", [P, NT])
        gsum = sb("gsum", [P, 2])
        gwv = sb("gwv", [P, 2])
        thr = sb("thr", [P, 2])
        nthr = sb("nthr", [P, 2])
        gsp = sb("gsp", [P, NT, 12])
        gr = sb("gr", [P, NT, 12])
        mx8 = sb("mx8", [P, NT, 8])
        rep8 = sb("rep8", [P, NT, 8])
        gmask = sb("gmask", [P, NT, GROUPS])
        den = sb("den", [P, NT])
        rden = sb("rden", [P, NT])
        empty = sb("empty", [P, NE])
        slotR = sb("slotR", [P, NGE * SB])
        slotE = sb("slotE", [NE, CAP])
        idxE = sb("idxE", [P, NE], I32)
        nmax = sb("nmax", [P, NT])
        rsum = sb("rsum", [P, NT])
        rinv = sb("rinv", [P, NT])

        A = sb("A", [P, 8192])
        xT = A[:, 0:4096].rearrange("p (t k n) -> p t k n", t=NT, k=KH)
        Wo_s = A[:, 4096:8192].rearrange("p (h n) -> p h n", h=HQ)
        sh_t, sh_a = A[0:FF, 6144:6656], A[0:FF, 6656:7168]
        sh_h = [A[0:FF, 7168 + 512 * i:7680 + 512 * i] for i in range(2)]
        probs = [A[:, 1024 * i:1024 * i + 1024] for i in range(2)]
        probT = [A[:, 2048 + 1024 * i:3072 + 1024 * i].rearrange("p (i j) -> p i j", i=8) for i in range(2)]
        s0 = A[:, 4096:8192].rearrange("p (t d) -> p t d", t=NT)

        F = sb("F", [P, 15104])
        def f_te(i):
            return F[:, 1024 * i:1024 * i + 1024].rearrange("p (t e) -> p t e", t=NT)
        s_sig, s_sc, s_masked, s_rep, s_sel, s_w = f_te(0), f_te(1), f_te(4), f_te(5), f_te(6), f_te(7)
        t_hi1 = F[:, 2048:2560].rearrange("p (g j) -> p g j", j=4)
        t_lo1 = F[:, 2560:3072].rearrange("p (g j) -> p g j", j=4)
        t_hi2, t_m2, t_l2, t_lo2 = [F[:, 3072 + 256 * i:3328 + 256 * i].rearrange("p (g j) -> p g j", j=2)
                                    for i in range(4)]
        t_hi3, t_m3, t_l3, t_lo3 = [F[:, 4096 + 128 * i:4224 + 128 * i].rearrange("p (g j) -> p g j", j=1)
                                    for i in range(4)]
        place_i, b_i, a_i = f_te(2).bitcast(I32), f_te(3).bitcast(I32), f_te(4).bitcast(I32)
        rw_s = F[0:NE, 5120:5120 + D]
        Wk_s, Wv_s = [F[:, 6144 + 256 * i:6400 + 256 * i].rearrange("p (k n) -> p k n", k=KH) for i in range(2)]
        H = F[:, 8192:10752].bitcast(F16)
        sel16 = H[:, 0:1024].rearrange("p (e t) -> p e t", t=NT)
        cum16 = H[:, 1024:2048].rearrange("p (e t) -> p e t", t=NT)
        keep16 = H[:, 2048:3072].rearrange("p (e t) -> p e t", t=NT)
        a16 = H[:, 3072:4096].rearrange("p (t e) -> p t e", t=NT)
        b16 = H[:, 4096:5120].rearrange("p (t e) -> p t e", t=NT)
        slot_m = F[:, 0:1024].rearrange("p (g e) -> p g e", e=GE)
        hot_a = F[:, 10752:14848].bitcast(F16).rearrange("p (t e a) -> p t e a", t=NT, a=SA)
        wfc_s = F[:, 0:2048].rearrange("p (c d) -> p c d", c=FF1 // P)
        wpj_s = F[:, 2048:4096].rearrange("p (c d) -> p c d", c=KH)
        wqkv_s = F[:, 4096:4864].rearrange("p (c d) -> p c d", c=QKV1 // P)
        wpo_s = F[:, 4864:5376].rearrange("p (c d) -> p c d", c=KH)
        tern_tmp = F[:, 8704:10752]
        acc1 = F[:, 10752:14848].rearrange("p (t d) -> p t d", t=NT)
        oT = [F[:, 14848 + 128 * i:14976 + 128 * i] for i in range(2)]

        at = [0]

        def l1(n):
            at[0] += n
            assert at[0] <= 10752, at
            return F[:, at[0] - n:at[0]]
        hiT = [l1(512).bitcast(F16) for _ in range(2)]
        loT = [l1(512).bitcast(F16) for _ in range(2)]
        hi16 = [l1(512).bitcast(F16) for _ in range(GT)]
        lo16 = [l1(512).bitcast(F16) for _ in range(GT)]
        xq = [l1(GT * D).rearrange("p (q d) -> p q d", q=GT) for _ in range(2)]
        qT_hi = l1(GT * D // 2).bitcast(F16).rearrange("p (q k n) -> p q k n", q=GT, k=KH)
        qT_lo = l1(GT * D // 2).bitcast(F16).rearrange("p (q k n) -> p q k n", q=GT, k=KH)
        s1 = [l1(GT * D).rearrange("p (q d) -> p q d", q=GT) for _ in range(2)]
        qkv1 = [l1(QKV1).rearrange("p (g c) -> p g c", c=GS1) for _ in range(2)]
        kv0 = [l1(NKV1 * 2 * HD1).rearrange("p (g c) -> p g c", c=2 * HD1) for _ in range(2)]
        pr = l1(D).rearrange("p (g r d) -> p g r d", r=REP1, d=HD1)
        dk, dv, hv, mid = [l1(NKV1 * HD1).rearrange("p (g d) -> p g d", d=HD1) for _ in range(4)]
        att = l1(GT * D).rearrange("p (s n) -> p s n", s=2)
        tg = [l1(GT * D).rearrange("p (s d) -> p s d", s=2) for _ in range(2)]
        tz = l1(GT * D).rearrange("p (q d) -> p q d", q=GT)
        zu = l1(GT * D).rearrange("p (q d) -> p q d", q=GT)

        W = sb("W", [P, 8192])
        hot_b = W[:, :].bitcast(F16).rearrange("p (b t e) -> p b t e", b=SB, t=NT)
        ring = [W[:, 1216 * r:1216 * r + 1216] for r in range(3)] + [F[:, 5376 + 1216 * r:6592 + 1216 * r] for r in range(2)]
        wgu = [w[:, 0:704].rearrange("p (e m k f) -> p e m k f", e=WG, m=2, k=KH) for w in ring]
        wdn = [w[0:FF, 704:1216].rearrange("p (e n) -> p e n", e=WG) for w in ring]
        xg = [W[:, 3648 + 320 * r:3968 + 320 * r] for r in range(7)] + [F[:, 7808:8128]]
        xgT = [W[:, 5888 + 256 * r:6144 + 256 * r].rearrange("p (k n) -> p k n", k=KH) for r in range(2)]
        hT = [W[0:FF, 6400 + 128 * r:6528 + 128 * r] for r in range(2)]
        eth = [W[:, 6656 + 128 * r:6656 + 128 * r + FF] for r in range(2)]
        h = [W[:, 6912 + 128 * r:6912 + 128 * r + FF] for r in range(2)]
        gu = [bk_(6 + r)[:, 0:2 * FF] for r in range(2)]
        hT_bank = [bk_(6 + r)[0:FF, 256:256 + CAP] for r in range(2)]
        ysb = [W[:, 7168 + 256 * r:7424 + 256 * r] for r in range(YS)]
        hid = [W[:, 2048 * i:2048 * i + 2048].rearrange("p (q f) -> p q f", q=GT) for i in range(2)]
        sq = [W[:, 4096 + FF1 * i:4096 + FF1 * i + FF1] for i in range(GT)]
        attT = W[:, 6144:6144 + GT * D].rearrange("p (s k n) -> p s k n", s=2, k=KH)
        st1 = sb("st1", [P, GT, 6])
        mv1 = sb("mv1", [P, GT, 2])
        amax, qscale, hsum, nmean, ssq, hscale, hbias, tmpc = [
            sb(n, [P, GT]) for n in ("amax", "qscale", "hsum", "nmean", "ssq", "hscale", "hbias", "tmpc")]
        kvscale, fcscale, zhalf = [[sb(f"{n}{i}", [P, GT]) for i in range(2)] for n in ("kvscale", "fcscale", "zhalf")]
        gwc = sb("gwc", [P, 2])
        nv, ny, nt2 = [sb(n, [P, 4 * GT]) for n in ("nv", "ny", "nt2")]
        ni = sb("ni", [P, 4 * GT], I32)
        dif, td = [sb(n, [P, NH1]) for n in ("dif", "td")]

        ld_x = [sem(f"ld_x{c}") for c in range(4)]
        ld_w0 = sem("ld_w0")
        ld_w1 = sem("ld_w1")
        ld_wo = sem("ld_wo")
        ld_w2 = sem("ld_w2")
        ld_sh = sem("ld_sh")
        ld_e = [sem(f"ld_e{r}") for r in range(WR)]
        consts = sem("consts")
        pool_seq = sem("pool_seq")
        wos_done = sem("wos_done")
        dve = sem("dve_seq")
        ln1_var, ln1_std, xn_ready, xn_stored, w_ready, w_stored = [sem(n) for n in (
            "ln1_var", "ln1_std", "xn_ready", "xn_stored", "w_ready", "w_stored")]
        rwT_ps, rwT_ready, xT_ps, xT_ready, logits_ps, tanh_ready, bks_ready = [sem(n) for n in (
            "rwT_ps", "rwT_ready", "xT_ps", "xT_ready", "logits_ps", "tanh_ready", "bks_ready")]
        kv_ps, kv_ready, vt_ps, v_ready, gsum_ready, gw_ps, gw_ready, tern_ready, prep_ps, prep_ready, prep_lo = [sem(n) for n in (
            "kv_ps", "kv_ready", "vt_ps", "v_ready", "gsum_ready", "gw_ps", "gw_ready", "tern_ready", "prep_ps", "prep_ready", "prep_lo")]
        sel_ready, pos_ps, hot_a_ready, tid_ready, hot_ready, slot_ps, slotR_ready, slot_out, slot_in, idx_ps, idxE_ready = [
            sem(n) for n in ("sel_ready", "pos_ps", "hot_a_ready", "tid_ready", "hot_ready", "slot_ps", "slotR_ready", "slot_out", "slot_in",
                             "idx_ps", "idxE_ready")]
        sgu_ps, stanh_ready, shT_ready, sdn_ps, sy_ready, acc_init = [sem(n) for n in (
            "sgu_ps", "stanh_ready", "shT_ready", "sdn_ps", "sy_ready", "acc_init")]
        xg_ld = [sem(f"xg_ld{r}") for r in range(XR)]
        xgT_ps, xgT_ready, gu_ps, gtanh_ready, h_ready, hT_ps, hT_ready, y_ps, y_ready = [sem(n) for n in (
            "xgT_ps", "xgT_ready", "gu_ps", "gtanh_ready", "h_ready", "hT_ps", "hT_ready", "y_ps", "y_ready")]
        y_added = [sem(f"y_added{i}") for i in range(2)]
        acc_ld = [sem(f"acc_ld{i}") for i in range(NP)]
        sc_ps, nmax_ready, probs_ready, pT_ps, pT_act, pT_dve, o_ps, oT_ready, wo_ps, s0_ready = [sem(n) for n in (
            "sc_ps", "nmax_ready", "probs_ready", "pT_ps", "pT_act", "pT_dve", "o_ps", "oT_ready", "wo_ps", "s0_ready")]
        acc_ready, gate_ready, silu_ready, x1_ready, xq_ready, qT_ps, qT_hi_ready, qT_lo_ready = [sem(n) for n in (
            "acc_ready", "gate_ready", "silu_ready", "x1_ready", "xq_ready", "qT_ps", "qT_hi_ready", "qT_lo_ready")]
        scale_ready, qkv_ps, qkv_ready, prod_ready, dif_ready, td_ready, att0_ready, att_ready, attT_ps, attT_ready, s1_ps, s1_ready = [
            sem(n) for n in ("scale_ready", "qkv_ps", "qkv_ready", "prod_ready", "dif_ready", "td_ready", "att0_ready",
                             "att_ready", "attT_ps",
                             "attT_ready", "s1_ps", "s1_ready")]
        fc_ps, gelu_ready, nmean_ready, sq_ready, zhalf_ready, hi_ready, lo_ready, hT1_ps, hT1_ready = [
            sem(n) for n in ("fc_ps", "gelu_ready", "nmean_ready", "sq_ready", "zhalf_ready",
                             "hi_ready", "lo_ready", "hT1_ps", "hT1_ready")]
        z_ps, ztanh_ready, zu_ready, out_ready, out_stored = [sem(n) for n in (
            "z_ps", "ztanh_ready", "zu_ready", "out_ready", "out_stored")]

        def pair(a, p):
            return a.rearrange("p (s i) d -> p s i d", s=2)[:, :, p, :]

        def heads(a):
            return a.unsqueeze(2).to_broadcast([P, NKV1, REP1, HD1])

        att_h = [att[:, s_, :].rearrange("p (g r d) -> p g r d", r=REP1, d=HD1) for s_ in range(2)]

        block = ctx.enter_context(nc.Block())

        @block.sync
        def _(sp):
            for c in range(4):
                sp.dma_start(x[:, 4 * c:4 * c + 4, :], x_v[:, 4 * c:4 * c + 4, :]).then_inc(ld_x[c], 16)
            sp.dma_start(rw_s, rw).then_inc(ld_w0, 16)
            sp.dma_start(eb_b[:, :], eb.rearrange("(a n) -> a n", a=1).to_broadcast([P, NE])).then_inc(ld_w0, 16)
            for dst, src in ((Wk_s, Wk), (Wv_s, Wv)):
                sp.dma_start(dst[:, :, :], src.rearrange("(p k) n -> p k n", k=KH)).then_inc(ld_w0, 16)
            for dst, src in ((bkc, bk), (bvc, bv)):
                sp.dma_start(dst[:, :], src.rearrange("(p a) -> p a", a=1)).then_inc(ld_w0, 16)
            sp.dma_start(Wo_s, Wo.rearrange("(h p) n -> p h n", p=P)).then_inc(ld_wo, 16)
            for m, src in enumerate((sg, su)):
                sp.dma_start(sgu[:, m, :, :], src.rearrange("(p k) f -> p k f", k=KH)).then_inc(ld_sh, 16)
            sp.dma_start(sdn[:, :], sd).then_inc(ld_sh, 16)
            sp.dma_start(bo_b[:, :], bo.rearrange("(a n) -> a n", a=1).to_broadcast([P, D])).then_inc(ld_sh, 16)
            for c in range(4):
                sp.wait_ge(xn_ready, 4 * c + 4)
                sp.dma_start(tok_v[:, 4 * c:4 * c + 4, 0:D], xn[:, 4 * c:4 * c + 4, :]).then_inc(xn_stored, 16)
            sp.wait_ge(xn_ready, NT)
            sp.dma_start(tok_d[NTOK:NTOK + P, 0:D], xn[:, 0, :]).then_inc(xn_stored, 16)
            sp.wait_ge(w_ready, 1)
            sp.dma_start(tok_v[:, 0:NT, D:D + NE], s_w).then_inc(w_stored, 16)
            sp.dma_start(tok_d[NTOK:NTOK + P, D:D + NE], s_w[:, 0, :]).then_inc(w_stored, 16)
            def load_experts(g):
                r, e = g % WR, g * WG
                for m, src in enumerate((wg, wu)):
                    sp.dma_start(wgu[r][:, :, m, :, :].rearrange("p e k f -> p e (k f)"),
                                 src[e:e + WG].rearrange("e (p k) f -> p e (k f)", k=KH)).then_inc(ld_e[r], 16)
                sp.dma_start(wdn[r], wd[e:e + WG].rearrange("e f n -> f e n")).then_inc(ld_e[r], 16)

            sp.wait_ge(slot_ps, 1)
            load_experts(0)
            sp.wait_ge(slotR_ready, 1)
            sp.dma_start(slot_d.rearrange("(g p b) -> p g b", p=P, b=SB),
                         slotR[:, :].rearrange("p (g b) -> p g b", b=SB)).then_inc(slot_out, 16)
            sp.wait_ge(slot_out, 16)
            sp.dma_start(slotE[:, :], slot_d.rearrange("(e s) -> e s", s=CAP)).then_inc(slot_in, 16)
            sp.wait_ge(w_stored, 32)
            for g in range(1, WR):
                load_experts(g)
            for g in range(WR, NE // WG):
                sp.wait_ge(y_ps, WG * (g - WR + 1))
                load_experts(g)
                if 1 <= g - WR <= 4:
                    m, c = divmod(g - WR - 1, 2)
                    cs = slice((4, 1)[m] * c, (4, 1)[m] * (c + 1))
                    sp.dma_start((wfc_s, wpj_s)[m][:, cs, :],
                                 (wfc, wpj)[m].rearrange("(c p) d -> p c d", p=P)[:, cs, :]).then_inc(ld_w1, 16)
                if g - WR == 5:
                    sp.dma_start(wqkv_s, wqkv.rearrange("(c p) d -> p c d", p=P)).then_inc(ld_w2, 16)
                    sp.dma_start(wpo_s, wpo.rearrange("(c p) d -> p c d", p=P)).then_inc(ld_w2, 16)
            for i in range(2):
                sp.wait_ge(y_added[i], 16 * (NE // 2))
            for p in range(NP):
                for a, dst in zip(acc_v, (xn, acc1)):
                    sp.dma_start(pair(dst, p), a[:, 0:NT, :].rearrange("p (s i) d -> p s i d", s=2)[:, :, p, :])\
                        .then_inc(acc_ld[p], 16)
            for p in range(NP):
                for q_ in range(GT):
                    t = p + NP * q_
                    sp.wait_ge(out_ready, GT * p + q_ + 1)
                    sp.dma_start(out_v[:, t, :], x[:, t, :]).then_inc(out_stored, 16)
            sp.wait_ge(out_stored, 16 * NT)

        @block.gpsimd
        def _(pool):
            step = [0]

            def then(ins):
                step[0] += 1
                ins.then_inc(pool_seq, 1)
                pool.wait_ge(pool_seq, step[0])

            then(pool.memset(ident[:, :], 0.0))
            then(pool.affine_select(out=ident[:, :], in_=ident[:, :], compare_op=ALU.not_equal, fill=1.0,
                                    base=0, pattern=[[-1, P]], channel_multiplier=1))
            then(pool.tensor_copy(ident16[:, :], ident[:, :]))
            then(pool.memset(ones[:, :], 1.0))
            then(pool.memset(ones16[:, :], 1.0))
            then(pool.memset(before16[:, :], 0.0))
            then(pool.affine_select(out=before16[:, :], in_=before16[:, :], compare_op=ALU.is_gt, fill=-1.0,
                                    base=0, pattern=[[1, P]], channel_multiplier=-1))
            then(pool.iota(tid_i[:, :], [[P, NT]], base=1, channel_multiplier=1))
            then(pool.tensor_copy(tid[:, :], tid_i[:, :]))
            then(pool.iota(trash_i[:, :], [[0, 1]], base=NTOK + 1, channel_multiplier=1))
            then(pool.tensor_copy(trash[:, :], trash_i[:, :]))
            then(pool.affine_select(out=diag[:, :], in_=ones[:, 0:GE], compare_op=ALU.is_ge, fill=0.0,
                                    base=0, pattern=[[-SA, GE]], channel_multiplier=1))
            then(pool.affine_select(out=diag[:, :], in_=diag[:, :], compare_op=ALU.is_ge, fill=0.0,
                                    base=SA - 1, pattern=[[SA, GE]], channel_multiplier=-1))
            then(pool.memset(keep16, 1.0))
            then(pool.memset(keep16[:, :, 0:1], 0.0))
            then(pool.memset(rep8[:, :, :], SENTINEL))
            then(pool.memset(gsp[:, :, :], SENTINEL))
            then(pool.memset(nv[:, :], 1.0))
            pool.memset(gsum[:, :], 0.0).then_inc(consts, 1)
            pool.wait_ge(ld_wo, 16)
            then(pool.tensor_tensor(WoS[:, :], Wo_s[:, 0, :], Wo_s[:, 1, :], ALU.add))
            for h in range(2, HQ):
                ins = pool.tensor_tensor(WoS[:, :], WoS[:, :], Wo_s[:, h, :], ALU.add)
                if h < HQ - 1:
                    then(ins)
            ins.then_inc(wos_done, 1)
            def gather(n):
                if n >= XR:
                    pool.wait_ge(y_ready, n - XR + 1)
                pool.indirect_dma_start(out=xg[n % XR], out_offset=None, in_=tok_d[:, :],
                                        in_offset=bass.IndirectOffsetOnAxis(ap=idxE[:, n:n + 1], axis=0))\
                    .then_inc(xg_ld[n % XR], 16)

            pool.wait_ge(hot_a_ready, 1)
            for t in range(POOL_T0, NT):
                pool.tensor_tensor(hot_a[:, t].rearrange("p e a -> p (e a)"), hot_a[:, t].rearrange("p e a -> p (e a)"),
                                   tid[:, t:t + 1].to_broadcast([P, NE * SA]), ALU.mult).then_inc(tid_ready, 1)
            pool.wait_ge(idxE_ready, 1)
            pool.wait_ge(xn_stored, 5 * 16)
            pool.wait_ge(w_stored, 2 * 16)
            for n in range(XR - 1):
                gather(n)
            pool.wait_ge(acc_init, 10 * 16)
            for n in range(NE):
                if n + XR - 1 < NE:
                    gather(n + XR - 1)
                pool.wait_ge(y_ready, n + 1)
                if n >= 2:
                    pool.wait_ge(y_added[n % 2], 16 * (n // 2))
                pool.indirect_dma_start(out=acc_d[n % 2][:, :],
                                        out_offset=bass.IndirectOffsetOnAxis(ap=idxE[:, n:n + 1], axis=0),
                                        in_=ysb[n % YS], in_offset=None, compute_op=ALU.add)\
                    .then_inc(y_added[n % 2], 16)

            def total(p):
                pool.wait_ge(acc_ld[p], 32)
                pool.tensor_tensor(pair(xn, p), pair(xn, p), pair(acc1, p), ALU.add).then_inc(acc_ready, 1)

            def add_gated(p):
                pool.wait_ge(silu_ready, p + 1)
                pool.wait_ge(s0_ready, 2 * p + 2)
                then(pool.tensor_tensor(tg[p % 2], tg[p % 2], pair(s0, p), ALU.mult))
                pool.tensor_tensor(pair(x, p), pair(x, p), tg[p % 2], ALU.add).then_inc(x1_ready, 1)

            def score_products(p):
                pool.wait_ge(qkv_ready, 2 * p + 2)
                new, old = qkv1[p % 2], kv0[p % 2]
                if p:
                    pool.wait_ge(dif_ready, p)
                then(pool.tensor_tensor(dk, new[:, :, REP1 * HD1:GS1 - HD1], old[:, :, 0:HD1], ALU.subtract))
                pool.tensor_tensor(pr, new[:, :, 0:REP1 * HD1].rearrange("p g (r d) -> p g r d", r=REP1), heads(dk),
                                   ALU.mult).then_inc(prod_ready, 1)
                then(pool.tensor_tensor(dv, new[:, :, GS1 - HD1:GS1], old[:, :, HD1:2 * HD1], ALU.subtract))
                then(pool.tensor_scalar(hv, dv, 0.5, None, ALU.mult))
                then(pool.tensor_tensor(mid, hv, old[:, :, HD1:2 * HD1], ALU.add))

            def attend(p):
                pool.wait_ge(td_ready, p + 1)
                if p:
                    pool.wait_ge(attT_ps, p)
                then(pool.tensor_tensor(att_h[1], heads(hv), td[:, :].rearrange("p (g r) -> p g r", r=REP1).unsqueeze(3)
                                        .to_broadcast([P, NKV1, REP1, HD1]), ALU.mult))
                pool.tensor_tensor(att_h[1], att_h[1], heads(mid), ALU.add).then_inc(att_ready, 1)

            def low(n):
                pool.wait_ge(hi_ready, n + 1)
                pool.tensor_tensor(lo16[n % GT], hid[n // GT % 2][:, n % GT, :], hi16[n % GT], ALU.subtract)\
                    .then_inc(lo_ready, 1)

            def finish(n):
                q_, t = n % GT, n // GT + NP * (n % GT)
                pool.wait_ge(zu_ready, n + 1)
                pool.wait_ge(s1_ready, n // GT + 1)
                then(pool.tensor_tensor(zu[:, q_, :], zu[:, q_, :], s1[n // GT % 2][:, q_, :], ALU.mult))
                pool.tensor_tensor(x[:, t, :], x[:, t, :], zu[:, q_, :], ALU.add).then_inc(out_ready, 1)

            for p in range(4):
                total(p)
            for p in range(3):
                add_gated(p)
            score_products(0)
            for p in range(NP + 2):
                if p + 4 < NP:
                    total(p + 4)
                if p < NP:
                    attend(p)
                if p >= 2:
                    for q_ in range(GT):
                        finish(GT * (p - 2) + q_)
                if p + 3 < NP:
                    add_gated(p + 3)
                if p + 1 < NP:
                    score_products(p + 1)
                if p < NP:
                    for q_ in range(GT):
                        low(GT * p + q_)

        @block.scalar
        def _(sc):
            step = [0]

            def then(ins):
                step[0] += 1
                ins.then_inc(act, 1)
                sc.wait_ge(act, step[0])

            def root(c):
                sc.wait_ge(ln1_var, c + 1)
                sc.activation(rstd[:, 4 * c:4 * c + 4], rstd[:, 4 * c:4 * c + 4], ACT.Sqrt).then_inc(ln1_std, 1)

            root(0)
            sc.wait_ge(rwT_ps, 1)
            sc.activation(rwT[:, :, :], bk_(4)[:, 0:KH * NE].rearrange("p (k e) -> p k e", k=KH), ACT.Copy).then_inc(rwT_ready, 1)
            root(1)
            for t in range(NT):
                sc.wait_ge(xT_ps, t + 1)
                sc.activation(xT[:, t, :, :], bk_(t % 2)[:, 0:D].rearrange("p (k n) -> p k n", k=KH), ACT.Copy)\
                    .then_inc(xT_ready, 1)
                if t in (0, 3):
                    root(2 + t // 3)
            for c in range(2):
                sc.wait_ge(logits_ps, c + 1)
                sc.activation(s_sig[:, 8 * c:8 * c + 8, :], bk_(2 + c).rearrange("p (t e) -> p t e", t=8), ACT.Tanh,
                              scale=0.5).then_inc(tanh_ready, 1)
            def take_v(c):
                sc.wait_ge(vt_ps, c + 1)
                sc.activation(v[:, 4 * c:4 * c + 4, :], bk_(c % 2).rearrange("p (t d) -> p t d", t=4), ACT.Copy)\
                    .then_inc(v_ready, 1)

            sc.wait_ge(bks_ready, 1)
            for c in range(4):
                cols = slice(512 * c, 512 * c + 512)
                sc.wait_ge(kv_ps, 2 * c + 1)
                sc.activation(kT[:, cols], bk_(4 + 2 * (c % 2)), ACT.Identity, bias=bks[:, 0:1], scale=1.0 / DH)\
                    .then_inc(kv_ready, 1)
                sc.wait_ge(kv_ps, 2 * c + 2)
                sc.activation(vT[:, cols], bk_(5 + 2 * (c % 2)), ACT.Identity, bias=bvc[:, 0:1], scale=1.0)\
                    .then_inc(kv_ready, 1)
                if c:
                    take_v(c - 1)
            take_v(3)

            def shared_gate(c):
                sc.wait_ge(sgu_ps, c + 1)
                if c >= 1:
                    sc.wait_ge(shT_ready, c)
                sc.activation(sh_t, bk_(0)[0:FF, :], ACT.Tanh, scale=0.5).then_inc(stanh_ready, 1)

            def shared_out(c):
                for j in range(2):
                    sc.wait_ge(sdn_ps, 2 * c + j + 1)
                    t = SC * c + 2 * j
                    sc.activation(xn[:, t:t + 2, :], bk_(2 + j).rearrange("p (t d) -> p t d", t=2), ACT.Copy, scale=0.25)\
                        .then_inc(sy_ready, 1)
                sc.wait_ge(sy_ready, 2 * c + 2)
                for a in acc_v:
                    sc.dma_start(a[:, SC * c:SC * c + SC, :], xn[:, SC * c:SC * c + SC, :]).then_inc(acc_init, 16)
                if c == 0:
                    for a in acc_d:
                        sc.dma_start(a[NTOK:NTOK + P, :], xn[:, 0, :]).then_inc(acc_init, 16)

            sc.wait_ge(wos_done, 1)
            sc.wait_ge(xn_stored, 5 * 16)
            shared_gate(0)
            shared_gate(1)
            shared_out(0)

            def exps(t):
                sc.wait_ge(nmax_ready, t + 1)
                if t >= 2:
                    sc.wait_ge(pT_ps, 2 * (t - 1))
                sc.activation(probs[t % 2], two[2][:, :], ACT.Exp, bias=nmax[:, t:t + 1], scale=1.0,
                              accum_out=rsum[:, t:t + 1]).then_inc(probs_ready, 1)

            def attention_step(t, step):
                if step == 0:
                    sc.wait_ge(pT_ps, 2 * t + 1)
                    if t >= 2:
                        sc.wait_ge(o_ps, t - 1)
                    sc.activation(probT[t % 2][:, 0:4, :], bk_(0).rearrange("p (i j) -> p i j", i=4), ACT.Copy)\
                        .then_inc(pT_act, 1)
                elif step == 2 and t + 1 < NT:
                    exps(t + 1)
                elif step == 3:
                    sc.wait_ge(o_ps, t + 1)
                    if t >= 2:
                        sc.wait_ge(wo_ps, t - 1)
                    sc.activation(oT[t % 2], bk_(1)[:, 0:P], ACT.Copy).then_inc(oT_ready, 1)

            sc.wait_ge(hot_a_ready, 1)
            for t in range(POOL_T0):
                sc.activation(hot_a[:, t], hot_a[:, t], ACT.Copy, scale=tid[:, t:t + 1]).then_inc(tid_ready, 1)

            shared_gate(2)
            shared_out(1)
            shared_out(2)
            shared_gate(3)
            exps(0)
            shared_out(3)
            for t in range(EARLY):
                for step_ in range(STEPS):
                    attention_step(t, step_)

            def prepare(j):
                sc.wait_ge(prep_ps, j + 1)
                b = bk_(2 + j % 2)
                if j < 4:
                    ins = sc.activation(wfcT[:, j // 2, 512 * (j % 2):512 * (j % 2) + 512], b, ACT.Copy)
                elif j < 8:
                    ins = sc.activation(wpjT[:, 2 * (j - 4):2 * (j - 4) + 2, :],
                                        b.rearrange("p (k n) -> p k n", k=2), ACT.Copy)
                elif j == 8:
                    ins = sc.activation(wpoT[:, :, :], b.rearrange("p (k n) -> p k n", k=KH), ACT.Copy)
                else:
                    ins = sc.activation(wqT_hi[:, j - 9, :], b[:, 0:QKV1], ACT.Copy, scale=WSCALE)
                ins.then_inc(prep_ready, 1)

            def turn(n):
                sc.wait_ge(xgT_ps, n + 1)
                if n >= 2:
                    sc.wait_ge(gu_ps, n - 1)
                sc.activation(xgT[n % 2], bk_(2)[:, 0:D].rearrange("p (k n) -> p k n", k=KH), ACT.Copy)\
                    .then_inc(xgT_ready, 1)

            def take_h(n):
                sc.wait_ge(hT_ps, n + 1)
                if n >= 2:
                    sc.wait_ge(y_ps, n - 1)
                sc.activation(hT[n % 2], hT_bank[n % 2], ACT.Copy).then_inc(hT_ready, 1)

            turn(0)
            for n in range(NE):
                if n + 1 < NE:
                    turn(n + 1)
                sc.wait_ge(gu_ps, n + 1)
                if n >= 2:
                    sc.wait_ge(h_ready, n - 1)
                sc.activation(eth[n % 2], gu[n % 2][:, 0:FF], ACT.Tanh, scale=0.5).then_inc(gtanh_ready, 1)
                if n:
                    take_h(n - 1)
                if beside(n):
                    attention_step(*beside(n))
                if n == SUM_AT - 2:
                    sc.wait_ge(ld_w1, 64)
                    for m, w in enumerate((wfc_s, wpj_s)):
                        sc.activation(tern_tmp, w.rearrange("p c d -> p (c d)"), ACT.Abs,
                                      accum_out=gsum[:, m:m + 1]).then_inc(gsum_ready, 1)
                        sc.wait_ge(gsum_ready, m + 1)
                if n == SUM_AT:
                    sc.wait_ge(gw_ps, 1)
                    sc.activation(gwv[:, :], bk_(3)[:, 0:2], ACT.Copy, scale=1.0 / (FF1 * D)).then_inc(gw_ready, 1)
            take_h(NE - 1)
            def gate(p):
                sc.wait_ge(acc_ready, p + 1)
                if p >= 2:
                    sc.wait_ge(x1_ready, p - 1)
                sc.activation(tg[p % 2], pair(xn, p), ACT.Tanh, scale=0.5).then_inc(gate_ready, 1)

            def high_q(p):
                sc.wait_ge(qT_ps, p + 1)
                if p:
                    sc.wait_ge(fc_ps, GT * p)
                sc.activation(qT_hi, bk_(0).rearrange("p (q k n) -> p q k n", q=GT, k=KH), ACT.Copy).then_inc(qT_hi_ready, 1)

            def take_qkv(p):
                sc.wait_ge(scale_ready, 2 * p + 2)
                sc.wait_ge(qkv_ps, p + 1)
                if p >= 2:
                    sc.wait_ge(att_ready, p - 1)
                sc.activation(qkv1[p % 2], bk_(1)[:, 0:QKV1].rearrange("p (g c) -> p g c", g=NKV1), ACT.Copy,
                              scale=kvscale[p % 2][:, 1:2]).then_inc(qkv_ready, 1)
                sc.activation(kv0[p % 2], bk_(1)[:, QKV1:512].rearrange("p (g c) -> p g c", g=NKV1), ACT.Copy,
                              scale=kvscale[p % 2][:, 0:1]).then_inc(qkv_ready, 1)

            def gelu(n):
                q_ = n % GT
                sc.wait_ge(scale_ready, 2 * (n // GT) + 2)
                sc.wait_ge(fc_ps, n + 1)
                if n >= 2 * GT:
                    sc.wait_ge(lo_ready, n - 2 * GT + 1)
                sc.activation(hid[n // GT % 2][:, q_, :], two[1][:, :], ACT.Gelu, scale=fcscale[n // GT % 2][:, q_:q_ + 1],
                              accum_out=hsum[:, q_:q_ + 1]).then_inc(gelu_ready, 1)

            def square(n):
                q_ = n % GT
                sc.wait_ge(nmean_ready, n // GT + 1)
                sc.activation(sq[q_], hid[n // GT % 2][:, q_, :], ACT.Square, bias=nmean[:, q_:q_ + 1], scale=1.0,
                              accum_out=ssq[:, q_:q_ + 1]).then_inc(sq_ready, 1)

            def take_hT(n):
                sc.wait_ge(hT1_ps, n + 1)
                if n >= 2:
                    sc.wait_ge(z_ps, n - 1)
                sc.activation(hiT[n % 2], bk_(4).bitcast(F16), ACT.Copy).then_inc(hT1_ready, 1)
                sc.activation(loT[n % 2], bk_(5).bitcast(F16), ACT.Copy).then_inc(hT1_ready, 1)

            def own_value(p):
                if p:
                    sc.wait_ge(attT_ps, p)
                sc.activation(att_h[0], heads(kv0[p % 2][:, :, HD1:2 * HD1]), ACT.Copy).then_inc(att0_ready, 1)

            def half_tanh(p):
                sc.wait_ge(dif_ready, p + 1)
                sc.activation(td[:, :], dif[:, :], ACT.Tanh, scale=0.5 / HD1 ** 0.5).then_inc(td_ready, 1)

            def take_attT(p):
                sc.wait_ge(attT_ps, p + 1)
                sc.activation(attT, bk_(6).rearrange("p (s k n) -> p s k n", s=2, k=KH), ACT.Copy).then_inc(attT_ready, 1)

            def take_s1(p):
                sc.wait_ge(s1_ps, p + 1)
                if p >= 2:
                    sc.wait_ge(out_ready, GT * (p - 1))
                sc.wait_ge(zhalf_ready, p + 1)
                for q_ in range(GT):
                    ins = sc.activation(s1[p % 2][:, q_, :], bk_(6)[:, D * q_:D * q_ + D], ACT.Copy,
                                        scale=zhalf[p % 2][:, q_:q_ + 1])
                ins.then_inc(s1_ready, 1)

            def gate2(p):
                sc.wait_ge(z_ps, GT * p + GT)
                for q_ in range(GT):
                    sc.activation(tz[:, q_, :], bk_(7)[:, D * q_:D * q_ + D], ACT.Tanh, scale=zhalf[p % 2][:, q_:q_ + 1])\
                        .then_inc(ztanh_ready, 1)

            for k, (t, step_) in enumerate(LATE_STEPS):
                if k < PREP:
                    prepare(k)
                attention_step(t, step_)
                if k in GATE_AT:
                    gate(GATE_AT.index(k))
            high_q(0)
            take_qkv(0)
            gelu(0)
            high_q(1)
            gelu(1)
            for q_ in range(GT):
                square(q_)
            for p in range(NP + 2):
                if p < NP:
                    own_value(p)
                    half_tanh(p)
                if 1 <= p <= NP:
                    take_s1(p - 1)
                if p >= 2:
                    gate2(p - 2)
                if p + 1 < NP:
                    take_qkv(p + 1)
                if p + 3 < NP:
                    gate(p + 3)
                if p + 1 < NP:
                    gelu(GT * (p + 1))
                if 1 <= p <= NP:
                    take_hT(GT * (p - 1))
                if p + 1 < NP:
                    gelu(GT * (p + 1) + 1)
                if p + 2 < NP:
                    high_q(p + 2)
                if p < NP:
                    take_attT(p)
                if 1 <= p <= NP:
                    take_hT(GT * (p - 1) + 1)
                if p < NP:
                    for q_ in range(GT):
                        if p + 1 < NP:
                            square(GT * (p + 1) + q_)

        @block.vector
        def _(ve):
            step = [0]

            def mark(ins):
                step[0] += 1
                ins.then_inc(dve, 1)
                return step[0]

            def then(ins):
                ve.wait_ge(dve, mark(ins))

            def centre(c):
                cols = slice(4 * c, 4 * c + 4)
                ve.wait_ge(ln1_std, c + 1)
                then(ve.reciprocal(rstd[:, cols], rstd[:, cols]))
                for t in range(4 * c, 4 * c + 4):
                    ve.tensor_scalar(xn[:, t, :], x[:, t, :], mv[:, t, 0:1], rstd[:, t:t + 1], ALU.subtract, ALU.mult)\
                        .then_inc(xn_ready, 1)

            for c in range(4):
                ve.wait_ge(ld_x[c], 16)
                for t in range(4 * c, 4 * c + 4):
                    last = mark(ve.bn_stats(st[:, t, :], x[:, t, :]))
                ve.wait_ge(dve, last)
                for t in range(4 * c, 4 * c + 4):
                    last = mark(ve.bn_aggr(mv[:, t, :], st[:, t, :]))
                ve.wait_ge(dve, last)
                ve.tensor_scalar(rstd[:, 4 * c:4 * c + 4], mv[:, 4 * c:4 * c + 4, 1], EPS_LN, None, ALU.add).then_inc(ln1_var, 1)
                if c:
                    centre(c - 1)
            centre(3)
            ve.wait_ge(ld_w0, 6 * 16)
            ve.tensor_scalar(bks[:, :], bkc[:, :], 1.0 / DH, None, ALU.mult).then_inc(bks_ready, 1)
            def shared_product(c):
                ve.wait_ge(stanh_ready, c + 1)
                then(ve.scalar_tensor_tensor(out=sh_a, in0=sh_t, scalar=1.0, in1=bk_(0)[0:FF, :], op0=ALU.add, op1=ALU.mult))
                if c >= 2:
                    ve.wait_ge(sdn_ps, 2 * (c - 1))
                ve.tensor_tensor(sh_h[c % 2], sh_a, bk_(1)[0:FF, :], ALU.mult).then_inc(shT_ready, 1)

            def flat(a):
                return a.rearrange("p t e -> p (t e)")

            ve.wait_ge(tanh_ready, 2)
            then(ve.tensor_scalar(flat(s_sig), flat(s_sig), 0.5, 0.5, ALU.mult, ALU.add))
            then(ve.tensor_tensor(s_sc, s_sig, eb_b[:, :].unsqueeze(1).to_broadcast([P, NT, NE]), ALU.add))
            sc_g = flat(s_sc).rearrange("p (g j) -> p g j", j=PER_G)
            mark(ve.tensor_tensor(t_hi1, sc_g[:, :, 0:4], sc_g[:, :, 4:8], ALU.max))
            then(ve.tensor_tensor(t_lo1, sc_g[:, :, 0:4], sc_g[:, :, 4:8], ALU.min))
            mark(ve.tensor_tensor(t_hi2, t_hi1[:, :, 0:2], t_hi1[:, :, 2:4], ALU.max))
            mark(ve.tensor_tensor(t_m2, t_hi1[:, :, 0:2], t_hi1[:, :, 2:4], ALU.min))
            then(ve.tensor_tensor(t_l2, t_lo1[:, :, 0:2], t_lo1[:, :, 2:4], ALU.max))
            then(ve.tensor_tensor(t_lo2, t_m2, t_l2, ALU.max))
            mark(ve.tensor_tensor(t_hi3, t_hi2[:, :, 0:1], t_hi2[:, :, 1:2], ALU.max))
            mark(ve.tensor_tensor(t_m3, t_hi2[:, :, 0:1], t_hi2[:, :, 1:2], ALU.min))
            then(ve.tensor_tensor(t_l3, t_lo2[:, :, 0:1], t_lo2[:, :, 1:2], ALU.max))
            then(ve.tensor_tensor(t_lo3, t_m3, t_l3, ALU.max))
            ve.wait_ge(consts, 1)
            then(ve.tensor_tensor(gsp[:, :, 0:GROUPS], t_hi3.rearrange("p (t g) j -> p t (g j)", t=NT),
                                  t_lo3.rearrange("p (t g) j -> p t (g j)", t=NT), ALU.add))
            for t in range(NT):
                last = mark(ve.max(mx8[:, t, :], gsp[:, t, 0:GROUPS]))
            ve.wait_ge(dve, last)
            then(ve.tensor_copy(rep8[:, :, 0:TOPG], mx8[:, :, 0:TOPG]))
            for t in range(NT):
                last = mark(ve.match_replace(gr[:, t, :], rep8[:, t, :], gsp[:, t, :], BIG))
            ve.wait_ge(dve, last)
            then(ve.tensor_scalar(gmask[:, :, :], gr[:, :, 0:GROUPS], BIG / 2, None, ALU.is_ge))
            then(ve.tensor_tensor(flat(s_masked).rearrange("p (g j) -> p g j", j=PER_G), sc_g,
                                  gmask[:, :, :].rearrange("p t g -> p (t g)").unsqueeze(2)
                                  .to_broadcast([P, NT * GROUPS, PER_G]), ALU.mult))
            then(ve.tensor_scalar(flat(s_masked), flat(s_masked), 0.0, None, ALU.add))
            for t in range(NT):
                last = mark(ve.max(mx8[:, t, :], s_masked[:, t, :]))
            ve.wait_ge(dve, last)
            for t in range(NT):
                last = mark(ve.match_replace(s_rep[:, t, :], mx8[:, t, :], s_masked[:, t, :], BIG))
            ve.wait_ge(dve, last)
            then(ve.tensor_scalar(sel16, s_rep.rearrange("p t e -> p e t"), BIG / 2, None, ALU.is_ge))
            ve.tensor_tensor_scan(cum16.rearrange("p e t -> p (e t)"), keep16.rearrange("p e t -> p (e t)"),
                                  sel16.rearrange("p e t -> p (e t)"), 0.0, ALU.mult, ALU.add).then_inc(sel_ready, 1)
            ve.wait_ge(kv_ready, 8)
            then(ve.tensor_scalar(flat(s_sel), flat(s_rep), BIG / 2, None, ALU.is_ge))
            shared_product(0)
            ve.wait_ge(pos_ps, 1)
            pos = two[3][:, :].rearrange("p (e t) -> p t e", t=NT)
            mark(ve.tensor_copy(place_i, pos))
            then(ve.scalar_tensor_tensor(out=s_sel, in0=pos, scalar=float(CAP), in1=s_sel, op0=ALU.is_lt,
                                         op1=ALU.mult))
            mark(ve.tensor_scalar(flat(a_i), flat(place_i), 4, None, ALU.logical_shift_right))
            then(ve.tensor_scalar(flat(b_i), flat(place_i), SB - 1, None, ALU.bitwise_and))
            mark(ve.scalar_tensor_tensor(out=a16, in0=s_sel, scalar=-128.0, in1=a_i, op0=ALU.mult, op1=ALU.add))
            then(ve.tensor_copy(b16, b_i))
            def top(t):
                ve.wait_ge(sc_ps, t + 1)
                ve.tensor_reduce(nmax[:, t:t + 1], two[2][:, :], AX.X, ALU.max, negate=True).then_inc(nmax_ready, 1)

            def take_projected(t):
                ve.wait_ge(wo_ps, t + 1)
                ve.scalar_tensor_tensor(out=s0[:, ORDER[t], :], in0=bk_(1)[:, 0:D], scalar=rinv[:, t:t + 1], in1=bo_b[:, :],
                                        op0=ALU.mult, op1=ALU.add).then_inc(s0_ready, 1)

            def attention_step(t, step):
                if step == 0 and t:
                    take_projected(t - 1)
                elif step == 1 and t + 1 < NT:
                    top(t + 1)
                elif step == 2:
                    ve.wait_ge(pT_ps, 2 * t + 2)
                    if t >= 2:
                        ve.wait_ge(o_ps, t - 1)
                    ve.tensor_copy(probT[t % 2][:, 4:8, :], bk_(0).rearrange("p (i j) -> p i j", i=4)).then_inc(pT_dve, 1)
                elif step == 3:
                    ve.wait_ge(probs_ready, t + 1)
                    then(ve.tensor_scalar(rsum[:, t:t + 1], rsum[:, t:t + 1], 2.0, None, ALU.mult))
                    then(ve.reciprocal(rinv[:, t:t + 1], rsum[:, t:t + 1]))

            for a in range(SA):
                ins = ve.tensor_scalar(hot_a[:, :, :, a], a16, float(a - 128), None, ALU.is_equal)
            ins.then_inc(hot_a_ready, 1)
            shared_product(1)
            for b in range(SB):
                ins = ve.tensor_scalar(flat(hot_b[:, b, :, :]), flat(b16), float(b), None, ALU.is_equal)
            ins.then_inc(hot_ready, 1)
            shared_product(2)
            then(ve.scalar_tensor_tensor(out=s_w, in0=s_rep, scalar=BIG / 2, in1=s_sig, op0=ALU.is_ge, op1=ALU.mult))
            then(ve.tensor_reduce(den[:, :], s_w, AX.X, ALU.add))
            then(ve.tensor_scalar(den[:, :], den[:, :], 1e-20, None, ALU.add))
            then(ve.reciprocal(rden[:, :], den[:, :]))
            then(ve.tensor_scalar(rden[:, :], rden[:, :], ROUTE_SCALE, None, ALU.mult))
            ve.tensor_tensor(s_w, s_w, rden[:, :].unsqueeze(2).to_broadcast([P, NT, NE]), ALU.mult).then_inc(w_ready, 1)
            ve.wait_ge(ld_sh, 4 * 16)
            then(ve.tensor_scalar(bo_b[:, :], bo_b[:, :], 0.5, None, ALU.mult))
            top(0)
            ve.wait_ge(slot_ps, 1)
            then(ve.tensor_tensor(slot_m, two[3][:, :].rearrange("p (g e) -> p g e", e=GE),
                                  diag[:, :].unsqueeze(1).to_broadcast([P, NGE * SB, GE]), ALU.mult))
            ve.tensor_reduce(slotR[:, :], slot_m, AX.X, ALU.add).then_inc(slotR_ready, 1)
            shared_product(3)
            ve.wait_ge(idx_ps, 1)
            then(ve.tensor_scalar(empty[:, :], bk_(6)[:, 0:NE], 0.5, trash[:, 0:1], ALU.is_lt, ALU.mult))
            then(ve.tensor_tensor(empty[:, :], empty[:, :], bk_(6)[:, 0:NE], ALU.add))
            ve.tensor_scalar(idxE[:, :], empty[:, :], -1.0, None, ALU.add).then_inc(idxE_ready, 1)
            for t in range(EARLY):
                for step_ in range(STEPS):
                    attention_step(t, step_)

            def put(n):
                ve.wait_ge(y_ps, n + 1)
                if n >= YS:
                    ve.wait_ge(y_added[n % 2], 16 * (n // 2 - 1))
                ve.tensor_scalar(ysb[n % YS], bk_(3)[:, 0:D], xg[n % XR][:, D + n:D + n + 1], 0.5, ALU.mult, ALU.mult)\
                    .then_inc(y_ready, 1)

            def thresholds():
                ve.wait_ge(gw_ready, 1)
                mark(ve.tensor_scalar(gwc[:, 0:1], gwv[:, 0:1], 1.0 / QB, None, ALU.mult))
                mark(ve.tensor_scalar(gwc[:, 1:2], gwv[:, 1:2], 0.5 / QB, None, ALU.mult))
                then(ve.tensor_scalar(thr[:, :], gwv[:, :], EPS_Q, 0.5, ALU.add, ALU.mult))
                then(ve.tensor_scalar(nthr[:, :], thr[:, :], -1.0, None, ALU.mult))

            def ternarise(m, c):
                w = (wfc_s, wpj_s)[m].rearrange("p c d -> p (c d)")[:, FF1 * c:FF1 * c + FF1]
                then(ve.tensor_scalar(tern_tmp[:, 0:FF1], w, nthr[:, m:m + 1], None, ALU.is_lt))
                ve.scalar_tensor_tensor(out=w, in0=w, scalar=thr[:, m:m + 1], in1=tern_tmp[:, 0:FF1], op0=ALU.is_gt,
                                        op1=ALU.subtract).then_inc(tern_ready, 1)
                ve.wait_ge(tern_ready, 2 * m + c + 1)

            for n in range(NE):
                ve.wait_ge(gtanh_ready, n + 1)
                if n >= 2:
                    ve.wait_ge(hT_ps, n - 1)
                then(ve.scalar_tensor_tensor(out=h[n % 2], in0=eth[n % 2], scalar=1.0, in1=gu[n % 2][:, 0:FF],
                                             op0=ALU.add, op1=ALU.mult))
                ve.tensor_tensor(h[n % 2], h[n % 2], gu[n % 2][:, FF:2 * FF], ALU.mult).then_inc(h_ready, 1)
                if n >= 2:
                    put(n - 2)
                if beside(n):
                    attention_step(*beside(n))
                if n == SUM_AT + 2:
                    thresholds()
                if n in TERN_AT:
                    ternarise(*divmod(TERN_AT.index(n), 2))
            for n in range(NE - 2, NE):
                put(n)

            def low_weights(j):
                ve.wait_ge(prep_ready, 10 + j)
                ve.scalar_tensor_tensor(out=wqT_lo[:, j, :], in0=bk_(2 + (9 + j) % 2)[:, 0:QKV1], scalar=WSCALE,
                                        in1=wqT_hi[:, j, :], op0=ALU.mult, op1=ALU.subtract).then_inc(prep_lo, 1)

            newton_at = [0]

            def newton(k, cols):
                v, y, t_, i_ = nv[:, cols], ny[:, cols], nt2[:, cols], ni[:, cols]
                if k:
                    ve.wait_ge(dve, newton_at[0])
                if k == 0:
                    ins = ve.tensor_scalar(i_, v.bitcast(I32), 1, None, ALU.logical_shift_right)
                elif k == 1:
                    ins = ve.tensor_scalar(y.bitcast(I32), i_, -1.0, RSQRT_SEED, ALU.mult, ALU.add)
                elif k % 3 == 2:
                    ins = ve.tensor_tensor(t_, y, y, ALU.mult)
                elif k % 3 == 0:
                    ins = ve.scalar_tensor_tensor(out=t_, in0=t_, scalar=-0.5, in1=v, op0=ALU.mult, op1=ALU.mult)
                else:
                    ins = ve.scalar_tensor_tensor(out=y, in0=t_, scalar=1.5, in1=y, op0=ALU.add, op1=ALU.mult)
                newton_at[0] = mark(ins)

            def silu(p):
                ve.wait_ge(gate_ready, p + 1)
                ve.scalar_tensor_tensor(out=tg[p % 2], in0=tg[p % 2], scalar=1.0, in1=pair(xn, p), op0=ALU.add, op1=ALU.mult)\
                    .then_inc(silu_ready, 1)

            def moments(p):
                ve.wait_ge(x1_ready, p + 1)
                for q_ in range(GT):
                    last = mark(ve.bn_stats(st1[:, q_, :], x[:, p + NP * q_, :]))
                ve.wait_ge(dve, last)
                for q_ in range(GT):
                    last = mark(ve.bn_aggr(mv1[:, q_, :], st1[:, q_, :]))
                ve.wait_ge(dve, last)
                var = mv1[:, :, 1]
                mark(ve.tensor_scalar(nv[:, 0:GT], var, EPS_LN, None, ALU.add))
                then(ve.tensor_scalar(nv[:, GT:2 * GT], var, 1.0 + EPS_Q, EPS_Q * EPS_LN, ALU.mult, ALU.add))

            row_at = [0]

            def quantise(k, p):
                xp = xq[p % 2]
                if k == 0:
                    if p >= 2:
                        ve.wait_ge(qT_ps, p - 1)
                elif k not in (1, 6):
                    ve.wait_ge(dve, row_at[0])
                if k < 2:
                    ins = ve.tensor_scalar(xp[:, k, :], x[:, p + NP * k, :], mv1[:, k, 0:1], None, ALU.subtract)
                elif k == 2:
                    ins = ve.tensor_reduce(amax[:, :], xp, AX.X, ALU.max, apply_absolute_value=True)
                elif k == 3:
                    ins = ve.reciprocal(qscale[:, :], amax[:, :])
                elif k == 4:
                    ins = ve.tensor_scalar(qscale[:, :], qscale[:, :], QB, None, ALU.mult)
                elif k < 7:
                    q_ = k - 5
                    ins = ve.tensor_scalar(xp[:, q_, :], xp[:, q_, :], qscale[:, q_:q_ + 1], QB, ALU.mult, ALU.min)
                else:
                    ve.tensor_scalar(xp, xp, -QB, None, ALU.max).then_inc(xq_ready, 1)
                    return
                row_at[0] = mark(ins)

            def scales_and_rows(p, cols):
                for k in range(NEWTON):
                    newton(k, cols)
                    if k < ROW_STEPS and p < NP:
                        quantise(k, p)
                    elif ROW_STEPS <= k < ROW_STEPS + GT and 4 <= p:
                        silu2(GT * (p - 4) + k - ROW_STEPS)
                ve.wait_ge(dve, newton_at[0])

            def product_scales(p):
                if p >= 2:
                    ve.wait_ge(qkv_ready, 2 * (p - 1))
                    ve.wait_ge(gelu_ready, GT * (p - 1))
                ve.scalar_tensor_tensor(out=kvscale[p % 2][:, :], in0=amax[:, :], scalar=1.0 / (QB * WSCALE),
                                        in1=ny[:, 0:GT], op0=ALU.mult, op1=ALU.mult).then_inc(scale_ready, 1)
                ve.scalar_tensor_tensor(out=fcscale[p % 2][:, :], in0=amax[:, :], scalar=gwc[:, 0:1], in1=ny[:, GT:2 * GT],
                                        op0=ALU.mult, op1=ALU.mult).then_inc(scale_ready, 1)

            def low_q(p):
                ve.wait_ge(qT_hi_ready, p + 1)
                ve.tensor_tensor(qT_lo, bk_(0).rearrange("p (q k n) -> p q k n", q=GT, k=KH), qT_hi, ALU.subtract)\
                    .then_inc(qT_lo_ready, 1)

            def score_difference(p):
                ve.wait_ge(prod_ready, p + 1)
                ve.tensor_reduce(dif[:, :].rearrange("p (g r) -> p g r", r=REP1), pr, AX.X, ALU.add).then_inc(dif_ready, 1)

            def means(p):
                ve.wait_ge(gelu_ready, GT * p + GT)
                ve.wait_ge(dve, step[0])
                ve.tensor_scalar(nmean[:, :], hsum[:, :], -1.0 / FF1, None, ALU.mult).then_inc(nmean_ready, 1)

            def spreads(p):
                for q_ in range(GT):
                    ve.wait_ge(sq_ready, GT * p + q_ + 1)
                    mark(ve.tensor_reduce(nv[:, 3 * GT + q_:3 * GT + q_ + 1], sq[q_], AX.X, ALU.max))
                then(ve.tensor_scalar(nv[:, 2 * GT:3 * GT], ssq[:, :], 1.0 / FF1, EPS_Q, ALU.mult, ALU.add))

            def hidden_scales(p):
                mark(ve.tensor_scalar(hscale[:, :], ny[:, 3 * GT:], QB, None, ALU.mult))
                got = mark(ve.tensor_tensor(tmpc[:, :], nv[:, 3 * GT:], ny[:, 3 * GT:], ALU.mult))
                ve.wait_ge(dve, got - 1)
                mark(ve.tensor_tensor(hbias[:, :], hscale[:, :], nmean[:, :], ALU.mult))
                ve.wait_ge(dve, got)
                if p >= 2:
                    ve.wait_ge(ztanh_ready, GT * (p - 1))
                    ve.wait_ge(s1_ready, p - 1)
                ve.scalar_tensor_tensor(out=zhalf[p % 2][:, :], in0=tmpc[:, :], scalar=gwc[:, 1:2], in1=ny[:, 2 * GT:3 * GT],
                                        op0=ALU.mult, op1=ALU.mult).then_inc(zhalf_ready, 1)

            def quantise_hidden(p):
                rows = [hid[p % 2][:, q_, :] for q_ in range(GT)]
                ve.wait_ge(dve, step[0])
                for q_, h in enumerate(rows):
                    last = mark(ve.tensor_scalar(h, h, hscale[:, q_:q_ + 1], hbias[:, q_:q_ + 1], ALU.mult, ALU.add))
                ve.wait_ge(dve, last)
                for h in rows:
                    last = mark(ve.tensor_scalar(h, h, QB, -QB, ALU.min, ALU.max))
                if p:
                    ve.wait_ge(hT1_ps, GT * p)
                for q_, h in enumerate(rows):
                    ve.wait_ge(dve, last - GT + 1 + q_)
                    ve.tensor_copy(hi16[q_], h).then_inc(hi_ready, 1)

            def silu2(n):
                p, q_ = n // GT, n % GT
                ve.wait_ge(ztanh_ready, GT * p + GT)
                if p:
                    ve.wait_ge(out_ready, GT * (p - 1) + q_ + 1)
                ve.scalar_tensor_tensor(out=zu[:, q_, :], in0=tz[:, q_, :], scalar=1.0, in1=bk_(7)[:, D * q_:D * q_ + D],
                                        op0=ALU.add, op1=ALU.mult).then_inc(zu_ready, 1)

            for k, (t, step_) in enumerate(LATE_STEPS):
                attention_step(t, step_)
                if k in GATE_AT:
                    silu(GATE_AT.index(k))
                if k == PREP:
                    for j in range(2):
                        low_weights(j)
                if k in MOMENTS_AT:
                    p = MOMENTS_AT.index(k)
                    moments(p)
                    scales_and_rows(p, slice(0, 2 * GT))
                    product_scales(p)
            low_q(0)
            take_projected(NT - 1)
            low_q(1)
            means(0)
            for p in range(NP + 2):
                if p < NP:
                    score_difference(p)
                    spreads(p)
                if p + 2 < NP:
                    moments(p + 2)
                if p < NP:
                    scales_and_rows(p + 2, slice(0, 4 * GT))
                    hidden_scales(p)
                if p + 3 < NP:
                    silu(p + 3)
                if p + 1 < NP:
                    means(p + 1)
                if p < NP:
                    quantise_hidden(p)
                if p + 2 < NP:
                    product_scales(p + 2)
                    low_q(p + 2)
                if p >= NP:
                    for q_ in range(GT):
                        silu2(GT * (p - 2) + q_)

        @block.tensor
        def _(pe):
            pe.wait_ge(consts, 1)
            pe.wait_ge(ld_w0, 6 * 16)
            for k in range(KH):
                ins = pe.transpose(bk_(4)[:, NE * k:NE * k + NE], rw_s.rearrange("e (n k) -> e k n", k=KH)[:, k, :],
                                   ident[0:NE, 0:NE])
            ins.then_inc(rwT_ps, 1)

            def logits(t):
                pe.wait_ge(xT_ready, t + 1)
                for k in range(KH):
                    ins = pe.matmul(bk_(2 + t // 8)[:, NE * (t % 8):NE * (t % 8) + NE], xT[:, t, k, :], rwT[:, k, :],
                                    start=(k == 0), stop=(k == KH - 1))
                if t % 8 == 7:
                    ins.then_inc(logits_ps, 1)

            for t in range(NT):
                pe.wait_ge(xn_ready, t + 1)
                if t >= 2:
                    pe.wait_ge(xT_ready, t - 1)
                for k in range(KH):
                    ins = pe.transpose(bk_(t % 2)[:, P * k:P * k + P],
                                       xn[:, t, :].rearrange("p (n k) -> p k n", k=KH)[:, k, :], ident[:, :])
                ins.then_inc(xT_ps, 1)
                if t == 0:
                    pe.wait_ge(rwT_ready, 1)
                if t >= 1:
                    logits(t - 1)
            logits(NT - 1)
            def turn_v(c):
                pe.wait_ge(kv_ready, 2 * c + 2)
                if c >= 2:
                    pe.wait_ge(v_ready, c - 1)
                for t in range(4):
                    at = P * (4 * c + t)
                    ins = pe.transpose(bk_(c % 2)[:, P * t:P * t + P], vT[:, at:at + P], ident[:, :])
                ins.then_inc(vt_ps, 1)

            pe.wait_ge(xT_ready, NT)
            for c in range(4):
                if c >= 2:
                    pe.wait_ge(kv_ready, 2 * (c - 1))
                for b, w in ((4, Wk_s), (5, Wv_s)):
                    for k in range(KH):
                        ins = pe.matmul(bk_(b + 2 * (c % 2)), w[:, k, :], xT[:, 4 * c:4 * c + 4, k, :], start=(k == 0),
                                        stop=(k == KH - 1))
                    ins.then_inc(kv_ps, 1)
                if c:
                    turn_v(c - 1)
            turn_v(3)
            pe.wait_ge(ld_sh, 4 * 16)

            def shared_up(c):
                if c:
                    pe.wait_ge(shT_ready, c)
                for m in range(2):
                    for k in range(KH):
                        ins = pe.matmul(bk_(m)[0:FF, :], sgu[:, m, k, :], xT[:, SC * c:SC * c + SC, k, :], start=(k == 0),
                                        stop=(k == KH - 1))
                ins.then_inc(sgu_ps, 1)

            def shared_down(c):
                pe.wait_ge(shT_ready, c + 1)
                for j in range(2):
                    if c:
                        pe.wait_ge(sy_ready, 2 * (c - 1) + j + 1)
                    for i in range(2):
                        at = P * (2 * j + i)
                        ins = pe.matmul(bk_(2 + j)[:, D * i:D * i + D], sh_h[c % 2][:, at:at + P], sdn[:, :], start=True,
                                        stop=True)
                    ins.then_inc(sdn_ps, 1)

            def positions():
                pe.wait_ge(sel_ready, 1)
                pe.wait_ge(kv_ready, 8)
                for h in range(2):
                    es = slice(32 * h, 32 * h + 32)
                    pe.matmul(bk_(6 + h), before16[:, :], sel16[:, es, :].rearrange("p e t -> p (e t)"), start=True,
                              stop=False)
                    ins = pe.matmul(bk_(6 + h), ones16[:, :], cum16[:, es, :].rearrange("p e t -> p (e t)"), start=False,
                                    stop=True)
                ins.then_inc(pos_ps, 1)

            pe.wait_ge(v_ready, 4)
            for c in range(3):
                shared_up(c)
                if c == 0:
                    positions()
                else:
                    shared_down(c - 1)

            def score(t):
                if t:
                    pe.wait_ge(probs_ready, t)
                for h in range(2):
                    at = (ORDER[t] // NP) * SEQ + 512 * h
                    rows = slice(P * ORDER[t], P * ORDER[t] + P)
                    ins = pe.matmul(two[2][:, 512 * h:512 * h + 512], vT[:, rows], kT[:, at:at + 512],
                                    start=True, stop=True)
                ins.then_inc(sc_ps, 1)

            def turn_probs(t, h):
                pe.wait_ge(probs_ready, t + 1)
                if h:
                    pe.wait_ge(pT_act, t + 1)
                elif t:
                    pe.wait_ge(pT_dve, t)
                for i in range(4):
                    ins = pe.transpose(bk_(0)[:, P * i:P * i + P], probs[t % 2][:, 512 * h + P * i:512 * h + P * i + P],
                                       ident[:, :])
                ins.then_inc(pT_ps, 1)

            def project0(t):
                pe.wait_ge(oT_ready, t + 1)
                pe.matmul(bk_(1)[:, 0:D], oT[t % 2], WoS[:, :], start=True, stop=True).then_inc(wo_ps, 1)

            def attention_step(t, step):
                if step == 0:
                    turn_probs(t, 0)
                    if t:
                        project0(t - 1)
                elif step == 1 and t + 1 < NT:
                    score(t + 1)
                elif step == 2:
                    turn_probs(t, 1)
                elif step == 3:
                    pe.wait_ge(pT_act, t + 1)
                    pe.wait_ge(pT_dve, t + 1)
                    if t:
                        pe.wait_ge(s0_ready, t)
                    for i in range(8):
                        ins = pe.matmul(bk_(1)[:, 0:P], v[:, (ORDER[t] // NP) * NP + i, :], probT[t % 2][:, i, :], start=(i == 0),
                                        stop=(i == 7))
                    ins.then_inc(o_ps, 1)

            score(0)
            pe.wait_ge(hot_ready, 1)
            pe.wait_ge(tid_ready, NT)
            for g in range(NGE):
                es = slice(GE * g, GE * g + GE)
                for t in range(NT):
                    ins = pe.matmul(two[3][:, 256 * g:256 * g + 256],
                                    hot_a[:, t, es, :].rearrange("p e a -> p (e a)"), hot_b[:, :, t, es],
                                    start=(t == 0), stop=(t == NT - 1))
            ins.then_inc(slot_ps, 1)
            shared_down(2)
            shared_up(3)
            shared_down(3)
            attention_step(0, 0)
            pe.wait_ge(slot_in, 16)
            pe.wait_ge(slotR_ready, 1)
            pe.transpose(bk_(6)[:, 0:NE], slotE[:, :], ident[0:NE, 0:NE]).then_inc(idx_ps, 1)

            def turn(n):
                pe.wait_ge(xg_ld[n % XR], 16 * (n // XR + 1))
                if n:
                    pe.wait_ge(xgT_ready, n)
                for k in range(KH):
                    ins = pe.transpose(bk_(2)[:, P * k:P * k + P],
                                       xg[n % XR][:, 0:D].rearrange("p (n k) -> p k n", k=KH)[:, k, :], ident[:, :])
                ins.then_inc(xgT_ps, 1)

            def up(n):
                pe.wait_ge(xgT_ready, n + 1)
                r = (n // WG) % WR
                pe.wait_ge(ld_e[r], 48 * (n // WG // WR + 1))
                if n >= 2:
                    pe.wait_ge(hT_ready, n - 1)
                for k in range(KH):
                    ins = pe.matmul(gu[n % 2].rearrange("p (m f) -> p m f", m=2), xgT[n % 2][:, k, :],
                                    wgu[r][:, n % WG, :, k, :], start=(k == 0), stop=(k == KH - 1))
                ins.then_inc(gu_ps, 1)

            def turn_h(n):
                pe.wait_ge(h_ready, n + 1)
                pe.transpose(hT_bank[n % 2], h[n % 2], ident[:, :]).then_inc(hT_ps, 1)

            def down(n):
                pe.wait_ge(hT_ready, n + 1)
                if n:
                    pe.wait_ge(y_ready, n)
                pe.matmul(bk_(3)[:, 0:D], hT[n % 2], wdn[(n // WG) % WR][:, n % WG, :], start=True, stop=True)\
                    .then_inc(y_ps, 1)

            for t in range(EARLY):
                for step_ in range(STEPS):
                    if t or step_:
                        attention_step(t, step_)
            pe.wait_ge(sy_ready, NT // 2)
            pe.wait_ge(idxE_ready, 1)
            turn(0)
            for n in range(NE):
                if n + 1 < NE:
                    turn(n + 1)
                up(n)
                if n >= 1:
                    turn_h(n - 1)
                if beside(n):
                    attention_step(*beside(n))
                if n == SUM_AT:
                    pe.wait_ge(gsum_ready, 2)
                    pe.wait_ge(y_ready, n - 2)
                    pe.matmul(bk_(3)[:, 0:2], ones[:, :], gsum[:, :], start=True, stop=True).then_inc(gw_ps, 1)
                    pe.wait_ge(gw_ready, 1)
                if n >= 2:
                    down(n - 2)
            turn_h(NE - 1)
            for n in range(NE - 2, NE):
                down(n)
            def prepare(j):
                if j >= 2:
                    pe.wait_ge(prep_ready, j - 1)
                if j < 4:
                    k, c0 = j // 2, 4 * (j % 2)
                    parts = [wfc_s[:, c0 + c, P * k:P * k + P] for c in range(4)]
                elif j < 8:
                    parts = [wpj_s[:, c, P * k:P * k + P] for k in (2 * (j - 4), 2 * (j - 4) + 1) for c in range(2)]
                elif j == 8:
                    parts = [wpo_s[:, c, P * k:P * k + P] for k in range(2) for c in range(2)]
                else:
                    parts = [wqkv_s[:, c, P * (j - 9):P * (j - 9) + P] for c in range(3)]
                for i, part in enumerate(parts):
                    ins = pe.transpose(bk_(2 + j % 2)[:, P * i:P * i + P], part, ident[:, :])
                ins.then_inc(prep_ps, 1)

            pe.wait_ge(tern_ready, 4)
            pe.wait_ge(ld_w2, 32)
            pe.wait_ge(y_ready, NE)
            for k, (t, step_) in enumerate(LATE_STEPS):
                if k < PREP:
                    prepare(k)
                attention_step(t, step_)

            def turn_q(p):
                pe.wait_ge(xq_ready, p + 1)
                if p:
                    pe.wait_ge(qT_lo_ready, p)
                for q_ in range(GT):
                    for k in range(KH):
                        ins = pe.transpose(bk_(0)[:, D * q_ + P * k:D * q_ + P * k + P], xq[p % 2][:, q_, P * k:P * k + P],
                                           ident[:, :])
                ins.then_inc(qT_ps, 1)

            def qkv(p):
                pe.wait_ge(qT_lo_ready, p + 1)
                if p:
                    pe.wait_ge(qkv_ready, 2 * p)
                for q_, cols, width in ((1, slice(0, QKV1), GS1), (0, slice(QKV1, 512), 2 * HD1)):
                    i = 0
                    for k in range(KH):
                        for part, w in ((qT_hi, wqT_hi), (qT_lo, wqT_hi), (qT_hi, wqT_lo)):
                            rhs = w[:, k, :].rearrange("p (g c) -> p g c", c=GS1)[:, :, GS1 - width:GS1]
                            ins = pe.matmul(bk_(1)[:, cols], part[:, q_, k, :], rhs, start=(i == 0), stop=(i == 5))
                            i += 1
                ins.then_inc(qkv_ps, 1)

            def fc(n):
                if n:
                    pe.wait_ge(gelu_ready, n)
                for h in range(2):
                    for i, (k, part) in enumerate((k, part) for k in range(KH) for part in (qT_hi, qT_lo)):
                        ins = pe.matmul(bk_(2 + h), part[:, n % GT, k, :], wfcT[:, k, 512 * h:512 * h + 512],
                                        start=(i == 0), stop=(i == 3))
                ins.then_inc(fc_ps, 1)

            def turn_att(p):
                pe.wait_ge(att0_ready, p + 1)
                pe.wait_ge(att_ready, p + 1)
                if p:
                    pe.wait_ge(s1_ready, p)
                for s_ in range(2):
                    for k in range(KH):
                        ins = pe.transpose(bk_(6)[:, D * s_ + P * k:D * s_ + P * k + P], att[:, s_, P * k:P * k + P],
                                           ident[:, :])
                ins.then_inc(attT_ps, 1)

            def project(p):
                pe.wait_ge(attT_ready, p + 1)
                for s_ in range(2):
                    for k in range(KH):
                        ins = pe.matmul(bk_(6)[:, D * s_:D * s_ + D], attT[:, s_, k, :], wpoT[:, k, :],
                                        start=(k == 0), stop=(k == KH - 1))
                ins.then_inc(s1_ps, 1)

            def turn_hidden(n):
                pe.wait_ge(lo_ready, n + 1)
                if n:
                    pe.wait_ge(hT1_ready, 2 * n)
                for b, part in ((4, hi16), (5, lo16)):
                    for k in range(FF1 // P):
                        ins = pe.transpose(bk_(b).bitcast(F16)[:, P * k:P * k + P], part[n % GT][:, P * k:P * k + P],
                                           ident16[:, :])
                ins.then_inc(hT1_ps, 1)

            def down1(n):
                pe.wait_ge(hT1_ready, 2 * n + 2)
                if n >= GT:
                    pe.wait_ge(zu_ready, n // GT * GT)
                i = 0
                for k in range(FF1 // P):
                    for part in (hiT, loT):
                        ins = pe.matmul(bk_(7)[:, D * (n % GT):D * (n % GT) + D], part[n % 2][:, P * k:P * k + P],
                                        wpjT[:, k, :], start=(i == 0), stop=(i == 2 * FF1 // P - 1))
                        i += 1
                ins.then_inc(z_ps, 1)

            turn_q(0)
            project0(NT - 1)
            pe.wait_ge(s0_ready, NT)
            pe.wait_ge(prep_lo, 2)
            qkv(0)
            fc(0)
            turn_q(1)
            fc(1)
            for p in range(NP + 2):
                if p + 1 < NP:
                    qkv(p + 1)
                    fc(GT * (p + 1))
                if 1 <= p <= NP:
                    turn_hidden(GT * (p - 1))
                if p + 1 < NP:
                    fc(GT * (p + 1) + 1)
                if p + 2 < NP:
                    turn_q(p + 2)
                if p < NP:
                    turn_att(p)
                if 1 <= p <= NP:
                    turn_hidden(GT * (p - 1) + 1)
                if p < NP:
                    project(p)
                if 1 <= p <= NP:
                    for q_ in range(GT):
                        down1(GT * (p - 1) + q_)


_INS = ["L0_attn_q", "L0_attn_Wk", "L0_attn_bk", "L0_attn_Wv", "L0_attn_bv", "L0_attn_Wo", "L0_attn_bo",
        "L0_ffn_router_weight", "L0_ffn_e_bias", "L0_ffn_w_gate", "L0_ffn_w_up", "L0_ffn_w_down", "L0_ffn_sh_gate",
        "L0_ffn_sh_up", "L0_ffn_sh_down", "L1_attn_weight_qkv", "L1_attn_weight_proj", "L1_ffn_w_fc", "L1_ffn_w_proj"]


def kernel(**inputs):
    import numpy as _np
    import concourse.bacc as _bacc
    from concourse import mybir as _mybir
    from concourse.bass_utils import run_bass_kernel_spmd as _run

    nc = _bacc.Bacc("TRN2", target_bir_lowering=False, num_devices=1)
    arrays, args = {}, []
    for name in _INS:
        a = _np.ascontiguousarray(inputs[name])
        arrays[f"in_{name}"] = a
        args.append(nc.dram_tensor(f"in_{name}", a.shape, _mybir.dt.from_np(a.dtype), kind="ExternalInput").ap())
    out = nc.dram_tensor("out_0", (BATCH, SEQ, D), F32, kind="ExternalOutput").ap()
    build(nc, *args, out)
    r = _run(nc, [arrays], core_ids=[0])
    return r.results[0]["out_0"]
```
